# Optimizing a Trainium2 kernel written in Bass

```python
import numpy as np
import jax
import jax.numpy as jnp

def _softmax(x, axis=-1):
    return jax.nn.softmax(x, axis=axis)

def _gelu(x):
    return jax.nn.gelu(x, approximate=True)

def _silu(x):
    return jax.nn.silu(x)

def _sigmoid(x):
    return jax.nn.sigmoid(x)

def _layernorm(x, axis=-1, eps=1e-05):
    m = jnp.mean(x, axis=axis, keepdims=True)
    v = jnp.var(x, axis=axis, keepdims=True)
    return (x - m) / jnp.sqrt(v + eps)

def _scatter_add(tgt, idx, src, axis=0):
    return tgt.at[idx].add(src)

def _segment_sum(src, seg, n):
    return jax.ops.segment_sum(src, seg, n)
kernel_name = 'mk_gnn_preln_d4_gnn_r32_8cab4d'

def setup_inputs(seed: int=0):
    np.random.seed(seed)
    _w = jnp.asarray

    def _rec_inputs():
        import jax
        import jax.numpy as jnp
        _gk = jax.random.key(seed)
        x = -0.0005121 + 1.001 * jax.random.normal(jax.random.fold_in(_gk, 1), (3125, 32), jnp.float32)
        src = jax.random.randint(jax.random.fold_in(_gk, 2), (100000,), 0, 3125, jnp.int32)
        dst = jnp.minimum((3125 * jax.random.uniform(jax.random.fold_in(_gk, 3), (100000,)) ** 2.0).astype(jnp.int32), 99999)
        _o = jnp.argsort(dst, stable=True)
        src = src[_o]
        dst = dst[_o]
        edge_attr_16 = 0.000254156 + 0.999948 * jax.random.normal(jax.random.fold_in(_gk, 11), (100000, 16), jnp.float32)
        edge_attr_3 = 0.000549083 + 1.00031 * jax.random.normal(jax.random.fold_in(_gk, 12), (100000, 3), jnp.float32)
        edge_attr_4 = jax.random.uniform(jax.random.fold_in(_gk, 13), (100000, 4), jnp.float32, 0.0, 1)
        edge_attr_5 = -0.000325185 + 1.00005 * jax.random.normal(jax.random.fold_in(_gk, 14), (100000, 5), jnp.float32)
        edge_weight1 = 0.000452788 + 0.999756 * jax.random.normal(jax.random.fold_in(_gk, 16), (100000, 1), jnp.float32)
        node_vec = jax.random.uniform(jax.random.fold_in(_gk, 17), (3125,), jnp.float32, 0.0, 0.999951)
        return (x, src, dst, edge_attr_16, edge_attr_3, edge_attr_4, edge_attr_5, edge_weight1, node_vec)
    x, src, dst, edge_attr_16, edge_attr_3, edge_attr_4, edge_attr_5, edge_weight1, node_vec = _rec_inputs()

    def _L0_gnn_setup():
        import jax, jax.numpy as jnp
        import numpy as np
        N_BASES = 8
        GRID = jnp.linspace(-2.0, 2.0, N_BASES)
        DENOM = GRID[1] - GRID[0]

        def fastkan(x, W, b):
            rbf = jnp.exp(-((x[..., None] - GRID) / DENOM) ** 2)
            flat = rbf.reshape(*x.shape[:-1], x.shape[-1] * N_BASES)
            return flat @ W.T + b
        key = jax.random.key(seed)
        ks = jax.random.split(key, 10)
        N, E, H = (3125, 50000, 32)
        h = jax.random.normal(ks[0], (N, H), dtype=jnp.float32)
        edge_index = jax.random.randint(ks[1], (2, E), 0, N, dtype=jnp.int64)
        edge_attr = jax.random.uniform(ks[2], (E, 4), dtype=jnp.float32)
        adult_female_counts = jax.random.uniform(ks[3], (N,), dtype=jnp.float32)
        s = lambda fan_in: 1.0 / np.sqrt(fan_in)
        W_edge = jax.random.normal(ks[4], (H, 4 * N_BASES), dtype=jnp.float32) * s(4 * N_BASES)
        b_edge = jnp.zeros((H,), dtype=jnp.float32)
        W_att = jax.random.normal(ks[5], (1, 2 * H * N_BASES), dtype=jnp.float32) * s(2 * H * N_BASES)
        b_att = jnp.zeros((1,), dtype=jnp.float32)
        W_lar = jax.random.normal(ks[6], (1, 1 * N_BASES), dtype=jnp.float32) * s(N_BASES)
        b_lar = jnp.zeros((1,), dtype=jnp.float32)
        return {'h': h, 'edge_index': edge_index, 'edge_attr': edge_attr, 'adult_female_counts': adult_female_counts, 'W_edge': W_edge, 'b_edge': b_edge, 'W_att': W_att, 'b_att': b_att, 'W_lar': W_lar, 'b_lar': b_lar}
    _L0_gnn_all = _L0_gnn_setup()
    _L0_gnn_in = {k: v for k, v in _L0_gnn_all.items() if k in ('W_edge', 'b_edge', 'W_att', 'b_att', 'W_lar', 'b_lar')}
    del _L0_gnn_all

    def _L1_gnn_setup():
        import jax, jax.numpy as jnp
        import numpy as np
        import math
        M = 8
        COMBOS = [(0, 0, 0), (0, 1, 1), (1, 0, 1), (1, 1, 0), (1, 1, 1), (2, 1, 1)]

        def _cg_coeff(j1, m1, j2, m2, j3, m3):
            if m3 != m1 + m2:
                return 0.0
            f = math.factorial
            vmin = max(0, j2 - j3 - m1, j1 + m2 - j3)
            vmax = min(j1 + j2 - j3, j1 - m1, j2 + m2)
            pref = (2 * j3 + 1) * f(j3 + j1 - j2) * f(j3 - j1 + j2) * f(j1 + j2 - j3) / f(j1 + j2 + j3 + 1)
            pref *= f(j3 + m3) * f(j3 - m3) * f(j1 - m1) * f(j1 + m1) * f(j2 - m2) * f(j2 + m2)
            s = 0.0
            for v in range(vmin, vmax + 1):
                s += (-1) ** v / (f(v) * f(j1 + j2 - j3 - v) * f(j1 - m1 - v) * f(j2 + m2 - v) * f(j3 - j2 + m1 + v) * f(j3 - j1 - m2 + v))
            return math.sqrt(pref) * s

        def _su2_cg(l1, l2, l3):
            C = np.zeros((2 * l1 + 1, 2 * l2 + 1, 2 * l3 + 1), dtype=np.complex128)
            for m1 in range(-l1, l1 + 1):
                for m2 in range(-l2, l2 + 1):
                    m3 = m1 + m2
                    if -l3 <= m3 <= l3:
                        C[m1 + l1, m2 + l2, m3 + l3] = _cg_coeff(l1, m1, l2, m2, l3, m3)
            return C

        def _qmat(l):
            q = np.zeros((2 * l + 1, 2 * l + 1), dtype=np.complex128)
            for m in range(-l, 0):
                q[l + m, l + abs(m)] = 1 / np.sqrt(2)
                q[l + m, l - abs(m)] = -1j / np.sqrt(2)
            q[l, l] = 1.0
            for m in range(1, l + 1):
                q[l + m, l + abs(m)] = (-1) ** m / np.sqrt(2)
                q[l + m, l - abs(m)] = 1j * (-1) ** m / np.sqrt(2)
            return (-1j) ** l * q

        def _so3_cg(l1, l2, l3):
            C = np.einsum('ij,kl,mn,ikn->jlm', _qmat(l1), _qmat(l2), np.conj(_qmat(l3)).T, _su2_cg(l1, l2, l3))
            assert np.abs(C.imag).max() < 1e-06
            C = C.real
            return C / np.linalg.norm(C)
        CG = {c: jnp.asarray(_so3_cg(*c), dtype=jnp.float32) for c in COMBOS}
        N, E = (3125, 50000)
        ks = jax.random.split(jax.random.key(seed), 6)
        return {'node_irreps': jax.random.normal(ks[0], (N, 4 * M), jnp.float32), 'edge_index': jax.random.randint(ks[1], (2, E), 0, N, dtype=jnp.int32), 'sh0': jax.random.normal(ks[2], (E, 1), jnp.float32), 'sh1': jax.random.normal(ks[3], (E, 3), jnp.float32), 'sh2': jax.random.normal(ks[4], (E, 5), jnp.float32), 'W': jax.random.normal(ks[5], (len(COMBOS), M, M), jnp.float32)}
    _L1_gnn_all = _L1_gnn_setup()
    _L1_gnn_in = {k: v for k, v in _L1_gnn_all.items() if k in ('W',)}
    del _L1_gnn_all

    def _L2_gnn_setup():
        import jax, jax.numpy as jnp
        import numpy as np
        N = 50000
        E = 25000
        IN, HID, OUT = (32, 64, 32)
        EPS = 1e-05

        def _gcn_norm(edge_index, n):
            loop = jnp.arange(n, dtype=edge_index.dtype)
            src = jnp.concatenate([edge_index[0], loop])
            dst = jnp.concatenate([edge_index[1], loop])
            deg = jax.ops.segment_sum(jnp.ones_like(dst, dtype=jnp.float32), dst, num_segments=n)
            dis = jnp.where(deg > 0, jax.lax.rsqrt(jnp.maximum(deg, 1.0)), 0.0)
            norm = dis[src] * dis[dst]
            return (src, dst, norm)

        def _gcn(x, W, b, src, dst, norm, n):
            xw = x @ W
            msg = xw[src] * norm[:, None]
            out = jax.ops.segment_sum(msg, dst, num_segments=n)
            return out + b

        def _bn(h, gamma, beta):
            mean = jnp.mean(h, axis=0)
            var = jnp.var(h, axis=0)
            return (h - mean) * jax.lax.rsqrt(var + EPS) * gamma + beta

        def _block(x, W, b, gamma, beta, src, dst, norm, n, Wr=None, br=None):
            identity = x if Wr is None else x @ Wr + br
            h = _gcn(x, W, b, src, dst, norm, n)
            h = jax.nn.relu(_bn(h, gamma, beta))
            return h + identity
        key = jax.random.key(seed)
        ks = jax.random.split(key, 24)

        def rn(k, shape, scale=0.1):
            return jax.random.normal(k, shape, dtype=jnp.float32) * scale
        inp = {'x': jax.random.normal(ks[0], (N, IN), dtype=jnp.float32), 'edge_index': jax.random.randint(ks[1], (2, E), 0, N, dtype=jnp.int32), 'W_enc1': rn(ks[2], (IN, HID)), 'b_enc1': jnp.zeros((HID,), jnp.float32), 'W_hid': rn(ks[3], (6, HID, HID)), 'b_hid': jnp.zeros((6, HID), jnp.float32), 'W_dec2': rn(ks[4], (HID, OUT)), 'b_dec2': jnp.zeros((OUT,), jnp.float32), 'W_dec3': rn(ks[5], (OUT, OUT)), 'b_dec3': jnp.zeros((OUT,), jnp.float32), 'bn_gamma_hid': jnp.ones((4, HID), jnp.float32), 'bn_beta_hid': jnp.zeros((4, HID), jnp.float32), 'bn_gamma_out': jnp.ones((2, OUT), jnp.float32), 'bn_beta_out': jnp.zeros((2, OUT), jnp.float32), 'Wres_enc1': rn(ks[6], (IN, HID)), 'bres_enc1': jnp.zeros((HID,), jnp.float32), 'Wres_dec2': rn(ks[7], (HID, OUT)), 'bres_dec2': jnp.zeros((OUT,), jnp.float32)}
        return inp
    _L2_gnn_all = _L2_gnn_setup()
    _L2_gnn_in = {k: v for k, v in _L2_gnn_all.items() if k in ('W_enc1', 'b_enc1', 'W_hid', 'b_hid', 'W_dec2', 'b_dec2', 'W_dec3', 'b_dec3', 'bn_gamma_hid', 'bn_beta_hid', 'bn_gamma_out', 'bn_beta_out', 'Wres_enc1', 'bres_enc1', 'Wres_dec2', 'bres_dec2')}
    del _L2_gnn_all

    def _L3_gnn_setup():
        import jax, jax.numpy as jnp
        import numpy as np
        N_NODES = 50000
        N_EDGES = 25000
        NODE_D, EDGE_D = (32, 16)
        FLOW_IN, FLOW_H, FLOW_OUT = (2 * NODE_D + EDGE_D, 64, 64)
        NODE_H, NODE_OUT = (64, 32)

        def _mlp(h, W1, b1, W2, b2):
            h = jax.nn.relu(h @ W1 + b1)
            return h @ W2 + b2
        key = jax.random.key(seed)
        ks = jax.random.split(key, 8)
        return {'x': jax.random.normal(ks[0], (N_NODES, NODE_D), dtype=jnp.float32), 'edge_index': jax.random.randint(ks[1], (2, N_EDGES), 0, N_NODES, dtype=jnp.int64), 'edge_attr': jax.random.normal(ks[2], (N_EDGES, EDGE_D), dtype=jnp.float32), 'Wf1': jax.random.normal(ks[3], (FLOW_IN, FLOW_H), dtype=jnp.float32) * (1.0 / np.sqrt(FLOW_IN)), 'bf1': jnp.zeros((FLOW_H,), dtype=jnp.float32), 'Wf2': jax.random.normal(ks[4], (FLOW_H, FLOW_OUT), dtype=jnp.float32) * (1.0 / np.sqrt(FLOW_H)), 'bf2': jnp.zeros((FLOW_OUT,), dtype=jnp.float32), 'Wn1': jax.random.normal(ks[5], (FLOW_OUT, NODE_H), dtype=jnp.float32) * (1.0 / np.sqrt(FLOW_OUT)), 'bn1': jnp.zeros((NODE_H,), dtype=jnp.float32), 'Wn2': jax.random.normal(ks[6], (NODE_H, NODE_OUT), dtype=jnp.float32) * (1.0 / np.sqrt(NODE_H)), 'bn2': jnp.zeros((NODE_OUT,), dtype=jnp.float32)}
    _L3_gnn_all = _L3_gnn_setup()
    _L3_gnn_in = {k: v for k, v in _L3_gnn_all.items() if k in ('Wf1', 'bf1', 'Wf2', 'bf2', 'Wn1', 'bn1', 'Wn2', 'bn2')}
    del _L3_gnn_all
    return {'x': x, 'src': src, 'dst': dst, 'edge_attr_16': edge_attr_16, 'edge_attr_3': edge_attr_3, 'edge_attr_4': edge_attr_4, 'edge_attr_5': edge_attr_5, 'edge_weight1': edge_weight1, 'node_vec': node_vec, 'L0_gnn_W_edge': _L0_gnn_in['W_edge'], 'L0_gnn_b_edge': _L0_gnn_in['b_edge'], 'L0_gnn_W_att': _L0_gnn_in['W_att'], 'L0_gnn_b_att': _L0_gnn_in['b_att'], 'L0_gnn_W_lar': _L0_gnn_in['W_lar'], 'L0_gnn_b_lar': _L0_gnn_in['b_lar'], 'L1_gnn_W': _L1_gnn_in['W'], 'L2_gnn_W_enc1': _L2_gnn_in['W_enc1'], 'L2_gnn_b_enc1': _L2_gnn_in['b_enc1'], 'L2_gnn_W_hid': _L2_gnn_in['W_hid'], 'L2_gnn_b_hid': _L2_gnn_in['b_hid'], 'L2_gnn_W_dec2': _L2_gnn_in['W_dec2'], 'L2_gnn_b_dec2': _L2_gnn_in['b_dec2'], 'L2_gnn_W_dec3': _L2_gnn_in['W_dec3'], 'L2_gnn_b_dec3': _L2_gnn_in['b_dec3'], 'L2_gnn_bn_gamma_hid': _L2_gnn_in['bn_gamma_hid'], 'L2_gnn_bn_beta_hid': _L2_gnn_in['bn_beta_hid'], 'L2_gnn_bn_gamma_out': _L2_gnn_in['bn_gamma_out'], 'L2_gnn_bn_beta_out': _L2_gnn_in['bn_beta_out'], 'L2_gnn_Wres_enc1': _L2_gnn_in['Wres_enc1'], 'L2_gnn_bres_enc1': _L2_gnn_in['bres_enc1'], 'L2_gnn_Wres_dec2': _L2_gnn_in['Wres_dec2'], 'L2_gnn_bres_dec2': _L2_gnn_in['bres_dec2'], 'L3_gnn_Wf1': _L3_gnn_in['Wf1'], 'L3_gnn_bf1': _L3_gnn_in['bf1'], 'L3_gnn_Wf2': _L3_gnn_in['Wf2'], 'L3_gnn_bf2': _L3_gnn_in['bf2'], 'L3_gnn_Wn1': _L3_gnn_in['Wn1'], 'L3_gnn_bn1': _L3_gnn_in['bn1'], 'L3_gnn_Wn2': _L3_gnn_in['Wn2'], 'L3_gnn_bn2': _L3_gnn_in['bn2']}

def reference(x, src, dst, edge_attr_16, edge_attr_3, edge_attr_4, edge_attr_5, edge_weight1, node_vec, L0_gnn_W_edge, L0_gnn_b_edge, L0_gnn_W_att, L0_gnn_b_att, L0_gnn_W_lar, L0_gnn_b_lar, L1_gnn_W, L2_gnn_W_enc1, L2_gnn_b_enc1, L2_gnn_W_hid, L2_gnn_b_hid, L2_gnn_W_dec2, L2_gnn_b_dec2, L2_gnn_W_dec3, L2_gnn_b_dec3, L2_gnn_bn_gamma_hid, L2_gnn_bn_beta_hid, L2_gnn_bn_gamma_out, L2_gnn_bn_beta_out, L2_gnn_Wres_enc1, L2_gnn_bres_enc1, L2_gnn_Wres_dec2, L2_gnn_bres_dec2, L3_gnn_Wf1, L3_gnn_bf1, L3_gnn_Wf2, L3_gnn_bf2, L3_gnn_Wn1, L3_gnn_bn1, L3_gnn_Wn2, L3_gnn_bn2):
    import jax
    import jax.numpy as jnp

    def _L0_gnn_ref(h, edge_index, edge_attr, adult_female_counts, W_edge, b_edge, W_att, b_att, W_lar, b_lar):
        import jax, jax.numpy as jnp
        import numpy as np
        N_BASES = 8
        GRID = jnp.linspace(-2.0, 2.0, N_BASES)
        DENOM = GRID[1] - GRID[0]

        def fastkan(x, W, b):
            rbf = jnp.exp(-((x[..., None] - GRID) / DENOM) ** 2)
            flat = rbf.reshape(*x.shape[:-1], x.shape[-1] * N_BASES)
            return flat @ W.T + b
        MAX_DIST, MAX_CUR = (50.0, 1.0)
        N = h.shape[0]
        src, dst = (edge_index[0], edge_index[1])
        ea = jnp.concatenate([edge_attr[:, 0:1] / MAX_DIST, edge_attr[:, 1:3] / MAX_CUR, (edge_attr[:, 3:4] - 10.0) / 10.0], axis=-1)
        edge_features = fastkan(ea, W_edge, b_edge)
        h_src = h[src]
        att_in = jnp.concatenate([edge_features, h_src], axis=-1)
        att_raw = fastkan(att_in, W_att, b_att)[:, 0]
        att_max = jax.ops.segment_max(att_raw, dst, num_segments=N)
        att_exp = jnp.exp(att_raw - att_max[dst])
        att_sum = jax.ops.segment_sum(att_exp, dst, num_segments=N)
        att_w = att_exp / (att_sum[dst] + 1e-08)
        larvae = jax.nn.softplus(fastkan(adult_female_counts[src][:, None], W_lar, b_lar))[:, 0]
        contrib = (att_w * larvae)[:, None] * h_src
        pressure = jax.ops.segment_sum(contrib, dst, num_segments=N)
        return pressure

    def _L1_gnn_ref(node_irreps, edge_index, sh0, sh1, sh2, W):
        import jax, jax.numpy as jnp
        import numpy as np
        import math
        M = 8
        COMBOS = [(0, 0, 0), (0, 1, 1), (1, 0, 1), (1, 1, 0), (1, 1, 1), (2, 1, 1)]

        def _cg_coeff(j1, m1, j2, m2, j3, m3):
            if m3 != m1 + m2:
                return 0.0
            f = math.factorial
            vmin = max(0, j2 - j3 - m1, j1 + m2 - j3)
            vmax = min(j1 + j2 - j3, j1 - m1, j2 + m2)
            pref = (2 * j3 + 1) * f(j3 + j1 - j2) * f(j3 - j1 + j2) * f(j1 + j2 - j3) / f(j1 + j2 + j3 + 1)
            pref *= f(j3 + m3) * f(j3 - m3) * f(j1 - m1) * f(j1 + m1) * f(j2 - m2) * f(j2 + m2)
            s = 0.0
            for v in range(vmin, vmax + 1):
                s += (-1) ** v / (f(v) * f(j1 + j2 - j3 - v) * f(j1 - m1 - v) * f(j2 + m2 - v) * f(j3 - j2 + m1 + v) * f(j3 - j1 - m2 + v))
            return math.sqrt(pref) * s

        def _su2_cg(l1, l2, l3):
            C = np.zeros((2 * l1 + 1, 2 * l2 + 1, 2 * l3 + 1), dtype=np.complex128)
            for m1 in range(-l1, l1 + 1):
                for m2 in range(-l2, l2 + 1):
                    m3 = m1 + m2
                    if -l3 <= m3 <= l3:
                        C[m1 + l1, m2 + l2, m3 + l3] = _cg_coeff(l1, m1, l2, m2, l3, m3)
            return C

        def _qmat(l):
            q = np.zeros((2 * l + 1, 2 * l + 1), dtype=np.complex128)
            for m in range(-l, 0):
                q[l + m, l + abs(m)] = 1 / np.sqrt(2)
                q[l + m, l - abs(m)] = -1j / np.sqrt(2)
            q[l, l] = 1.0
            for m in range(1, l + 1):
                q[l + m, l + abs(m)] = (-1) ** m / np.sqrt(2)
                q[l + m, l - abs(m)] = 1j * (-1) ** m / np.sqrt(2)
            return (-1j) ** l * q

        def _so3_cg(l1, l2, l3):
            C = np.einsum('ij,kl,mn,ikn->jlm', _qmat(l1), _qmat(l2), np.conj(_qmat(l3)).T, _su2_cg(l1, l2, l3))
            assert np.abs(C.imag).max() < 1e-06
            C = C.real
            return C / np.linalg.norm(C)
        CG = {c: jnp.asarray(_so3_cg(*c), dtype=jnp.float32) for c in COMBOS}
        N, E = (node_irreps.shape[0], edge_index.shape[1])
        src = node_irreps[edge_index[0]]
        feats = {0: src[:, :M][:, :, None], 1: src[:, M:].reshape(E, M, 3)}
        sh = {0: sh0, 1: sh1, 2: sh2}
        msg = {0: jnp.zeros((E, M, 1), node_irreps.dtype), 1: jnp.zeros((E, M, 3), node_irreps.dtype)}
        for idx, (le, ln, lo) in enumerate(COMBOS):
            base = jnp.einsum('ijk,ei,emj->emk', CG[le, ln, lo], sh[le], feats[ln])
            msg[lo] = msg[lo] + jnp.einsum('io,eik->eok', W[idx], base)
        tgt = edge_index[1]
        agg0 = jax.ops.segment_sum(msg[0].reshape(E, M), tgt, num_segments=N)
        agg1 = jax.ops.segment_sum(msg[1].reshape(E, 3 * M), tgt, num_segments=N)
        return jnp.concatenate([agg0, agg1], axis=1)

    def _L2_gnn_ref(x, edge_index, W_enc1, b_enc1, W_hid, b_hid, W_dec2, b_dec2, W_dec3, b_dec3, bn_gamma_hid, bn_beta_hid, bn_gamma_out, bn_beta_out, Wres_enc1, bres_enc1, Wres_dec2, bres_dec2):
        import jax, jax.numpy as jnp
        import numpy as np
        N = 50000
        E = 25000
        IN, HID, OUT = (32, 64, 32)
        EPS = 1e-05

        def _gcn_norm(edge_index, n):
            loop = jnp.arange(n, dtype=edge_index.dtype)
            src = jnp.concatenate([edge_index[0], loop])
            dst = jnp.concatenate([edge_index[1], loop])
            deg = jax.ops.segment_sum(jnp.ones_like(dst, dtype=jnp.float32), dst, num_segments=n)
            dis = jnp.where(deg > 0, jax.lax.rsqrt(jnp.maximum(deg, 1.0)), 0.0)
            norm = dis[src] * dis[dst]
            return (src, dst, norm)

        def _gcn(x, W, b, src, dst, norm, n):
            xw = x @ W
            msg = xw[src] * norm[:, None]
            out = jax.ops.segment_sum(msg, dst, num_segments=n)
            return out + b

        def _bn(h, gamma, beta):
            mean = jnp.mean(h, axis=0)
            var = jnp.var(h, axis=0)
            return (h - mean) * jax.lax.rsqrt(var + EPS) * gamma + beta

        def _block(x, W, b, gamma, beta, src, dst, norm, n, Wr=None, br=None):
            identity = x if Wr is None else x @ Wr + br
            h = _gcn(x, W, b, src, dst, norm, n)
            h = jax.nn.relu(_bn(h, gamma, beta))
            return h + identity
        n = x.shape[0]
        src, dst, norm = _gcn_norm(edge_index, n)
        g, bt = (bn_gamma_hid, bn_beta_hid)
        go, bo = (bn_gamma_out, bn_beta_out)
        e1 = _block(x, W_enc1, b_enc1, g[0], bt[0], src, dst, norm, n, Wres_enc1, bres_enc1)
        e2 = _block(e1, W_hid[0], b_hid[0], g[1], bt[1], src, dst, norm, n)
        e3 = _block(e2, W_hid[1], b_hid[1], g[2], bt[2], src, dst, norm, n)
        m = _gcn(e1, W_hid[2], b_hid[2], src, dst, norm, n) + _gcn(e2, W_hid[3], b_hid[3], src, dst, norm, n) + _gcn(e3, W_hid[4], b_hid[4], src, dst, norm, n)
        d1 = _block(m, W_hid[5], b_hid[5], g[3], bt[3], src, dst, norm, n)
        d2 = _block(d1, W_dec2, b_dec2, go[0], bo[0], src, dst, norm, n, Wres_dec2, bres_dec2)
        d3 = _block(d2, W_dec3, b_dec3, go[1], bo[1], src, dst, norm, n)
        return d3

    def _L3_gnn_ref(x, edge_index, edge_attr, Wf1, bf1, Wf2, bf2, Wn1, bn1, Wn2, bn2):
        import jax, jax.numpy as jnp
        import numpy as np
        N_NODES = 50000
        N_EDGES = 25000
        NODE_D, EDGE_D = (32, 16)
        FLOW_IN, FLOW_H, FLOW_OUT = (2 * NODE_D + EDGE_D, 64, 64)
        NODE_H, NODE_OUT = (64, 32)

        def _mlp(h, W1, b1, W2, b2):
            h = jax.nn.relu(h @ W1 + b1)
            return h @ W2 + b2
        past, future = (edge_index[0], edge_index[1])
        x_p = x[past]
        x_f = x[future]
        flow_fwd = jnp.concatenate([x_f, x_p, edge_attr], axis=1)
        flow_bwd = jnp.concatenate([x_p, x_f, edge_attr], axis=1)
        flow_total_in = jnp.concatenate([flow_fwd, flow_bwd], axis=0)
        flow_processed = _mlp(flow_total_in, Wf1, bf1, Wf2, bf2)
        dest = jnp.concatenate([future, past], axis=0)
        flow_total = jax.ops.segment_sum(flow_processed, dest, num_segments=x.shape[0])
        return _mlp(flow_total, Wn1, bn1, Wn2, bn2)
    edge_index = jnp.stack([src, dst])
    h = jnp.maximum(_layernorm(x, axis=-1), 0.0)
    x = x + _L0_gnn_ref(h, edge_index, edge_attr_4, node_vec, L0_gnn_W_edge, L0_gnn_b_edge, L0_gnn_W_att, L0_gnn_b_att, L0_gnn_W_lar, L0_gnn_b_lar)
    h = jnp.maximum(_layernorm(x, axis=-1), 0.0)
    x = x + _L1_gnn_ref(h, edge_index, edge_weight1, edge_attr_3, edge_attr_5, L1_gnn_W)
    h = jnp.maximum(_layernorm(x, axis=-1), 0.0)
    x = x + _L2_gnn_ref(h, edge_index, L2_gnn_W_enc1, L2_gnn_b_enc1, L2_gnn_W_hid, L2_gnn_b_hid, L2_gnn_W_dec2, L2_gnn_b_dec2, L2_gnn_W_dec3, L2_gnn_b_dec3, L2_gnn_bn_gamma_hid, L2_gnn_bn_beta_hid, L2_gnn_bn_gamma_out, L2_gnn_bn_beta_out, L2_gnn_Wres_enc1, L2_gnn_bres_enc1, L2_gnn_Wres_dec2, L2_gnn_bres_dec2)
    h = jnp.maximum(_layernorm(x, axis=-1), 0.0)
    x = x + _L3_gnn_ref(h, edge_index, edge_attr_16, L3_gnn_Wf1, L3_gnn_bf1, L3_gnn_Wf2, L3_gnn_bf2, L3_gnn_Wn1, L3_gnn_bn1, L3_gnn_Wn2, L3_gnn_bn2)
    return x

_drawn_inputs = setup_inputs


def setup_inputs(seed=0):
    import zlib

    import numpy as np

    out = dict(_drawn_inputs(seed))
    spreads = {'L0_gnn_b_edge': (0.0, 0.8),
     'L2_gnn_b_enc1': (0.0, 2.0),
     'L2_gnn_b_hid': (0.0, 0.376),
     'L2_gnn_b_dec2': (0.0, 2.0),
     'L2_gnn_b_dec3': (0.0, 2.0),
     'L2_gnn_bn_gamma_hid': (1.0, 0.549),
     'L2_gnn_bn_beta_hid': (0.0, 0.497),
     'L2_gnn_bn_gamma_out': (1.0, 0.6),
     'L2_gnn_bn_beta_out': (0.0, 0.8),
     'L2_gnn_bres_enc1': (0.0, 0.483),
     'L2_gnn_bres_dec2': (0.0, 0.8),
     'L3_gnn_bf1': (0.0, 0.1),
     'L3_gnn_bf2': (0.0, 0.1),
     'L3_gnn_bn1': (0.0, 2.0),
     'L3_gnn_bn2': (0.0, 2.0)}
    factors = {'edge_attr_4': 6.393,
     'node_vec': 8.0,
     'L0_gnn_W_edge': 7.543,
     'L0_gnn_W_att': 3.181,
     'L0_gnn_W_lar': 5.645}
    for name, (base, spread) in spreads.items():
        noise = np.random.default_rng([zlib.crc32(name.encode()), seed]).standard_normal(out[name].shape)
        drawn = base * np.exp(spread * noise) if base else spread * noise
        out[name] = jnp.asarray(drawn.astype(out[name].dtype))
    for name, factor in factors.items():
        out[name] = (out[name] * factor).astype(out[name].dtype)
    return out
```

```python
from contextlib import ExitStack, contextmanager

import concourse.bass as bass
import numpy as np
from concourse import mybir

F32 = mybir.dt.float32
F16 = mybir.dt.float16
I32 = mybir.dt.int32
U32 = mybir.dt.uint32
ALU = mybir.AluOpType
ACT = mybir.ActivationFunctionType
X = mybir.AxisListType.X
ds = bass.ds

P = 128
N = 3125
NB = -(-N // P)
NP = NB * P
E = 100000
J = 4
TS = J * P
T = -(-E // TS)
EC = T * J
D = 32
K8 = 8
HALF = NP // 2
BIG = 1.0e30
EPS = 1e-5
GRID = np.linspace(-2.0, 2.0, K8, dtype=np.float32)
DENOM = float(GRID[1] - GRID[0])
QT = 4
QN = T // QT
AW = 36
GC = 8
GN = EC // GC // 2
assert T % QT == 0 and EC % (2 * GC) == 0 and T % 2 == 0
PHASES = 6


class Tools:

    def __init__(self, nc, ctx, stage):
        self.nc, self.ctx, self.stage, self.sems = nc, ctx, stage, []

    def sb(self, name, shape, dt=F32):
        return self.ctx.enter_context(self.nc.sbuf_tensor(f"{self.stage}_{name}", shape, dt))

    def ps(self, name, shape, dt=F32):
        return self.ctx.enter_context(self.nc.psum_tensor(f"{self.stage}_{name}", shape, dt))

    def sem(self, name):
        self.sems.append(self.ctx.enter_context(self.nc.semaphore(f"{self.stage}_{name}")))
        return self.sems[-1]


@contextmanager
def stage_tools(nc, stage):
    with ExitStack() as ctx:
        t = Tools(nc, ctx, stage)
        yield t
        with nc.Block() as block:
            @block.sync
            def _(e):
                for s in t.sems:
                    e.sem_clear(s)


class Chain:

    def __init__(self, eng, sem):
        self.eng, self.sem, self.n = eng, sem, 0

    def __call__(self, ins):
        ins.then_inc(self.sem, 1)
        self.n += 1
        self.eng.wait_ge(self.sem, self.n)
        return self.n


def bcast(ap, shape):
    return ap.broadcast_to(shape)


def setup(nc, g, a, dr):
    with stage_tools(nc, "setup") as t:
        s_load, s_pool, s_v, s_pe = t.sem("loaded"), t.sem("pool"), t.sem("vector"), t.sem("tensor")
        dst_t = t.sb("dst_t", [T // 2, 2 * TS], I32)
        dst_f = t.sb("dst_f", [T // 2, 2 * TS])
        dst_i = t.sb("dst_i", [P, EC], I32)
        hi_t, lo_t = t.sb("hi_t", [T // 2, 2]), t.sb("lo_t", [T // 2, 2])
        first_id, next_id = g.block_first, t.sb("next_id", [P, NB])
        rank, back = t.sb("rank", [P, 2]), t.sb("back", [P, 2])
        keys = t.sb("keys", [T // 2, 2, 2, NB])
        key = t.sb("key", [T // 2, 2 * NB])
        best, bounds = t.sb("best", [2 * NB, 1]), t.sb("bounds", [1, 2 * NB])
        ids = t.sb("ids", [P, NP])
        pk, pb = t.ps("pk", [2 * NB, P]), t.ps("pb", [1, 2 * NB])
        with nc.Block() as block:
            @block.sync
            def _(e):
                e.dma_start(g.src_i[:, :], a["src"]).then_inc(s_load, 16)
                e.dma_start(dst_i[:, :], a["dst"]).then_inc(s_load, 16)
                e.dma_start(dst_t[:, :], a["dst_rows"].rearrange("(p c) n -> p (c n)", c=2)).then_inc(s_load, 16)
                e.wait_ge(s_v, 8)
                e.dma_start(dr["dst"].rearrange("(p c) n -> p (c n)", c=2), dst_f[:, :]).then_inc(s_load, 16)
                e.wait_ge(s_load, 64)

            @block.gpsimd
            def _(e):
                e.iota(ids[:, :], [[1, NP]], base=-HALF, channel_multiplier=0,
                       allow_small_or_imprecise_dtypes=True).then_inc(s_pool, 1)
                e.iota(g.pcol[:, :], [[1, 1]], base=0, channel_multiplier=1,
                       allow_small_or_imprecise_dtypes=True).then_inc(s_pool, 1)
                e.iota(g.node_id[:, :], [[P, NB]], base=0, channel_multiplier=1,
                       allow_small_or_imprecise_dtypes=True).then_inc(s_pool, 1)
                e.iota(g.iota[:, :], [[1, P]], base=0, channel_multiplier=0,
                       allow_small_or_imprecise_dtypes=True).then_inc(s_pool, 1)
                e.iota(first_id[:, :], [[P, NB + 1]], base=0, channel_multiplier=0,
                       allow_small_or_imprecise_dtypes=True).then_inc(s_pool, 1)
                e.iota(next_id[:, :], [[P, NB]], base=P, channel_multiplier=0,
                       allow_small_or_imprecise_dtypes=True).then_inc(s_pool, 1)
                e.iota(rank[:, :], [[1, 2]], base=1, channel_multiplier=2,
                       allow_small_or_imprecise_dtypes=True).then_inc(s_pool, 1)
                e.iota(back[:, :], [[-1, 2]], base=T, channel_multiplier=-2,
                       allow_small_or_imprecise_dtypes=True).then_inc(s_pool, 1)

            @block.vector
            def _(e):
                c = Chain(e, s_v)
                c(e.memset(g.ones[:, :], 1.0))
                e.wait_ge(s_pool, 8)
                c(e.tensor_copy(g.ids16[:, :], ids[:, :]))
                c(e.tensor_scalar(g.ident[:, :], g.iota[:, :], g.pcol[:, 0:1], None, ALU.is_equal))
                c(e.tensor_copy(g.ident16[:, :], g.ident[:, :]))
                e.wait_ge(s_load, 48)
                c(e.tensor_copy(g.dst_f[:, :], dst_i[:, :]))
                c(e.tensor_copy(g.src_f[:, :], g.src_i[:, :]))
                c(e.tensor_scalar(g.src_f[:, :], g.src_f[:, :], -float(HALF), None, ALU.add))
                c(e.tensor_copy(dst_f[:, :], dst_t[:, :]))
                rows = dst_f[:, :].rearrange("p (c n) -> p c n", c=2)
                c(e.tensor_reduce(hi_t[:, :], rows, X, ALU.max))
                c(e.tensor_reduce(lo_t[:, :], rows, X, ALU.min))
                n2 = T // 2
                for k in range(2):
                    c(e.tensor_scalar(keys[:, 0, k, :], first_id[0:n2, 0:NB], hi_t[:, k:k + 1], back[0:n2, k:k + 1],
                                      ALU.is_le, ALU.mult))
                    c(e.tensor_scalar(keys[:, 1, k, :], next_id[0:n2, :], lo_t[:, k:k + 1], rank[0:n2, k:k + 1],
                                      ALU.is_gt, ALU.mult))
                c(e.tensor_tensor(key[:, :].rearrange("p (a b) -> p a b", a=2), keys[:, :, 0, :], keys[:, :, 1, :],
                                  ALU.max))
                e.wait_ge(s_pe, 1)
                c(e.tensor_reduce(best[:, :], pk[:, 0:n2], X, ALU.max))
                e.wait_ge(s_pe, 2)
                c(e.tensor_scalar(bounds[:, 0:NB], pb[:, 0:NB], -1.0, float(T), ALU.mult, ALU.add))
                c(e.tensor_copy(bounds[:, NB:], pb[:, NB:]))
                c(e.tensor_copy(g.bounds[:, :], bounds[:, :]))
                g.setup_v = c.n

            @block.tensor
            def _(e):
                e.wait_ge(s_v, 15)
                e.transpose(pk[:, 0:T // 2], key[:, :], g.ident[0:T // 2, 0:T // 2]).then_inc(s_pe, 1)
                e.wait_ge(s_v, 16)
                e.transpose(pb[:, :], best[:, :], g.ident[0:2 * NB, 0:2 * NB]).then_inc(s_pe, 1)


def layernorm_relu(e, c, wait_scalar, t, x, h, s_root):
    m, v, sq = t
    c(e.tensor_reduce(m[:, :], x, X, ALU.add))
    c(e.tensor_scalar(m[:, :], m[:, :], 1.0 / D, None, ALU.mult))
    c(e.tensor_tensor(h, x, bcast(m[:, :].unsqueeze(2), [P, NB, D]), ALU.subtract))
    c(e.tensor_tensor(sq, h, h, ALU.mult))
    c(e.tensor_reduce(v[:, :], sq, X, ALU.add))
    c(e.tensor_scalar(v[:, :], v[:, :], 1.0 / D, EPS, ALU.mult, ALU.add))
    wait_scalar()
    c(e.reciprocal(v[:, :], v[:, :]))
    c(e.tensor_tensor(h, h, bcast(v[:, :].unsqueeze(2), [P, NB, D]), ALU.mult))
    c(e.tensor_scalar(h, h, 0.0, None, ALU.max))


def table0(nc, g, a, dr):
    with stage_tools(nc, "table0") as t:
        s_load, s_v, s_a, s_out = t.sem("loaded"), t.sem("vector"), t.sem("scalar"), t.sem("stored")
        m, v = t.sb("mean", [P, NB]), t.sb("var", [P, NB])
        h, sq = t.sb("h", [P, NB, D]), t.sb("sq", [P, NB, D])
        z, w = t.sb("z", [P, NB, D, K8]), t.sb("w", [P, D * K8])
        grid, wl = t.sb("grid", [P, K8]), t.sb("wl", [P, K8])
        ba, bl = t.sb("ba", [P, 1]), t.sb("bl", [P, 1])
        cnt, zc = t.sb("cnt", [P, NB]), t.sb("zc", [P, NB, K8])
        u, ua, ul = t.sb("u", [P, NB]), t.sb("ua", [P, NB]), t.sb("ul", [P, NB])
        tab = t.sb("tab", [P, NB, AW])
        with nc.Block() as block:
            @block.vector
            def _(e):
                c = Chain(e, s_v)
                e.wait_ge(s_load, 16 * 7)
                c(e.memset(tab[:, :, :], 0.0))
                layernorm_relu(e, c, lambda: e.wait_ge(s_a, 1), (m, v, sq[:, :, :]), g.x[:, :, :], h[:, :, :], None)
                gz = grid[:, :].unsqueeze(1).unsqueeze(1)
                c(e.tensor_tensor(z[:, :, :, :], bcast(h[:, :, :].unsqueeze(3), [P, NB, D, K8]),
                                  bcast(gz, [P, NB, D, K8]), ALU.subtract))
                c(e.tensor_tensor(z[:, :, :, :], z[:, :, :, :], z[:, :, :, :], ALU.mult))
                c(e.tensor_tensor(zc[:, :, :], bcast(cnt[:, :].unsqueeze(2), [P, NB, K8]),
                                  bcast(grid[:, :].unsqueeze(1), [P, NB, K8]), ALU.subtract))
                g.t0_exp = c(e.tensor_tensor(zc[:, :, :], zc[:, :, :], zc[:, :, :], ALU.mult))
                e.wait_ge(s_a, 3)
                wz = w[:, :].rearrange("p (f k) -> p f k", k=K8).unsqueeze(1)
                c(e.tensor_tensor(z[:, :, :, :], z[:, :, :, :], bcast(wz, [P, NB, D, K8]), ALU.mult))
                c(e.tensor_reduce(u[:, :], z[:, :, :, :].rearrange("p b f k -> p b (f k)"), X, ALU.add))
                c(e.tensor_scalar(tab[:, :, D], u[:, :], ba[:, 0:1], None, ALU.add))
                c(e.tensor_tensor(zc[:, :, :], zc[:, :, :], bcast(wl[:, :].unsqueeze(1), [P, NB, K8]), ALU.mult))
                c(e.tensor_reduce(u[:, :], zc[:, :, :], X, ALU.add))
                c(e.tensor_scalar(u[:, :], u[:, :], bl[:, 0:1], None, ALU.add))
                c(e.tensor_scalar(ua[:, :], u[:, :], -1.0, None, ALU.mult))
                g.t0_abs = c(e.tensor_tensor(ua[:, :], ua[:, :], u[:, :], ALU.min))
                e.wait_ge(s_a, 5)
                c(e.tensor_scalar(u[:, :], u[:, :], 0.0, None, ALU.max))
                c(e.tensor_tensor(ul[:, :], ul[:, :], u[:, :], ALU.add))
                g.t0_done = c(e.tensor_tensor(tab[:, :, 0:D], h[:, :, :],
                                              bcast(ul[:, :].unsqueeze(2), [P, NB, D]), ALU.mult))

            @block.sync
            def _(e):
                e.dma_start(g.x[:, :, :], a["x"].rearrange("(b p) f -> p b f", p=P)).then_inc(s_load, 16)
                e.dma_start(cnt[:, :], a["node_vec"]).then_inc(s_load, 16)
                e.dma_start(w[:, :], a["W_att"][0:1, D * K8:].partition_broadcast(P)).then_inc(s_load, 16)
                e.dma_start(wl[:, :], a["W_lar"][0:1, :].partition_broadcast(P)).then_inc(s_load, 16)
                e.dma_start(ba[:, :], a["b_att"].unsqueeze(0).partition_broadcast(P)).then_inc(s_load, 16)
                e.dma_start(bl[:, :], a["b_lar"].unsqueeze(0).partition_broadcast(P)).then_inc(s_load, 16)
                e.dma_start(grid[:, :], a["grid"][0:1, :].partition_broadcast(P)).then_inc(s_load, 16)
                e.wait_ge(s_v, g.t0_done)
                e.dma_start(dr["table0"].rearrange("(b p) f -> p b f", p=P), tab[:, :, :]).then_inc(s_out, 16)
                e.wait_ge(s_out, 16)

            @block.scalar
            def _(e):
                e.wait_ge(s_v, 7)
                e.activation(v[:, :], v[:, :], ACT.Sqrt).then_inc(s_a, 1)
                e.wait_ge(s_v, g.t0_exp)
                e.activation(z[:, :, :, :], z[:, :, :, :], ACT.Exp, scale=-1.0 / DENOM ** 2).then_inc(s_a, 1)
                e.activation(zc[:, :, :], zc[:, :, :], ACT.Exp, scale=-1.0 / DENOM ** 2).then_inc(s_a, 1)
                e.wait_ge(s_v, g.t0_abs)
                e.activation(ul[:, :], ua[:, :], ACT.Exp).then_inc(s_a, 1)
                e.wait_ge(s_a, 4)
                e.activation(ul[:, :], ul[:, :], ACT.Ln, bias=1.0).then_inc(s_a, 1)



def edge_logits(nc, g, a, dr):
    with stage_tools(nc, "logit") as t:
        s_load, s_w = t.sem("loaded"), t.sem("weights")
        s_p1, s_sq1, s_r1 = t.sem("spread"), t.sem("squared1"), t.sem("bases1")
        s_z2, s_sq2, s_r2 = t.sem("features"), t.sem("squared2"), t.sem("bases2")
        s_wr, s_wd, s_at, s_ev = t.sem("half_weighed"), t.sem("weighed"), t.sem("summed"), t.sem("copied")
        s_out, s_st = t.sem("landed"), t.sem("stored")
        ea = t.sb("ea", [4 * QT, QN * TS])
        spread, bias1 = t.sb("spread", [4 * QT, P]), t.sb("bias1", [P, 1])
        w_edge, watt = t.sb("w_edge", [P, QT, 2 * P]), t.sb("watt", [P, 2])
        bias2, gcol, brep = t.sb("bias2", [P, 2]), t.sb("gcol", [P, 1]), t.sb("brep", [P, 2])
        pick = t.sb("pick", [P, QT, QT])
        r1, r2 = t.sb("r1", [P, 2, TS]), t.sb("r2", [P, 2, 2, TS])
        wr, wd = t.sb("wr", [P, 2, TS]), t.sb("wd", [P, 2, TS])
        el = t.sb("el", [QT, 2, TS])
        p1, pa = t.ps("p1", [P, TS]), [t.ps(f"pa{i}", [QT, TS]) for i in range(2)]
        z2 = [t.ps(f"z2_{i}", [P, 2, TS]) for i in range(2)]
        with nc.Block() as block:
            def steps(eng, step):
                with eng.Fori(0, QN // 2, 1) as k:
                    step(2 * k, 0)
                    step(2 * k + 1, 1)
                step(QN - 1, 0)

            @block.sync
            def _(e):
                for dst_ap, src_ap in ((spread[:, :], a["spread"]), (bias1[:, :], a["bias1"]), (w_edge[:, :, :], a["W_edge"]),
                                       (watt[:, :], a["W_att_edge"]), (brep[:, :], a["b_edge"]), (gcol[:, :], a["grid_col"]),
                                       (ea[:, :], a["edge_attr_4"])):
                    e.dma_start(dst_ap, src_ap).then_inc(s_load, 16)

                def step(i, par):
                    e.wait_ge(s_ev, i + 3)
                    e.dma_start(dr["edge_logit"][ds(i * QT, QT), :], el[:, par, :]).then_inc(s_out, 16)
                    e.wait_ge(s_out, 16 * (i + 1))
                    e.sem_inc(s_st, 1)
                e.sem_inc(s_st, 2)
                steps(e, step)

            @block.vector
            def _(e):
                c = Chain(e, s_w)
                e.wait_ge(s_load, 16 * 7)
                c(e.memset(pick[:, :, :], 0.0))
                for q in range(QT):
                    c(e.memset(pick[:, q, q:q + 1], 1.0))
                c(e.tensor_tensor(bias2[:, :], brep[:, :], bcast(gcol[:, 0:1], [P, 2]), ALU.subtract))
                c(e.tensor_scalar(bias2[:, :], bias2[:, :], 1.0 / DENOM, None, ALU.mult))

                e.sem_inc(s_wd, 2)
                e.sem_inc(s_ev, 2)

                def step(i, par):
                    for q in range(QT):
                        n, s = i * QT + q, q % 2
                        e.wait_ge(s_r2, n + 3)
                        e.tensor_scalar(wr[:, s, :], r2[:, s, 0, :], watt[:, 0:1], None, ALU.mult).then_inc(s_wr, 1)
                        e.wait_ge(s_wr, n + 1)
                        e.wait_ge(s_at, n + 1)
                        e.scalar_tensor_tensor(wd[:, s, :], r2[:, s, 1, :], watt[:, 1:2], wr[:, s, :],
                                               ALU.mult, ALU.add).then_inc(s_wd, 1)
                    e.wait_ge(s_at, i * QT + QT + 2)
                    e.wait_ge(s_st, i + 1)
                    e.tensor_copy(el[:, par, :], pa[par][:, :]).then_inc(s_ev, 1)
                steps(e, step)

            @block.scalar
            def _(e):
                e.wait_ge(s_w, 7)
                e.sem_inc(s_r2, 2)

                def bases1(i, par):
                    e.wait_ge(s_p1, i + 1)
                    e.activation(r1[:, par, :], p1[:, :], ACT.Square, bias=bias1[:, 0:1]).then_inc(s_sq1, 1)
                    e.wait_ge(s_sq1, i + 1)
                    e.activation(r1[:, par, :], r1[:, par, :], ACT.Exp, scale=-1.0).then_inc(s_r1, 1)

                def step(i, par, last=False):
                    for q in range(QT):
                        n, s = i * QT + q, q % 2
                        e.wait_ge(s_z2, n + 1)
                        e.wait_ge(s_wd, n + 1)
                        for h in range(2):
                            e.activation(r2[:, s, h, :], z2[s][:, h, :], ACT.Square, bias=bias2[:, h:h + 1],
                                         scale=1.0 / DENOM).then_inc(s_sq2, 1)
                        e.wait_ge(s_sq2, 2 * n + 2)
                        e.activation(r2[:, s, :, :], r2[:, s, :, :], ACT.Exp, scale=-1.0).then_inc(s_r2, 1)
                        if q == 1 and not last:
                            bases1(i + 1, 1 - par)
                bases1(0, 0)
                with e.Fori(0, QN // 2, 1) as k:
                    step(2 * k, 0)
                    step(2 * k + 1, 1)
                step(QN - 1, 0, True)

            @block.tensor
            def _(e):
                e.wait_ge(s_w, 7)
                e.sem_inc(s_at, 2)

                def expand(i):
                    e.matmul(p1[:, :], spread[:, :], ea[:, ds(i * TS, TS)], start=True, stop=True).then_inc(s_p1, 1)

                def features(n, par, q):
                    for h in range(2):
                        m = e.matmul(z2[q % 2][:, h, :], w_edge[:, q, h * P:(h + 1) * P],
                                     r1[:, par, :], start=True, stop=True)
                    m.then_inc(s_z2, 1)

                def weigh(n, par, q):
                    e.wait_ge(s_wd, n + 3)
                    e.matmul(pa[par][:, :], pick[:, q, :], wd[:, q % 2, :], start=(q == 0), stop=(q == QT - 1)).then_inc(s_at, 1)

                def step(i, par, last=False):
                    for q in range(QT):
                        n = i * QT + q
                        if q == 0:
                            e.wait_ge(s_r1, i + 1)
                        e.wait_ge(s_r2, n + 1)
                        features(n, par, q)
                        if q == 0 and not last:
                            e.wait_ge(s_sq1, i + 1)
                            expand(i + 1)
                        if q == 0:
                            e.wait_ge(s_ev, i + 1)
                        if q > 0:
                            weigh(n - 1, par, q - 1)
                    weigh(i * QT + QT - 1, par, QT - 1)
                expand(0)
                with e.Fori(0, QN // 2, 1) as k:
                    step(2 * k, 0)
                    step(2 * k + 1, 1)
                step(QN - 1, 0, True)


def node_gather(e, t, g, table, width, slots, everything, s_slot, s_claim, s_kept):
    idx = t.sb("idx", [P, 2, GC], I32)
    s_idx = t.sem("idx")

    def fetch(c, k, h):
        e.wait_ge(s_slot[h][1], k + 1)
        e.sem_inc(s_claim, 1)
        e.tensor_copy(idx[:, h, :], g.src_i[:, ds(c * GC, GC)]).then_inc(s_idx, 1)
        e.wait_ge(s_idx, c + 1)
        e.sem_inc(s_claim, 1)
        for j in range(GC):
            e.indirect_dma_start(slots[:, h, j, :], None, table,
                                 bass.IndirectOffsetOnAxis(ap=idx[:, h, j:j + 1].bitcast(U32), axis=0)).then_inc(s_slot[h][0], 16)

    def keep(c, k, h):
        e.wait_ge(s_slot[h][0], 16 * GC * (k + 1))
        e.sem_inc(s_claim, 1)
        e.tensor_copy(everything[:, ds(c * GC, GC), :], slots[:, h, :, 0:width]).then_inc(s_kept, 2)
        e.wait_ge(s_kept, 2 * (c + 1))
        e.sem_inc(s_slot[h][1], 1)

    e.sem_inc(s_slot[0][1], 1)
    e.sem_inc(s_slot[1][1], 1)
    fetch(0, 0, 0)
    fetch(1, 0, 1)
    with e.Fori(1, GN, 1) as i:
        keep(2 * i - 2, i - 1, 0)
        fetch(2 * i, i, 0)
        keep(2 * i - 1, i - 1, 1)
        fetch(2 * i + 1, i, 1)
    keep(2 * GN - 2, GN - 1, 0)
    keep(2 * GN - 1, GN - 1, 1)


def block_range(e, g, b):
    return (e.value_load(g.bounds[0:1, ds(b, 1)], min_val=0, max_val=T - 1),
            e.value_load(g.bounds[0:1, ds(b + NB, 1)], min_val=0, max_val=T))


class Count:

    def __init__(self, e, name, most):
        self.e, self.most = e, most
        self.reg = e.alloc_register(name)
        e.reg_mov(self.reg, 0)

    def now(self):
        return self.e.snap(self.reg, min_val=0, max_val=self.most)

    def up(self):
        self.e.reg_add(self.reg, self.reg, 1)


VISITS = NB * T
CB = -(-NP // 512)


def count_and_gather(nc, g, a, dr, G):
    with stage_tools(nc, "count") as t:
        s_slot = [(g.rows_landed[0][h], t.sem(f"free{h}")) for h in range(2)]
        s_claim, s_kept = t.sem("claim"), t.sem("kept")
        s_ib, s_oh, s_used, s_sum, s_ev, s_out, s_st = (t.sem(n) for n in (
            "block_ids", "onehot", "used", "summed", "copied", "landed", "stored"))
        s_z, s_turn = t.sem("zeros"), t.sem("turn")
        slots = t.sb("slots", [P, 2, GC, AW])
        ids_b = t.sb("ids_b", [P, P])
        ohs = t.sb("ohs", [P, J, NP], F16)
        ohd = t.sb("ohd", [P, J, P], F16)
        zero = t.sb("zero", [1, 512], F16)
        row = t.sb("row", [P, 2, NP], F16)
        degc = t.sb("degc", [P, NB, CB])
        acc = t.ps("acc", [P, CB, 512])
        with nc.Block() as block:
            @block.gpsimd
            def _(e):
                node_gather(e, t, g, dr["table0"][:, :], D + 1, slots, G, s_slot, s_claim, s_kept)

            @block.vector
            def _(e):
                e.memset(zero[:, :], 0.0).then_inc(s_z, 1)
                v = Count(e, "v", VISITS)
                with e.Fori(0, NB, 1) as b:
                    lo, hi = block_range(e, g, b)
                    e.tensor_scalar(ids_b[:, :], g.iota[:, :], g.block_first[:, ds(b, 1)], None, ALU.add).then_inc(s_ib, 1)
                    e.wait_ge(s_ib, b + 1)
                    e.sem_inc(s_turn, 1)
                    with e.Fori(lo, hi, 1) as tt:
                        n = v.now()
                        for j in range(J):
                            e.wait_ge(s_used, n * J + j + 1)
                            e.tensor_scalar(ohd[:, j, :], ids_b[:, :], g.dst_f[:, ds(tt * J + j, 1)], None, ALU.is_equal).then_inc(s_oh, 1)
                            e.tensor_scalar(ohs[:, j, :], g.ids16[:, :], g.src_f[:, ds(tt * J + j, 1)], None, ALU.is_equal).then_inc(s_oh, 1)
                        v.up()
                    e.wait_ge(s_oh, v.now() * (2 * J))
                    e.sem_inc(s_turn, 1)

            @block.tensor
            def _(e):
                e.wait_ge(s_z, 1)
                e.sem_inc(s_used, J)
                v = Count(e, "v", VISITS)
                with e.Fori(0, NB, 1) as b:
                    lo, hi = block_range(e, g, b)
                    e.wait_ge(s_ev, CB * b + 1)
                    for k in range(CB):
                        if k:
                            e.wait_ge(s_ev, CB * b + k + 1)
                        w = min(512, NP - 512 * k)
                        e.matmul(acc[:, k, 0:w], zero[0:1, 0:P], zero[0:1, 0:w], start=True, stop=False, skip_group_check=True)
                    with e.Fori(lo, hi, 1) as tt:
                        n = v.now()
                        for j in range(J):
                            e.wait_ge(s_oh, (n * J + j) * 2 + 2)
                            for k in range(CB):
                                w = min(512, NP - 512 * k)
                                m = e.matmul(acc[:, k, 0:w], ohd[:, j, :], ohs[:, j, 512 * k:512 * k + w],
                                             start=False, stop=False, skip_group_check=True)
                            m.then_inc(s_used, 1)
                        v.up()
                    e.matmul(acc[:, CB - 1, 0:P], zero[0:1, 0:P], zero[0:1, 0:P], start=False, stop=True,
                             skip_group_check=True).then_inc(s_sum, 1)

            @block.scalar
            def _(e):
                e.sem_inc(s_ev, CB)
                with e.Fori(0, NB, 1) as b:
                    e.wait_ge(s_sum, b + 1)
                    e.wait_ge(s_st, b + 1)
                    for k in range(CB):
                        w = min(512, NP - 512 * k)
                        e.activation(row[:, ds(b % 2, 1), 512 * k:512 * k + w].rearrange("p a n -> p (a n)"), acc[:, k, 0:w],
                                     ACT.Copy, accum_out=degc[:, ds(b, 1), k:k + 1].rearrange("p a n -> p (a n)")).then_inc(s_ev, 1)

            @block.sync
            def _(e):
                e.sem_inc(s_st, 2)
                with e.Fori(0, NB, 1) as b:
                    e.wait_ge(s_ev, CB * (b + 2))
                    e.dma_start(dr["counts"][ds(b * P, P), :], row[:, ds(b % 2, 1), :].rearrange("p a n -> p (a n)")).then_inc(s_out, 16)
                    e.wait_ge(s_out, 16 * (b + 1))
                    e.sem_inc(s_st, 1)
        s_d = t.sem("degree")
        with nc.Block() as block:
            @block.vector
            def _(e):
                e.tensor_reduce(g.deg[:, :], degc[:, :, :], X, ALU.add).then_inc(s_d, 1)
                e.wait_ge(s_d, 1)


def pair_range(e, g, b):
    lo, hi = block_range(e, g, b)
    return e.snap(lo // 2, min_val=0, max_val=T // 2 - 1), e.snap((hi + 1) // 2, min_val=0, max_val=T // 2)


def attention(nc, g, a, dr, G):
    bf = mybir.dt.bfloat16
    R = EC // 7
    with stage_tools(nc, "attn") as t:
        s_load, s_pe, s_v, s_a, s_out = (t.sem(n) for n in ("loaded", "tensor", "vector", "scalar", "stored"))
        cols, back = t.sb("cols", [R, 7, P]), t.sb("back", [R, 7, P])
        raw = t.sb("raw", [P, EC])
        pc = t.ps("pc", [P, 2, 512])
        pr = t.ps("pr", [R, 2, 512])
        with nc.Block() as block:
            @block.sync
            def _(e):
                e.dma_start(cols[:, :, :], dr["edge_logit"].rearrange("t (j n) -> (t j) n", n=P)
                            .rearrange("(c r) n -> r c n", r=R)).then_inc(s_load, 16)
                e.wait_ge(s_a, 2)
                e.dma_start(dr["raw"].rearrange("t (j n) -> (t j) n", n=P).rearrange("(c r) n -> r c n", r=R),
                            back[:, :, :]).then_inc(s_out, 16)
                e.dma_start(dr["raw_cols"], raw[:, :]).then_inc(s_out, 16)
                e.wait_ge(s_out, 32)

            @block.tensor
            def _(e):
                e.wait_ge(s_load, 16)
                for c in range(7):
                    m = e.transpose(pc[:, c // 4, (c % 4) * R:(c % 4 + 1) * R], cols[:, c, :], g.ident[0:R, 0:R])
                m.then_inc(s_pe, 1)
                e.wait_ge(s_v, 2)
                for c in range(7):
                    m = e.transpose(pr[:, c // 4, (c % 4) * P:(c % 4 + 1) * P], raw[:, c * R:(c + 1) * R], g.ident[:, :])
                m.then_inc(s_pe, 1)

            @block.vector
            def _(e):
                e.wait_ge(s_pe, 1)
                e.tensor_tensor(raw[:, 0:4 * R], pc[:, 0, 0:4 * R], G[:, 0:4 * R, D], ALU.add).then_inc(s_v, 1)
                e.tensor_tensor(raw[:, 4 * R:], pc[:, 1, 0:3 * R], G[:, 4 * R:, D], ALU.add).then_inc(s_v, 1)
                e.wait_ge(s_v, 2)
                e.memset(G[:, :, D:D + 1], 1.0).then_inc(s_v, 1)

            @block.scalar
            def _(e):
                e.wait_ge(s_pe, 2)
                e.activation(back[:, 0:4, :], pr[:, 0, :].rearrange("p (c n) -> p c n", n=P), ACT.Copy).then_inc(s_a, 1)
                e.activation(back[:, 4:7, :], pr[:, 1, 0:3 * P].rearrange("p (c n) -> p c n", n=P), ACT.Copy).then_inc(s_a, 1)

    with stage_tools(nc, "amax") as t:
        s_ld = [t.sem(f"loaded{i}") for i in range(2)]
        s_free = [t.sem(f"free{i}") for i in range(2)]
        s_mld = [t.sem(f"mloaded{i}") for i in range(2)]
        s_mfree = [t.sem(f"mfree{i}") for i in range(2)]
        s_v, s_m, s_mask, s_used, s_z, s_last, s_rl, s_a, s_turn = (t.sem(n) for n in (
            "step", "maximum", "mask", "used", "zeros", "last", "logits", "scalar", "turn"))
        raw_b, dst_b = t.sb("raw_b", [P, 2, TS]), t.sb("dst_b", [P, 2, TS])
        dst_m = t.sb("dst_m", [P, 2, TS])
        pen, dump = t.sb("pen", [P, 2, TS]), t.sb("dump", [P, 2, TS])
        top, best = t.sb("top", [P, 2]), t.sb("best", [P, 1])
        part, rest = t.sb("part", [P, 3], bf), t.sb("rest", [P, 2])
        mask = t.sb("mask", [P, 2, TS], bf)
        zero = t.sb("zero", [1, 512], bf)
        me, w = t.sb("me", [P, EC]), t.sb("w", [P, EC])
        raw = t.sb("raw", [P, EC])
        MB = -(-EC * 4 // 512)
        pm = t.ps("pm", [P, MB * 512])
        with nc.Block() as block:
            @block.sync
            def _(e):
                v, m = Count(e, "amax_sync", VISITS), Count(e, "amax_sync2", VISITS)
                e.dma_start(raw[:, :], dr["raw_cols"]).then_inc(s_rl, 16)
                for s in range(2):
                    e.sem_inc(s_free[s], 1)
                    e.sem_inc(s_mfree[s], 1)
                with e.Fori(0, NB, 1) as b:
                    lo, hi = pair_range(e, g, b)
                    with e.Fori(lo, hi, 1) as u:
                        n = v.now()
                        for s in range(2):
                            e.wait_ge(s_free[s], n + 1)
                            e.dma_start(raw_b[:, s, :], dr["raw"][ds(u * 2 + s, 1), :].partition_broadcast(P)).then_inc(s_ld[s], 16)
                            e.dma_start(dst_b[:, s, :], dr["dst"][ds(u * 2 + s, 1), :].partition_broadcast(P)).then_inc(s_ld[s], 16)
                        v.up()
                    with e.Fori(lo, hi, 1) as u:
                        n = m.now()
                        for s in range(2):
                            e.wait_ge(s_mfree[s], n + 1)
                            e.dma_start(dst_m[:, s, :], dr["dst"][ds(u * 2 + s, 1), :].partition_broadcast(P)).then_inc(s_mld[s], 16)
                        m.up()

            @block.vector
            def _(e):
                v, m = Count(e, "amax_v", VISITS), Count(e, "amax_m", VISITS)
                c = Chain(e, s_z)
                c(e.memset(zero[:, :], 0.0))
                c(e.memset(top[:, :], -BIG))
                e.sem_inc(s_m, 1)
                with e.Fori(0, NB, 1) as b:
                    lo, hi = pair_range(e, g, b)
                    e.wait_ge(s_m, b * 8 + 1)
                    e.memset(best[:, :], -0.1 * BIG).then_inc(s_m, 1)
                    e.wait_ge(s_m, b * 8 + 2)
                    e.sem_inc(s_turn, 1)
                    with e.Fori(lo, hi, 1) as u:
                        n = v.now()
                        for s in range(2):
                            e.wait_ge(s_ld[s], 32 * n + 32)
                            e.tensor_scalar(pen[:, s, :], dst_b[:, s, :], g.node_id[:, ds(b, 1)], -BIG,
                                            ALU.not_equal, ALU.mult).then_inc(s_v, 1)
                            e.wait_ge(s_v, n * 6 + 3 * s + 1)
                            e.sem_inc(s_turn, 1)
                            e.tensor_tensor_reduce(dump[:, s, :], raw_b[:, s, :], pen[:, s, :], 1.0, -BIG,
                                                   ALU.add, ALU.max, top[:, s:s + 1]).then_inc(s_v, 1)
                            e.wait_ge(s_v, n * 6 + 3 * s + 2)
                            e.sem_inc(s_free[s], 1)
                            e.tensor_tensor(best[:, :], best[:, :], top[:, s:s + 1], ALU.max).then_inc(s_v, 1)
                            e.wait_ge(s_v, n * 6 + 3 * s + 3)
                        v.up()
                    e.wait_ge(s_last, b + 1)
                    e.tensor_copy(part[:, 0:1], best[:, :]).then_inc(s_m, 1)
                    e.wait_ge(s_m, b * 8 + 3)
                    e.tensor_tensor(rest[:, 0:1], best[:, :], part[:, 0:1], ALU.subtract).then_inc(s_m, 1)
                    e.wait_ge(s_m, b * 8 + 4)
                    e.tensor_copy(part[:, 1:2], rest[:, 0:1]).then_inc(s_m, 1)
                    e.wait_ge(s_m, b * 8 + 5)
                    e.tensor_tensor(rest[:, 1:2], rest[:, 0:1], part[:, 1:2], ALU.subtract).then_inc(s_m, 1)
                    e.wait_ge(s_m, b * 8 + 6)
                    e.tensor_copy(part[:, 2:3], rest[:, 1:2]).then_inc(s_m, 1)
                    e.wait_ge(s_m, b * 8 + 7)
                    e.sem_inc(s_m, 2)
                    with e.Fori(lo, hi, 1) as u:
                        n = m.now()
                        for s in range(2):
                            e.wait_ge(s_mld[s], 16 * n + 16)
                            e.wait_ge(s_used, n * 2 + s + 1)
                            e.tensor_scalar(mask[:, s, :], dst_m[:, s, :], g.node_id[:, ds(b, 1)], None,
                                            ALU.is_equal).then_inc(s_mask, 1)
                            e.wait_ge(s_mask, n * 2 + s + 1)
                            e.sem_inc(s_mfree[s], 1)
                        m.up()
                e.wait_ge(s_last, NB + 1)
                p4 = pm[:, 0:EC * 4].rearrange("p (c k) -> p c k", k=4)
                e.wait_ge(s_rl, 16)
                c(e.tensor_copy(w[:, :], p4[:, :, 2]))
                c(e.tensor_tensor(w[:, :], w[:, :], p4[:, :, 1], ALU.add))
                c(e.tensor_tensor(w[:, :], w[:, :], p4[:, :, 0], ALU.add))
                c(e.tensor_tensor(w[:, :], raw[:, :], w[:, :], ALU.subtract))
                g.am_w = c(e.tensor_scalar(w[:, :], w[:, :], 0.0, None, ALU.min))
                e.wait_ge(s_a, 1)
                c(e.tensor_tensor(G[:, :, 0:D + 1], G[:, :, 0:D + 1], bcast(w[:, :].unsqueeze(2), [P, EC, D + 1]), ALU.mult))

            @block.scalar
            def _(e):
                e.wait_ge(s_z, g.am_w)
                e.activation(w[:, :], w[:, :], ACT.Exp).then_inc(s_a, 1)

            @block.tensor
            def _(e):
                v = Count(e, "amax_pe", VISITS)
                e.wait_ge(s_z, 1)
                e.sem_inc(s_used, 2)
                for k in range(MB):
                    e.matmul(pm[:, 512 * k:512 * k + 512], zero[0:1, 0:P], zero[0:1, :], start=True, stop=False,
                             skip_group_check=True)
                e.sem_inc(s_last, 1)
                with e.Fori(0, NB, 1) as b:
                    lo, hi = pair_range(e, g, b)
                    e.wait_ge(s_m, b * 8 + 7)
                    e.sem_inc(s_turn, 1)
                    with e.Fori(lo, hi, 1) as u:
                        n = v.now()
                        for s in range(2):
                            e.wait_ge(s_mask, n * 2 + s + 1)
                            for j in range(J):
                                mm = e.matmul(pm[:, ds((u * 2 + s) * (4 * J) + 4 * j, 3)], mask[:, s, j * P:(j + 1) * P], part[:, :],
                                              start=False, stop=False, skip_group_check=True)
                            mm.then_inc(s_used, 1)
                        v.up()
                    e.matmul(pm[:, 0:1], zero[0:1, 0:P], zero[0:1, 0:1], start=False, stop=True,
                             skip_group_check=True).then_inc(s_last, 1)


H9 = 9
BW = 96


def scatter(nc, g, dr, G, sums, harmonics=None, table=None):
    width = H9 * D if harmonics is not None else D + 1
    with stage_tools(nc, "scatter1" if harmonics is not None else "scatter0") as t:
        s_oh = [t.sem(f"onehot{s}") for s in range(2)]
        s_used = [t.sem(f"used{s}") for s in range(2)]
        s_ib, s_z, s_sum, s_ev, s_load, s_turn = (t.sem(n) for n in (
            "block_ids", "zeros", "summed", "copied", "loaded", "turn"))
        s_slot = [(g.rows_landed[1][h], t.sem(f"free{h}")) for h in range(2)]
        s_claim, s_kept = t.sem("claim"), t.sem("kept")
        ids_b = t.sb("ids_b", [P, P])
        oh = t.sb("oh", [P, 2, J, P])
        zero = t.sb("zero", [1, 512], F16)
        if harmonics is not None:
            prod = t.sb("prod", [P, 2, J, H9, D])
            sh = t.sb("sh", [P, EC, H9])
            slots = t.sb("slots", [P, 2, GC, D])
        acc = t.ps("acc", [P, 512])
        with nc.Block() as block:
            if harmonics is not None:
                @block.sync
                def _(e):
                    e.dma_start(sh[:, :, :], harmonics).then_inc(s_load, 16)

                @block.gpsimd
                def _(e):
                    node_gather(e, t, g, table, D, slots, G, s_slot, s_claim, s_kept)

            @block.vector
            def _(e):
                e.memset(zero[:, :], 0.0).then_inc(s_z, 1)
                if harmonics is not None:
                    e.wait_ge(s_load, 16)
                v = Count(e, f"{t.stage}_v", VISITS)
                with e.Fori(0, NB, 1) as b:
                    lo, hi = pair_range(e, g, b)
                    e.tensor_scalar(ids_b[:, :], g.iota[:, :], g.block_first[:, ds(b, 1)], None, ALU.add).then_inc(s_ib, 1)
                    e.wait_ge(s_ib, b + 1)
                    e.sem_inc(s_turn, 1)
                    with e.Fori(lo, hi, 1) as u:
                        n = v.now()
                        for s in range(2):
                            e.wait_ge(s_used[s], n + 1)
                            for j in range(J):
                                m = e.tensor_scalar(oh[:, s, j, :], ids_b[:, :], g.dst_f[:, ds((u * 2 + s) * J + j, 1)], None,
                                                    ALU.is_equal)
                                if harmonics is None and j == J - 1:
                                    m.then_inc(s_oh[s], 1)
                            if harmonics is not None:
                                if s == 0:
                                    e.wait_ge(s_kept, u * 2 + 2)
                                c0 = (u * 2 + s) * J
                                e.tensor_tensor(prod[:, s, :, :, :],
                                                bcast(G[:, ds(c0, J), :].unsqueeze(2), [P, J, H9, D]),
                                                bcast(sh[:, ds(c0, J), :].unsqueeze(3), [P, J, H9, D]),
                                                ALU.mult).then_inc(s_oh[s], 1)
                        v.up()
                    e.wait_ge(s_oh[1], v.now())
                    e.sem_inc(s_turn, 1)

            @block.tensor
            def _(e):
                e.wait_ge(s_z, 1)
                e.sem_inc(s_used[0], 1)
                e.sem_inc(s_used[1], 1)
                v = Count(e, f"{t.stage}_pe", VISITS)
                with e.Fori(0, NB, 1) as b:
                    lo, hi = pair_range(e, g, b)
                    e.wait_ge(s_ev, b + 1)
                    e.matmul(acc[:, 0:width], zero[0:1, 0:P], zero[0:1, 0:width], start=True, stop=False, skip_group_check=True)
                    with e.Fori(lo, hi, 1) as u:
                        n = v.now()
                        for s in range(2):
                            e.wait_ge(s_oh[s], n + 1)
                            for j in range(J):
                                if harmonics is not None:
                                    rows = prod[:, s, j, :, :].rearrange("p c f -> p (c f)")
                                else:
                                    rows = G[:, ds((u * 2 + s) * J + j, 1), :].rearrange("p a f -> p (a f)")
                                m = e.matmul(acc[:, 0:width], oh[:, s, j, :], rows, start=False, stop=False, skip_group_check=True)
                            m.then_inc(s_used[s], 1)
                        v.up()
                    e.matmul(acc[:, 0:1], zero[0:1, 0:P], zero[0:1, 0:1], start=False, stop=True,
                             skip_group_check=True).then_inc(s_sum, 1)

            @block.scalar
            def _(e):
                e.sem_inc(s_ev, 1)
                with e.Fori(0, NB, 1) as b:
                    e.wait_ge(s_sum, b + 1)
                    e.activation(sums[:, ds(b, 1), :].rearrange("p a f -> p (a f)"), acc[:, 0:width], ACT.Copy).then_inc(s_ev, 1)


def next_layer(nc, g, a, stage, table, sums=None, mixed=None):
    with stage_tools(nc, stage) as t:
        s_v, s_a, s_out = t.sem("vector"), t.sem("scalar"), t.sem("stored")
        m, v, sq = t.sb("mean", [P, NB]), t.sb("var", [P, NB]), t.sb("sq", [P, NB, D])
        den, mix = t.sb("den", [P, NB]), t.sb("mix", [P, NB, D])
        with nc.Block() as block:
            root = [0, 0]

            @block.vector
            def _(e):
                c = Chain(e, s_v)
                if sums is not None:
                    c(e.tensor_scalar(den[:, :], sums[:, :, D], 1e-8, None, ALU.add))
                    c(e.reciprocal(den[:, :], den[:, :]))
                    c(e.tensor_tensor(mix[:, :, :], sums[:, :, 0:D], bcast(den[:, :].unsqueeze(2), [P, NB, D]), ALU.mult))
                    c(e.tensor_tensor(g.x[:, :, :], g.x[:, :, :], mix[:, :, :], ALU.add))
                if mixed is not None:
                    c(e.tensor_tensor(g.x[:, :, :], g.x[:, :, :], mixed[:, :, :], ALU.add))
                root[0] = c.n + 6
                layernorm_relu(e, c, lambda: e.wait_ge(s_a, 1), (m, v, sq[:, :, :]), g.x[:, :, :], g.h[:, :, :], None)
                root[1] = c.n

            @block.scalar
            def _(e):
                e.wait_ge(s_v, root[0])
                e.activation(v[:, :], v[:, :], ACT.Sqrt).then_inc(s_a, 1)

            @block.sync
            def _(e):
                if table is not None:
                    e.wait_ge(s_v, root[1])
                    e.dma_start(table.rearrange("(b p) f -> p b f", p=P), g.h[:, :, :]).then_inc(s_out, 16)
                    e.wait_ge(s_out, 16)


def mix_products(nc, g, a, sums, mixed):
    with stage_tools(nc, "mix") as t:
        s_load, s_w, s_pe, s_a, s_out, s_v = (t.sem(n) for n in ("loaded", "weights", "turned", "copied", "mixed", "kept"))
        wrep, cg = t.sb("wrep", [BW, 3, D]), t.sb("cg", [BW, 3, D])
        turned = t.sb("turned", [BW, 2, 3, P])
        pt = [t.ps(f"pt{i}", [BW, 3 * P]) for i in range(2)]
        po = [t.ps(f"po{i}", [P, D]) for i in range(2)]
        with nc.Block() as block:
            @block.sync
            def _(e):
                e.dma_start(wrep[:, :, :], a["W1_rep"].rearrange("(q r) o -> r q o", r=BW)).then_inc(s_load, 16)
                e.dma_start(cg[:, :, :], a["cg"].rearrange("(q r) o -> r q o", r=BW)).then_inc(s_load, 16)

            @block.vector
            def _(e):
                e.wait_ge(s_load, 32)
                e.tensor_tensor(wrep[:, :, :], wrep[:, :, :], cg[:, :, :], ALU.mult).then_inc(s_w, 1)
                for b in range(NB):
                    e.wait_ge(s_out, b + 1)
                    e.tensor_copy(mixed[:, b, :], po[b % 2][:, :]).then_inc(s_v, 1)

            @block.scalar
            def _(e):
                for b in range(NB):
                    e.wait_ge(s_pe, b + 1)
                    if b >= 2:
                        e.wait_ge(s_out, b - 1)
                    e.activation(turned[:, b % 2, :, :].rearrange("p q n -> p (q n)"), pt[b % 2][:, :], ACT.Copy).then_inc(s_a, 1)

            @block.tensor
            def _(e):
                e.wait_ge(s_w, 1)

                def mix(b):
                    e.wait_ge(s_a, b + 1)
                    if b >= 2:
                        e.wait_ge(s_v, b - 1)
                    for q in range(3):
                        m = e.matmul(po[b % 2][:, :], turned[:, b % 2, q, :], wrep[:, q, :], start=(q == 0), stop=(q == 2))
                    m.then_inc(s_out, 1)
                for b in range(NB):
                    if b >= 2:
                        e.wait_ge(s_a, b - 1)
                    for q in range(3):
                        m = e.transpose(pt[b % 2][:, q * P:(q + 1) * P], sums[:, b, q * BW:(q + 1) * BW], g.ident[:, :])
                    m.then_inc(s_pe, 1)
                    if b:
                        mix(b - 1)
                mix(NB - 1)


HID = 64
LOW = 4096.0
DC = [min(512, N - c) for c in range(0, N, 512)]
TAIL = N - (NB - 1) * P


def turn_counts(nc, g, dr, CT):
    SG = [(s, min(8, NB - s)) for s in range(0, NB, 8)]
    with stage_tools(nc, "turn") as t:
        s_ld = [t.sem(f"loaded{i}") for i in range(2)]
        s_t, s_ea, s_ev, s_one, s_deg, s_id = (t.sem(n) for n in ("turned", "copied_a", "copied_v", "ones", "degree", "diagonal"))
        row = t.sb("row", [P, 2, NP], F16)
        one = t.sb("one", [P, 1], F16)
        pt = [t.ps(f"pt{i}", [P, 8, P], F16) for i in range(4)]
        pd = t.ps("pd", [P, NB])
        zero = t.sb("zero", [1, P], F16)
        with nc.Block() as block:
            @block.sync
            def _(e):
                for b in range(NB):
                    if b >= 2:
                        e.wait_ge(s_t, 4 * (b - 1))
                    e.dma_start(row[:, b % 2, :], dr["counts"][b * P:(b + 1) * P, :]).then_inc(s_ld[b % 2], 16)

            @block.tensor
            def _(e):
                e.wait_ge(s_one, 2)
                e.matmul(pd[:, :], zero[0:1, :], zero[0:1, 0:NB], start=True, stop=False, skip_group_check=True)
                for b in range(NB):
                    e.wait_ge(s_ld[b % 2], 16 * (b // 2 + 1))
                    for k, (s0, n) in enumerate(SG):
                        if b:
                            e.wait_ge(s_ea if k % 2 else s_ev, 2 * b if k >= 2 else 2 * b - 1)
                        for s in range(s0, s0 + n):
                            e.matmul(pd[:, s:s + 1], row[:, b % 2, s * P:(s + 1) * P], one[:, :], start=False,
                                     stop=(b == NB - 1), skip_group_check=True)
                        for s in range(s0, s0 + n):
                            m = e.transpose(pt[k][:, s - s0, :], row[:, b % 2, s * P:(s + 1) * P], g.ident16[:, :])
                        m.then_inc(s_t, 1)

            @block.vector
            def _(e):
                e.memset(zero[:, :], 0.0).then_inc(s_one, 1)
                e.memset(one[:, :], 1.0).then_inc(s_one, 1)
                for b in range(NB):
                    w = min(P, N - b * P)
                    for k in (0, 2):
                        s0, n = SG[k]
                        e.wait_ge(s_t, 4 * b + k + 1)
                        e.tensor_copy(CT[:, s0:s0 + n, b * P:b * P + w], pt[k][:, 0:n, 0:w]).then_inc(s_ev, 1)
                e.wait_ge(s_ev, 2 * NB)
                e.wait_ge(s_ea, 2 * NB)
                for s in range(NB):
                    w = min(P, N - s * P)
                    d = CT[:, s, s * P:s * P + w]
                    e.tensor_tensor(d, d, g.ident16[:, 0:w], ALU.add).then_inc(s_id, 1)
                e.tensor_copy(g.deg_out[:, :], pd[:, :]).then_inc(s_id, 1)
                e.tensor_scalar(g.dis[:, :], g.deg[:, :], 1.0, None, ALU.add).then_inc(s_deg, 1)
                e.wait_ge(s_deg, 2)
                e.reciprocal(g.dis[:, :], g.dis[:, :]).then_inc(s_deg, 1)
                e.wait_ge(s_id, NB + 1)

            @block.scalar
            def _(e):
                for b in range(NB):
                    w = min(P, N - b * P)
                    for k in (1, 3):
                        s0, n = SG[k]
                        e.wait_ge(s_t, 4 * b + k + 1)
                        e.activation(CT[:, s0:s0 + n, b * P:b * P + w], pt[k][:, 0:n, 0:w], ACT.Copy).then_inc(s_ea, 1)
                e.wait_ge(s_deg, 1)
                e.activation(g.dis[:, :], g.dis[:, :], ACT.Sqrt).then_inc(s_deg, 1)


def gcn(nc, g, stage, CT, z, fin, weights, outs):
    fo = sum(w.shape[1] for w in weights)
    with stage_tools(nc, stage) as t:
        s_v, s_a, s_w, s_agg, s_ev, s_y, s_yv, s_b = (t.sem(n) for n in (
            "vector", "scalar", "weights", "aggregated", "copied", "mixed", "used", "bias"))
        zs = t.sb("zs", [P, NB, fin])
        parts = t.sb("parts", [P, NB, 2 * fin], F16)
        W = t.sb("W", [2 * fin, fo])
        bias = t.sb("bias", [P, fo])
        agg = t.sb("agg", [2 * fin, 2, 512])
        pa = [t.ps(f"pa{i}", [2 * fin, 512]) for i in range(2)]
        py = [t.ps(f"py{i}", [P, 4, fo]) for i in range(2)]
        yv = t.sb("yv", [P, 2, 4, fo])
        nload = 3 * len(weights)
        with nc.Block() as block:
            @block.sync
            def _(e):
                c = 0
                for w, (b, _, _) in zip(weights, outs):
                    n = w.shape[1]
                    e.dma_start(W[0:fin, c:c + n], w).then_inc(s_w, 16)
                    e.dma_start(W[fin:2 * fin, c:c + n], w).then_inc(s_w, 16)
                    e.dma_start(bias[:, c:c + n], b.unsqueeze(0).partition_broadcast(P)).then_inc(s_w, 16)
                    c += n

            @block.vector
            def _(e):
                c = Chain(e, s_v)
                c(e.tensor_tensor(zs[:, :, :], z, bcast(g.dis[:, :].unsqueeze(2), [P, NB, fin]), ALU.mult))
                e.wait_ge(s_a, 1)
                c(e.tensor_tensor(zs[:, :, :], zs[:, :, :], parts[:, :, 0:fin], ALU.subtract))
                e.wait_ge(s_w, 16 * nload)
                c(e.tensor_scalar(W[fin:2 * fin, :], W[fin:2 * fin, :], 1.0 / LOW, None, ALU.mult))
                for _, h, add in outs:
                    if not add:
                        c(e.memset(h[:, NB - 1, :], 0.0))
                for k, n in enumerate(DC):
                    rows, nb = (P, n // P) if n >= P else (n, 1)
                    e.wait_ge(s_y, k + 1)
                    y = yv[0:rows, k % 2, 0:nb, :]
                    e.tensor_tensor(y, py[k % 2][0:rows, 0:nb, :],
                                    bcast(g.dis[0:rows, 4 * k:4 * k + nb].unsqueeze(2), [rows, nb, fo]), ALU.mult).then_inc(s_yv, 1)
                    e.wait_ge(s_yv, k + 1)
                    o = 0
                    for _, h, add in outs:
                        w = h.shape[2]
                        d = h[0:rows, 4 * k:4 * k + nb, :]
                        if add:
                            c(e.tensor_tensor(d, d, yv[0:rows, k % 2, 0:nb, o:o + w], ALU.add))
                            c(e.tensor_tensor(d, d, bcast(bias[0:rows, o:o + w].unsqueeze(1), [rows, nb, w]), ALU.add))
                        else:
                            c(e.tensor_tensor(d, yv[0:rows, k % 2, 0:nb, o:o + w],
                                              bcast(bias[0:rows, o:o + w].unsqueeze(1), [rows, nb, w]), ALU.add))
                        o += w

            @block.scalar
            def _(e):
                e.wait_ge(s_v, 1)
                e.activation(parts[:, :, 0:fin], zs[:, :, :], ACT.Copy).then_inc(s_a, 1)
                e.wait_ge(s_v, 2)
                e.activation(parts[:, :, fin:], zs[:, :, :], ACT.Copy, scale=LOW).then_inc(s_a, 1)
                for k, n in enumerate(DC):
                    e.wait_ge(s_agg, k + 1)
                    if k >= 2:
                        e.wait_ge(s_y, k - 1)
                    e.activation(agg[:, k % 2, 0:n], pa[k % 2][:, 0:n], ACT.Copy).then_inc(s_ev, 1)

            @block.tensor
            def _(e):
                e.wait_ge(s_a, 2)
                e.wait_ge(s_v, 3)

                def mix(k):
                    n = DC[k]
                    rows, nb = (P, n // P) if n >= P else (n, 1)
                    e.wait_ge(s_ev, k + 1)
                    if k >= 2:
                        e.wait_ge(s_yv, k - 1)
                    for i in range(nb):
                        m = e.matmul(py[k % 2][0:rows, i, :], agg[:, k % 2, i * P:i * P + rows], W[:, :], start=True, stop=True)
                    m.then_inc(s_y, 1)
                for k, n in enumerate(DC):
                    if k >= 2:
                        e.wait_ge(s_ev, k - 1)
                    for s in range(NB):
                        m = e.matmul(pa[k % 2][:, 0:n], parts[:, s, :], CT[:, s, 512 * k:512 * k + n],
                                     start=(s == 0), stop=(s == NB - 1))
                    m.then_inc(s_agg, 1)
                    if k:
                        mix(k - 1)
                mix(len(DC) - 1)


def batchnorm(nc, g, stage, h, w, gamma, beta, into, add):
    with stage_tools(nc, stage) as t:
        s_v, s_a, s_pe, s_ld = t.sem("vector"), t.sem("scalar"), t.sem("tensor"), t.sem("loaded")
        part, part2 = t.sb("part", [P, w]), t.sb("part2", [P, w])
        mean, var = t.sb("mean", [P, w]), t.sb("var", [P, w])
        ga, be = t.sb("gamma", [P, w]), t.sb("beta", [P, w])
        sq = t.sb("sq", [P, NB, w])
        pm, pv = t.ps("pm", [P, w]), t.ps("pv", [P, w])
        with nc.Block() as block:
            @block.sync
            def _(e):
                e.dma_start(ga[:, :], gamma.unsqueeze(0).partition_broadcast(P)).then_inc(s_ld, 16)
                e.dma_start(be[:, :], beta.unsqueeze(0).partition_broadcast(P)).then_inc(s_ld, 16)

            @block.vector
            def _(e):
                c = Chain(e, s_v)
                full = lambda v: bcast(v[:, :].unsqueeze(1), [P, NB, w])
                c(e.tensor_reduce(part[:, :], h.rearrange("p b f -> p f b"), X, ALU.add))
                e.wait_ge(s_pe, 1)
                c(e.tensor_scalar(mean[:, :], pm[:, :], 1.0 / N, None, ALU.mult))
                c(e.tensor_tensor(h, h, full(mean), ALU.subtract))
                c(e.tensor_tensor(sq[:, :, :], h, h, ALU.mult))
                c(e.tensor_reduce(part2[:, :], sq[:, 0:NB - 1, :].rearrange("p b f -> p f b"), X, ALU.add))
                e.wait_ge(s_pe, 2)
                c(e.tensor_scalar(var[:, :], pv[:, :], 1.0 / N, EPS, ALU.mult, ALU.add))
                e.wait_ge(s_a, 1)
                e.wait_ge(s_ld, 32)
                c(e.reciprocal(var[:, :], var[:, :]))
                c(e.tensor_tensor(var[:, :], var[:, :], ga[:, :], ALU.mult))
                c(e.tensor_tensor(h, h, full(var), ALU.mult))
                c(e.tensor_tensor(h, h, full(be), ALU.add))
                c(e.scalar_tensor_tensor(into, h, 0.0, add, ALU.max, ALU.add))

            @block.scalar
            def _(e):
                e.wait_ge(s_v, 6)
                e.activation(var[:, :], var[:, :], ACT.Sqrt).then_inc(s_a, 1)

            @block.tensor
            def _(e):
                e.wait_ge(s_v, 1)
                e.matmul(pm[:, :], g.ones[:, :], part[:, :], start=True, stop=True).then_inc(s_pe, 1)
                e.wait_ge(s_v, 5)
                e.matmul(pv[:, :], g.ones[:, :], part2[:, :], start=True, stop=False)
                e.matmul(pv[:, :], g.ones[0:TAIL, :], sq[0:TAIL, NB - 1, :], start=False, stop=True).then_inc(s_pe, 1)


def linear(nc, g, stage, z, fin, w, b, res):
    fo = w.shape[1]
    with stage_tools(nc, stage) as t:
        s_ld, s_t, s_a, s_y, s_v = (t.sem(n) for n in ("loaded", "turned", "copied", "mixed", "vector"))
        W, bias = t.sb("W", [fin, fo]), t.sb("bias", [P, fo])
        zt = t.sb("zt", [fin, 2, P])
        pt = [t.ps(f"pt{i}", [fin, P]) for i in range(2)]
        py = [t.ps(f"py{i}", [P, fo]) for i in range(2)]
        with nc.Block() as block:
            @block.sync
            def _(e):
                e.dma_start(W[:, :], w).then_inc(s_ld, 16)
                e.dma_start(bias[:, :], b.unsqueeze(0).partition_broadcast(P)).then_inc(s_ld, 16)

            @block.tensor
            def _(e):
                e.wait_ge(s_ld, 32)

                def mix(k):
                    e.wait_ge(s_a, k + 1)
                    if k >= 2:
                        e.wait_ge(s_v, k - 1)
                    e.matmul(py[k % 2][:, :], zt[:, k % 2, :], W[:, :], start=True, stop=True).then_inc(s_y, 1)
                for k in range(NB):
                    if k >= 2:
                        e.wait_ge(s_a, k - 1)
                    e.transpose(pt[k % 2][:, :], z[:, k, :], g.ident[:, :]).then_inc(s_t, 1)
                    if k:
                        mix(k - 1)
                mix(NB - 1)

            @block.scalar
            def _(e):
                for k in range(NB):
                    e.wait_ge(s_t, k + 1)
                    if k >= 2:
                        e.wait_ge(s_y, k - 1)
                    e.activation(zt[:, k % 2, :], pt[k % 2][:, :], ACT.Copy).then_inc(s_a, 1)

            @block.vector
            def _(e):
                e.wait_ge(s_ld, 32)
                for k in range(NB):
                    e.wait_ge(s_y, k + 1)
                    e.tensor_tensor(res[:, k, :], py[k % 2][:, :], bias[:, :], ALU.add).then_inc(s_v, 1)


def residual_gcn(nc, g, a, dr):
    with stage_tools(nc, "l2") as t:
        CT = t.sb("CT", [P, NB, N], F16)
        turn_counts(nc, g, dr, CT)
        A, B, M = t.sb("A", [P, NB, HID]), t.sb("B", [P, NB, HID]), t.sb("M", [P, NB, HID])
        Av, Bv, Mv = A[:, :, :], B[:, :, :], M[:, :, :]
        W, gm, bt = a["W_hid"], a["gamma_hid"], a["beta_hid"]
        bh = a["b_hid"]
        h = g.h[:, :, :]
        linear(nc, g, "enc1_res", h, D, a["Wres_enc1"], a["bres_enc1"], Bv)
        gcn(nc, g, "enc1", CT, h, D, [a["W_enc1"]], [(a["b_enc1"], Av, False)])
        batchnorm(nc, g, "enc1_bn", Av, HID, gm[0], bt[0], Bv, Bv)
        gcn(nc, g, "enc2", CT, Bv, HID, [W[0], W[2]], [(bh[0], Av, False), (bh[2], Mv, False)])
        batchnorm(nc, g, "enc2_bn", Av, HID, gm[1], bt[1], Bv, Bv)
        gcn(nc, g, "enc3", CT, Bv, HID, [W[1], W[3]], [(bh[1], Av, False), (bh[3], Mv, True)])
        batchnorm(nc, g, "enc3_bn", Av, HID, gm[2], bt[2], Bv, Bv)
        gcn(nc, g, "mid", CT, Bv, HID, [W[4]], [(bh[4], Mv, True)])
        gcn(nc, g, "dec1", CT, Mv, HID, [W[5]], [(bh[5], Av, False)])
        batchnorm(nc, g, "dec1_bn", Av, HID, gm[3], bt[3], Mv, Mv)
        linear(nc, g, "dec2_res", Mv, HID, a["Wres_dec2"], a["bres_dec2"], B[:, :, 0:D])
        gcn(nc, g, "dec2", CT, Mv, HID, [a["W_dec2"]], [(a["b_dec2"], A[:, :, 0:D], False)])
        batchnorm(nc, g, "dec2_bn", A[:, :, 0:D], D, a["gamma_out"][0], a["beta_out"][0], B[:, :, 0:D], B[:, :, 0:D])
        gcn(nc, g, "dec3", CT, B[:, :, 0:D], D, [a["W_dec3"]], [(a["b_dec3"], A[:, :, 0:D], False)])
        batchnorm(nc, g, "dec3_bn", A[:, :, 0:D], D, a["gamma_out"][1], a["beta_out"][1], A[:, :, HID - D:], B[:, :, 0:D])
        next_layer(nc, g, a, "layer3", dr["table1"], mixed=A[:, :, HID - D:])


ED = 16
GROUPS = [(b, min(NB, b + 10)) for b in range(0, NB, 10)]
KIN = D + ED
FH = 2 * HID


def edge_flows(nc, g, a, dr, G, PD, sums):
    with stage_tools(nc, "flow") as t:
        two = lambda n: [t.sem(f"{n}{i}") for i in range(2)]
        s_oh, s_gs, s_t, s_x, s_ot, s_e, s_hid, s_used, s_ea, s_free, s_hl, s_st, s_stf = (two(n) for n in (
            "onehot", "rows", "turned", "inputs", "onehot_turned", "edges", "hidden", "used", "attrs", "free",
            "parts", "stored", "place"))
        s_ib, s_z, s_sum, s_ev, s_ld, s_turn, s_m = (t.sem(n) for n in (
            "block_ids", "zeros", "summed", "copied", "weights", "turn", "steps"))
        s_slot = [(g.rows_landed[2][h], t.sem(f"slot_free{h}")) for h in range(2)]
        s_claim, s_kept = t.sem("claim"), t.sem("kept")
        slots = t.sb("slots", [P, 2, GC, D])
        ids_b, zero = t.sb("ids_b", [P, P]), t.sb("zero", [1, 512], F16)
        W = t.sb("W", [KIN, FH])
        oh, oht = t.sb("oh", [P, 2, J, P]), t.sb("oht", [P, 2, J, P])
        gs, xin = t.sb("gs", [P, 2, J, D]), t.sb("xin", [KIN, 2, J, P])
        hid, hl = t.sb("hid", [P, 2, J, FH]), t.sb("hl", [P, 2, J, FH], F16)
        m1, mask = t.sb("m1", [P, 2, J]), t.sb("mask", [P, 2, J])
        bm = t.sb("bm", [P, 2, J, HID])
        pt, po, ph = ([t.ps(f"{n}{i}", sh) for i in range(2)] for n, sh in (
            ("pt", [D, J, P]), ("po", [P, J, P]), ("ph", [P, J, FH])))
        acc = t.ps("acc", [P, 512])
        with nc.Block() as block:
            @block.gpsimd
            def _(e):
                node_gather(e, t, g, dr["table1"][:, :], D, slots, G, s_slot, s_claim, s_kept)

            @block.sync
            def _(e):
                e.dma_start(W[:, :], a["Wf1_src"]).then_inc(s_ld, 16)
                e.sem_inc(s_stf[0], 1)
                e.sem_inc(s_stf[1], 1)
                v = Count(e, "flow_sync", VISITS)
                for hidden, (b0, b1) in zip(dr["hidden"], GROUPS):
                    place = Count(e, f"flow_place{b0}", (b1 - b0) * (T // 2) - 1)
                    with e.Fori(b0, b1, 1) as b:
                        lo, hi = pair_range(e, g, b)
                        with e.Fori(lo, hi, 1) as u:
                            n, k = v.now(), place.now()
                            for s in range(2):
                                e.wait_ge(s_free[s], n + 1)
                                e.dma_start(xin[D:KIN, s, :, :], a["edge_attr_16"][ds(u * 2 + s, 1), :, :, :]
                                            .rearrange("a k j p -> (a k) j p")).then_inc(s_ea[s], 16)
                            for s in range(2):
                                e.wait_ge(s_hl[s], n + 1)
                                e.dma_start(hidden[ds(k * 2 + s, 1), :, :].rearrange("a p n -> (a p) n"),
                                            hl[:, s, :, :].rearrange("p j f -> p (j f)")).then_inc(s_st[s], 16)
                            for s in range(2):
                                e.wait_ge(s_st[s], 16 * n + 16)
                                e.sem_inc(s_stf[s], 1)
                            v.up()
                            place.up()

            @block.vector
            def _(e):
                e.memset(zero[:, :], 0.0).then_inc(s_z, 1)
                v = Count(e, "flow_v", VISITS)
                with e.Fori(0, NB, 1) as b:
                    lo, hi = pair_range(e, g, b)
                    e.tensor_scalar(ids_b[:, :], g.iota[:, :], g.block_first[:, ds(b, 1)], None, ALU.add).then_inc(s_ib, 1)
                    e.wait_ge(s_ib, b + 1)
                    e.sem_inc(s_turn, 1)
                    with e.Fori(lo, hi, 1) as u:
                        n = v.now()
                        for s in range(2):
                            c0 = (u * 2 + s) * J
                            e.wait_ge(s_used[s], n + 1)
                            for j in range(J):
                                m = e.tensor_scalar(oh[:, s, j, :], ids_b[:, :], g.dst_f[:, ds(c0 + j, 1)], None, ALU.is_equal)
                            m.then_inc(s_oh[s], 1)
                            if s == 0:
                                e.wait_ge(s_kept, u * 2 + 2)
                            e.tensor_copy(gs[:, s, :, :], G[:, ds(c0, J), :]).then_inc(s_gs[s], 1)
                            e.tensor_scalar(m1[:, s, :], g.dst_f[:, ds(c0, J)], g.block_first[:, ds(b, 1)], None,
                                            ALU.is_ge).then_inc(s_m, 1)
                            e.wait_ge(s_m, n * 10 + 2 * s + 1)
                            e.scalar_tensor_tensor(mask[:, s, :], g.dst_f[:, ds(c0, J)], g.block_first[:, ds(b + 1, 1)],
                                                   m1[:, s, :], ALU.is_lt, ALU.mult).then_inc(s_m, 1)
                        for s in range(2):
                            e.wait_ge(s_hid[s], n + 1)
                            e.wait_ge(s_m, n * 10 + 4)
                            e.tensor_tensor(bm[:, s, :, :], hid[:, s, :, HID:], bcast(mask[:, s, :].unsqueeze(2), [P, J, HID]),
                                            ALU.mult).then_inc(s_m, 1)
                            e.wait_ge(s_m, n * 10 + 3 * s + 5)
                            e.wait_ge(s_stf[s], n + 1)
                            e.tensor_copy(hl[:, s, :, 0:HID], bm[:, s, :, :]).then_inc(s_m, 1)
                            e.wait_ge(s_m, n * 10 + 3 * s + 6)
                            e.tensor_tensor(bm[:, s, :, :], bm[:, s, :, :], hl[:, s, :, 0:HID], ALU.subtract).then_inc(s_m, 1)
                            e.wait_ge(s_m, n * 10 + 3 * s + 7)
                            e.tensor_scalar(hl[:, s, :, HID:], bm[:, s, :, :], LOW, None, ALU.mult).then_inc(s_hl[s], 1)
                        v.up()
                    e.wait_ge(s_hl[1], v.now())
                    e.sem_inc(s_turn, 1)

            @block.scalar
            def _(e):
                v = Count(e, "flow_a", VISITS)
                e.sem_inc(s_ev, 1)
                with e.Fori(0, NB, 1) as b:
                    lo, hi = pair_range(e, g, b)
                    with e.Fori(lo, hi, 1) as u:
                        n = v.now()
                        for s in range(2):
                            e.wait_ge(s_t[s], n + 1)
                            e.activation(xin[0:D, s, :, :], pt[s][:, :, :], ACT.Copy).then_inc(s_x[s], 1)
                            e.activation(oht[:, s, :, :], po[s][:, :, :], ACT.Copy).then_inc(s_ot[s], 1)
                        for s in range(2):
                            e.wait_ge(s_e[s], n + 1)
                            e.activation(hid[:, s, :, :], ph[s][:, :, :], ACT.Relu).then_inc(s_hid[s], 1)
                        v.up()
                    e.wait_ge(s_sum, b + 1)
                    e.activation(sums[:, ds(b, 1), :].rearrange("p a f -> p (a f)"), acc[:, 0:HID], ACT.Copy).then_inc(s_ev, 1)

            @block.tensor
            def _(e):
                e.wait_ge(s_z, 1)
                e.wait_ge(s_ld, 16)
                for s in range(2):
                    e.sem_inc(s_used[s], 1)
                    e.sem_inc(s_free[s], 1)
                v = Count(e, "flow_pe", VISITS)
                with e.Fori(0, NB, 1) as b:
                    lo, hi = pair_range(e, g, b)
                    e.wait_ge(s_ev, b + 1)
                    e.matmul(acc[:, 0:HID], zero[0:1, 0:P], zero[0:1, 0:HID], start=True, stop=False, skip_group_check=True)
                    with e.Fori(lo, hi, 1) as u:
                        n = v.now()
                        for s in range(2):
                            e.wait_ge(s_oh[s], n + 1)
                            for j in range(J):
                                e.transpose(po[s][:, j, :], oh[:, s, j, :], g.ident[:, :])
                            e.wait_ge(s_gs[s], n + 1)
                            for j in range(J):
                                m = e.transpose(pt[s][:, j, :], gs[:, s, j, :], g.ident[:, :])
                            m.then_inc(s_t[s], 1)
                        for s in range(2):
                            e.wait_ge(s_x[s], n + 1)
                            e.wait_ge(s_ea[s], 16 * n + 16)
                            e.wait_ge(s_ot[s], n + 1)
                            for j in range(J):
                                e.matmul(ph[s][:, j, :], xin[:, s, j, :], W[:, :], start=True, stop=False)
                                m = e.matmul(ph[s][:, j, :], oht[:, s, j, :], PD[:, ds(b, 1), :].rearrange("p a f -> p (a f)"),
                                             start=False, stop=True)
                            m.then_inc(s_e[s], 1)
                        for s in range(2):
                            e.wait_ge(s_hid[s], n + 1)
                            for j in range(J):
                                m = e.matmul(acc[:, 0:HID], oh[:, s, j, :], hid[:, s, j, 0:HID], start=False, stop=False,
                                             skip_group_check=True)
                            m.then_inc(s_used[s], 1)
                            e.wait_ge(s_used[s], n + 2)
                            e.sem_inc(s_free[s], 1)
                        v.up()
                    e.matmul(acc[:, 0:1], zero[0:1, 0:P], zero[0:1, 0:1], start=False, stop=True,
                             skip_group_check=True).then_inc(s_sum, 1)


def backward_sums(nc, g, a, dr, back):
    with stage_tools(nc, "back") as t:
        s_ld = [t.sem(f"loaded{i}") for i in range(2)]
        s_free = [t.sem(f"free{i}") for i in range(2)]
        s_oh, s_used, s_z, s_sum, s_ev, s_ids = (t.sem(n) for n in ("onehot", "used", "zeros", "summed", "copied", "ids"))
        hl = t.sb("hl", [P, 2, J * FH], F16)
        ohs = t.sb("ohs", [P, J, NP], F16)
        ids = t.sb("ids", [P, NP])
        ids16 = t.sb("ids16", [P, NP], F16)
        zero = t.sb("zero", [1, 512], F16)
        acc = t.ps("acc", [P, CB, 512])
        with nc.Block() as block:
            @block.gpsimd
            def _(e):
                e.iota(ids[:, :], [[1, NP]], base=-HALF, channel_multiplier=0,
                       allow_small_or_imprecise_dtypes=True).then_inc(s_ids, 1)

            @block.sync
            def _(e):
                v = Count(e, "back_sync", VISITS)
                for hidden, (b0, b1) in zip(dr["hidden"], GROUPS):
                    place = Count(e, f"back_place{b0}", (b1 - b0) * (T // 2) - 1)
                    with e.Fori(b0, b1, 1) as b:
                        lo, hi = pair_range(e, g, b)
                        with e.Fori(lo, hi, 1) as u:
                            n, k = v.now(), place.now()
                            for s in range(2):
                                e.wait_ge(s_free[s], n + 1)
                                e.dma_start(hl[:, s, :], hidden[ds(k * 2 + s, 1), :, :].rearrange("a p n -> (a p) n")).then_inc(s_ld[s], 16)
                            v.up()
                            place.up()

            @block.vector
            def _(e):
                e.memset(zero[:, :], 0.0).then_inc(s_z, 1)
                e.wait_ge(s_ids, 1)
                e.tensor_copy(ids16[:, :], ids[:, :]).then_inc(s_ids, 1)
                e.wait_ge(s_ids, 2)
                v = Count(e, "back_v", VISITS)
                with e.Fori(0, NB, 1) as b:
                    lo, hi = pair_range(e, g, b)
                    with e.Fori(lo, hi, 1) as u:
                        n = v.now()
                        for s in range(2):
                            for j in range(J):
                                e.wait_ge(s_used, n * (2 * J) + s * J + j + 1)
                                e.tensor_scalar(ohs[:, j, :], ids16[:, :], g.src_f[:, ds((u * 2 + s) * J + j, 1)], None,
                                                ALU.is_equal).then_inc(s_oh, 1)
                        v.up()
                e.memset(back[:, N:NP], 0.0).then_inc(s_z, 1)

            @block.tensor
            def _(e):
                e.wait_ge(s_z, 1)
                for s in range(2):
                    e.sem_inc(s_free[s], 1)
                e.sem_inc(s_used, J)
                for k, w in enumerate(DC):
                    e.matmul(acc[:, k, 0:w], zero[0:1, 0:P], zero[0:1, 0:w], start=True, stop=False, skip_group_check=True)
                v = Count(e, "back_pe", VISITS)
                with e.Fori(0, NB, 1) as b:
                    lo, hi = pair_range(e, g, b)
                    with e.Fori(lo, hi, 1) as u:
                        n = v.now()
                        for s in range(2):
                            e.wait_ge(s_ld[s], 16 * n + 16)
                            for j in range(J):
                                e.wait_ge(s_oh, n * (2 * J) + s * J + j + 1)
                                for k, w in enumerate(DC):
                                    m = e.matmul(acc[:, k, 0:w], hl[:, s, j * FH:(j + 1) * FH], ohs[:, j, 512 * k:512 * k + w],
                                                 start=False, stop=False, skip_group_check=True)
                                m.then_inc(s_used, 1)
                            e.wait_ge(s_used, n * (2 * J) + s * J + 2 * J)
                            e.sem_inc(s_free[s], 1)
                        v.up()
                e.matmul(acc[:, CB - 1, 0:1], zero[0:1, 0:P], zero[0:1, 0:1], start=False, stop=True,
                         skip_group_check=True).then_inc(s_sum, 1)

            @block.scalar
            def _(e):
                e.wait_ge(s_sum, 1)
                for k, w in enumerate(DC):
                    e.activation(back[:, 512 * k:512 * k + w], acc[:, k, 0:w], ACT.Copy).then_inc(s_ev, 1)
                e.wait_ge(s_ev, CB)


def node_flows(nc, g, a, fwd, back, res):
    with stage_tools(nc, "node_flow") as t:
        s_ld, s_t, s_a, s_y, s_v, s_w = (t.sem(n) for n in ("loaded", "turned", "copied", "mixed", "vector", "weights"))
        W, bias = t.sb("W", [FH, HID]), t.sb("bias", [P, HID])
        deg = t.sb("deg", [P, NB])
        zt = t.sb("zt", [HID, 2, P])
        pt = [t.ps(f"pt{i}", [HID, P]) for i in range(2)]
        py = [t.ps(f"py{i}", [P, HID]) for i in range(2)]
        with nc.Block() as block:
            @block.sync
            def _(e):
                e.dma_start(W[0:HID, :], a["Wf2"]).then_inc(s_ld, 16)
                e.dma_start(W[HID:, :], a["Wf2"]).then_inc(s_ld, 16)
                e.dma_start(bias[:, :], a["bf2"].unsqueeze(0).partition_broadcast(P)).then_inc(s_ld, 16)

            @block.vector
            def _(e):
                e.wait_ge(s_ld, 48)
                e.tensor_scalar(W[HID:, :], W[HID:, :], 1.0 / LOW, None, ALU.mult).then_inc(s_w, 1)
                e.tensor_tensor(deg[:, :], g.deg[:, :], g.deg_out[:, :], ALU.add).then_inc(s_w, 1)
                e.wait_ge(s_w, 2)
                for k in range(NB):
                    e.wait_ge(s_y, k + 1)
                    e.scalar_tensor_tensor(res[:, k, :], bias[:, :], deg[:, k:k + 1], py[k % 2][:, :], ALU.mult, ALU.add).then_inc(s_v, 1)

            @block.tensor
            def _(e):
                e.wait_ge(s_w, 1)

                def mix(k):
                    e.wait_ge(s_a, k + 1)
                    if k >= 2:
                        e.wait_ge(s_v, k - 1)
                    e.matmul(py[k % 2][:, :], zt[:, k % 2, :], W[0:HID, :], start=True, stop=False)
                    e.matmul(py[k % 2][:, :], back[:, k * P:(k + 1) * P], W[:, :], start=False, stop=True).then_inc(s_y, 1)
                for k in range(NB):
                    if k >= 2:
                        e.wait_ge(s_a, k - 1)
                    e.transpose(pt[k % 2][:, :], fwd[:, k, :], g.ident[:, :]).then_inc(s_t, 1)
                    if k:
                        mix(k - 1)
                mix(NB - 1)

            @block.scalar
            def _(e):
                for k in range(NB):
                    e.wait_ge(s_t, k + 1)
                    if k >= 2:
                        e.wait_ge(s_y, k - 1)
                    e.activation(zt[:, k % 2, :], pt[k % 2][:, :], ACT.Copy).then_inc(s_a, 1)


def pointwise(nc, stage, ins):
    with stage_tools(nc, stage) as t:
        s_v = t.sem("vector")
        with nc.Block() as block:
            @block.vector
            def _(e):
                ins(e).then_inc(s_v, 1)
                e.wait_ge(s_v, 1)


def flow_layer(nc, g, a, dr):
    with stage_tools(nc, "l3") as t:
        s_ld, s_v = t.sem("loaded"), t.sem("vector")
        g.src_i, g.dst_f, g.src_f = t.sb("src_i", [P, EC], I32), t.sb("dst_f", [P, EC]), t.sb("src_f", [P, EC])
        dst_i = t.sb("dst_i", [P, EC], I32)
        sums, res = t.sb("sums", [P, NB, HID]), t.sb("res", [P, NB, HID])
        with nc.Block() as block:
            @block.sync
            def _(e):
                e.dma_start(g.src_i[:, :], a["src"]).then_inc(s_ld, 16)
                e.dma_start(dst_i[:, :], a["dst"]).then_inc(s_ld, 16)

            @block.vector
            def _(e):
                c = Chain(e, s_v)
                e.wait_ge(s_ld, 32)
                c(e.tensor_copy(g.dst_f[:, :], dst_i[:, :]))
                c(e.tensor_copy(g.src_f[:, :], g.src_i[:, :]))
                c(e.tensor_scalar(g.src_f[:, :], g.src_f[:, :], -float(HALF), None, ALU.add))
        with ExitStack() as c1:
            t1 = Tools(nc, c1, "l3a")
            PD, G = t1.sb("PD", [P, NB, FH]), t1.sb("G", [P, EC, D])
            linear(nc, g, "flow_dst", g.h[:, :, :], D, a["Wf1_dst"], a["bf1_twice"], PD)
            edge_flows(nc, g, a, dr, G, PD, sums)
        with ExitStack() as c2:
            back = Tools(nc, c2, "l3b").sb("back", [P, NP])
            backward_sums(nc, g, a, dr, back)
            node_flows(nc, g, a, sums, back, res)
        linear(nc, g, "node1", res[:, :, :], HID, a["Wn1"], a["bn1"], sums)
        pointwise(nc, "node_relu", lambda e: e.tensor_scalar(sums[:, :, :], sums[:, :, :], 0.0, None, ALU.max))
        linear(nc, g, "node2", sums[:, :, :], HID, a["Wn2"], a["bn2"], res[:, :, 0:D])
        pointwise(nc, "last_add", lambda e: e.tensor_tensor(g.x[:, :, :], g.x[:, :, :], res[:, :, 0:D], ALU.add))


def cg_tables():
    import math
    combos = [(0, 0, 0), (0, 1, 1), (1, 0, 1), (1, 1, 0), (1, 1, 1), (2, 1, 1)]

    def coeff(j1, m1, j2, m2, j3, m3):
        if m3 != m1 + m2:
            return 0.0
        f = math.factorial
        pref = (2 * j3 + 1) * f(j3 + j1 - j2) * f(j3 - j1 + j2) * f(j1 + j2 - j3) / f(j1 + j2 + j3 + 1)
        pref *= f(j3 + m3) * f(j3 - m3) * f(j1 - m1) * f(j1 + m1) * f(j2 - m2) * f(j2 + m2)
        s = 0.0
        for v in range(max(0, j2 - j3 - m1, j1 + m2 - j3), min(j1 + j2 - j3, j1 - m1, j2 + m2) + 1):
            s += (-1) ** v / (f(v) * f(j1 + j2 - j3 - v) * f(j1 - m1 - v) * f(j2 + m2 - v) * f(j3 - j2 + m1 + v) * f(j3 - j1 - m2 + v))
        return math.sqrt(pref) * s

    def qmat(l):
        q = np.zeros((2 * l + 1, 2 * l + 1), dtype=np.complex128)
        for m in range(-l, 0):
            q[l + m, l + abs(m)] = 1 / np.sqrt(2)
            q[l + m, l - abs(m)] = -1j / np.sqrt(2)
        q[l, l] = 1.0
        for m in range(1, l + 1):
            q[l + m, l + abs(m)] = (-1) ** m / np.sqrt(2)
            q[l + m, l - abs(m)] = 1j * (-1) ** m / np.sqrt(2)
        return (-1j) ** l * q

    M = 8
    cg = np.zeros((H9 * D, D), np.float32)
    which = np.zeros((H9 * D, D, 3), np.int64)
    first = {0: 0, 1: 1, 2: 4}
    for idx, (le, ln, lo) in enumerate(combos):
        C = np.zeros((2 * le + 1, 2 * ln + 1, 2 * lo + 1), dtype=np.complex128)
        for m1 in range(-le, le + 1):
            for m2 in range(-ln, ln + 1):
                if -lo <= m1 + m2 <= lo:
                    C[m1 + le, m2 + ln, m1 + m2 + lo] = coeff(le, m1, ln, m2, lo, m1 + m2)
        C = np.einsum('ij,kl,mn,ikn->jlm', qmat(le), qmat(ln), np.conj(qmat(lo)).T, C).real
        C = (C / np.linalg.norm(C)).astype(np.float32)
        for i in range(2 * le + 1):
            for m in range(M):
                for j in range(2 * ln + 1):
                    for o in range(M):
                        for k in range(2 * lo + 1):
                            r = (first[le] + i) * D + (m if ln == 0 else M + 3 * m + j)
                            q = o if lo == 0 else M + 3 * o + k
                            cg[r, q] = C[i, j, k]
                            which[r, q] = (idx, m, o)
    return cg, which


def program(nc, a, out, upto):
    dr = {n: nc.dram_tensor(n, s, d).ap() for n, s, d in [
        ("table0", (NP, AW), F32), ("table1", (NP, D), F32), ("edge_logit", (T, TS), F32), ("raw", (T, TS), F32),
        ("dst", (T, TS), F32), ("raw_cols", (P, EC), F32), ("counts", (NP, NP), F16),
        ] + [(f"hidden{b0}", ((b1 - b0) * T, P, J * FH), F16) for b0, b1 in GROUPS]}
    dr["hidden"] = [dr[f"hidden{b0}"] for b0, _ in GROUPS]
    with ExitStack() as ctx:
        t = Tools(nc, ctx, "keep")

        class Kept:
            pass
        g = Kept()
        g.rows_landed = [[t.sem(f"rows_landed{k}{h}") for h in range(2)] for k in range(3)]
        g.bounds = t.sb("bounds", [1, 2 * NB], I32)
        g.pcol, g.node_id, g.iota = t.sb("pcol", [P, 1]), t.sb("node_id", [P, NB]), t.sb("iota", [P, P])
        g.block_first = t.sb("block_first", [P, NB + 1])
        g.ident, g.ident16 = t.sb("ident", [P, P]), t.sb("ident16", [P, P], F16)
        g.x, g.h, g.deg = t.sb("x", [P, NB, D]), t.sb("h", [P, NB, D]), t.sb("deg", [P, NB])
        g.deg_out, g.dis, g.ones = t.sb("deg_out", [P, NB]), t.sb("dis", [P, NB]), t.sb("ones", [P, P])
        g.t0_done = g.t0_exp = g.t0_abs = 0
        edges = ExitStack()
        te = Tools(nc, edges, "edges")
        g.src_i, g.dst_f, g.src_f = te.sb("src_i", [P, EC], I32), te.sb("dst_f", [P, EC]), te.sb("src_f", [P, EC])
        with ExitStack() as early:
            te = Tools(nc, early, "early")
            g.ids16 = te.sb("ids16", [P, NP], F16)
            setup(nc, g, a, dr)
            table0(nc, g, a, dr)
            edge_logits(nc, g, a, dr)
            with ExitStack() as l0:
                G = Tools(nc, l0, "l0").sb("G", [P, EC, D + 1])
                if upto >= 1:
                    count_and_gather(nc, g, a, dr, G)
                if upto >= 2:
                    attention(nc, g, a, dr, G)
                if upto >= 3:
                    sums = Tools(nc, l0, "l0b").sb("sums", [P, NB, D + 1])
                    scatter(nc, g, dr, G, sums)
                    next_layer(nc, g, a, "layer1", dr["table1"], sums=sums)
        if upto >= 4:
            with ExitStack() as l1:
                t1 = Tools(nc, l1, "l1")
                sums = t1.sb("sums", [P, NB, H9 * D])
                mixed = t1.sb("mixed", [P, NB, D])
                G = t1.sb("G", [P, EC, D])
                scatter(nc, g, dr, G, sums, a["harmonics"], dr["table1"])
                mix_products(nc, g, a, sums, mixed)
                next_layer(nc, g, a, "layer2", None, mixed=mixed)
        edges.close()
        if upto >= 5:
            residual_gcn(nc, g, a, dr)
        if upto >= 6:
            flow_layer(nc, g, a, dr)
        with ExitStack() as fin:
            s_out = Tools(nc, fin, "fin").sem("stored")
            with nc.Block() as block:
                @block.sync
                def _(e):
                    full = N // P
                    e.dma_start(out[0:full * P, :].rearrange("(b p) f -> p b f", p=P), g.x[:, 0:full, :]).then_inc(s_out, 16)
                    e.dma_start(out[full * P:N, :], g.x[0:N - full * P, full, :]).then_inc(s_out, 16)
                    e.wait_ge(s_out, 32)


def layouts(inp):
    def rows(v, n, fill=0):
        return np.concatenate([v, np.full((n - v.shape[0],) + v.shape[1:], fill, v.dtype)])

    def columns(v):
        return np.ascontiguousarray(v.reshape(EC, P, -1).transpose(1, 0, 2))
    i = {k: np.asarray(v) for k, v in inp.items()}
    ep = T * TS
    src, dst = rows(i["src"], ep), rows(i["dst"], ep, NP)
    off = np.array([0.0, 0.0, 0.0, -1.0], np.float32)
    per = np.array([1 / 50.0, 1.0, 1.0, 1 / 10.0], np.float32)
    spread = np.zeros((QT, 4, QT, 4, K8), np.float32)
    for q in range(QT):
        for c in range(4):
            spread[q, c, q, c, :] = per[c] / DENOM
    bias1 = np.tile(((off[:, None] - GRID[None, :]) / DENOM).reshape(-1), QT).astype(np.float32)
    w_edge = np.zeros((QT, 4 * K8, QT, 2 * P), np.float32)
    for q in range(QT):
        w_edge[q, :, q, :] = np.repeat(i["L0_gnn_W_edge"].T, K8, axis=1)
    w_edge = w_edge.reshape(P, QT, 2 * P)
    cg, which = cg_tables()
    w1 = i["L1_gnn_W"][which[..., 0], which[..., 1], which[..., 2]]
    return {
        "x": rows(i["x"], NP), "src": columns(src)[:, :, 0], "dst": columns(dst)[:, :, 0], "dst_rows": dst.reshape(T, TS),
        "node_vec": np.ascontiguousarray(rows(i["node_vec"], NP).reshape(NB, P).T),
        "edge_attr_4": np.ascontiguousarray(rows(i["edge_attr_4"], ep).reshape(QN, QT, TS, 4).transpose(1, 3, 0, 2)
                                            .reshape(4 * QT, QN * TS)),
        "harmonics": columns(rows(np.concatenate([i["edge_weight1"], i["edge_attr_3"], i["edge_attr_5"]], axis=1), ep)),
        "W_att": i["L0_gnn_W_att"], "W_lar": i["L0_gnn_W_lar"], "b_att": i["L0_gnn_b_att"], "b_lar": i["L0_gnn_b_lar"],
        "grid": GRID[None, :], "grid_col": np.tile(GRID, P // K8)[:, None].copy(),
        "spread": spread.reshape(4 * QT, P), "bias1": bias1[:, None], "W_edge": w_edge,
        "W_att_edge": np.ascontiguousarray(i["L0_gnn_W_att"][0, :D * K8].reshape(2, P).T),
        "b_edge": np.ascontiguousarray(np.repeat(i["L0_gnn_b_edge"], K8).reshape(2, P).T),
        "cg": cg, "W1_rep": w1,
        "gamma_hid": i["L2_gnn_bn_gamma_hid"], "beta_hid": i["L2_gnn_bn_beta_hid"],
        "gamma_out": i["L2_gnn_bn_gamma_out"], "beta_out": i["L2_gnn_bn_beta_out"],
        "edge_attr_16": rows(i["edge_attr_16"], ep).reshape(T, J, P, ED).transpose(0, 3, 1, 2),
        "Wf1_dst": np.concatenate([i["L3_gnn_Wf1"][0:D], i["L3_gnn_Wf1"][D:2 * D]], axis=1),
        "Wf1_src": np.concatenate([np.concatenate([i["L3_gnn_Wf1"][D:2 * D], i["L3_gnn_Wf1"][2 * D:]]),
                                   np.concatenate([i["L3_gnn_Wf1"][0:D], i["L3_gnn_Wf1"][2 * D:]])], axis=1),
        "bf1_twice": np.concatenate([i["L3_gnn_bf1"], i["L3_gnn_bf1"]]),
        **{k: i["L3_gnn_" + k] for k in ("Wf2", "bf2", "Wn1", "bn1", "Wn2", "bn2")},
        **{k: i["L2_gnn_" + k] for k in ("W_enc1", "b_enc1", "W_hid", "b_hid", "W_dec2", "b_dec2", "W_dec3", "b_dec3",
                                         "Wres_enc1", "bres_enc1", "Wres_dec2", "bres_dec2")},
    }


def kernel(**inputs):
    import concourse.bacc as bacc
    from concourse.bass_utils import run_bass_kernel_spmd as run

    nc = bacc.Bacc("TRN2", target_bir_lowering=False, num_devices=1)
    arrays, a = {}, {}
    for name, v in layouts(inputs).items():
        v = np.ascontiguousarray(v)
        arrays[f"in_{name}_dram"] = v
        a[name] = nc.dram_tensor(f"in_{name}_dram", v.shape, mybir.dt.from_np(v.dtype), kind="ExternalInput").ap()
    out = nc.dram_tensor("out_0_dram", (N, D), F32, kind="ExternalOutput").ap()
    program(nc, a, out, PHASES)
    r = run(nc, [arrays], core_ids=[0])
    return r.results[0]["out_0_dram"]
```

```python
from contextlib import ExitStack, contextmanager

import concourse.bass as bass
import numpy as np
from concourse import mybir

F32 = mybir.dt.float32
F16 = mybir.dt.float16
I32 = mybir.dt.int32
U32 = mybir.dt.uint32
ALU = mybir.AluOpType
ACT = mybir.ActivationFunctionType
X = mybir.AxisListType.X
ds = bass.ds

P = 128
N = 3125
NB = -(-N // P)
NP = NB * P
E = 100000
J = 4
TS = J * P
T = -(-E // TS)
EC = T * J
D = 32
K8 = 8
HALF = NP // 2
BIG = 1.0e30
EPS = 1e-5
GRID = np.linspace(-2.0, 2.0, K8, dtype=np.float32)
DENOM = float(GRID[1] - GRID[0])
QT = 4
QN = T // QT
AW = 36
GC = 8
GN = EC // GC // 2
JP = 2 * J
PS = JP * P
PN = T // 2
SL = 2
assert PN % SL == 0 and T % QT == 0 and EC % (2 * GC) == 0 and T % 2 == 0
PHASES = 6


class Tools:

    def __init__(self, nc, ctx, stage):
        self.nc, self.ctx, self.stage, self.sems = nc, ctx, stage, []

    def sb(self, name, shape, dt=F32):
        return self.ctx.enter_context(self.nc.sbuf_tensor(f"{self.stage}_{name}", shape, dt))

    def ps(self, name, shape, dt=F32):
        return self.ctx.enter_context(self.nc.psum_tensor(f"{self.stage}_{name}", shape, dt))

    def sem(self, name):
        self.sems.append(self.ctx.enter_context(self.nc.semaphore(f"{self.stage}_{name}")))
        return self.sems[-1]


@contextmanager
def stage_tools(nc, stage):
    with ExitStack() as ctx:
        t = Tools(nc, ctx, stage)
        yield t
        with nc.Block() as block:
            @block.sync
            def _(e):
                for s in t.sems:
                    e.sem_clear(s)


class Chain:

    def __init__(self, eng, sem):
        self.eng, self.sem, self.n = eng, sem, 0

    def __call__(self, ins):
        ins.then_inc(self.sem, 1)
        self.n += 1
        self.eng.wait_ge(self.sem, self.n)
        return self.n


def bcast(ap, shape):
    return ap.broadcast_to(shape)


def setup(nc, g, a, dr):
    with stage_tools(nc, "setup") as t:
        s_load, s_pool, s_v, s_pe = t.sem("loaded"), t.sem("pool"), t.sem("vector"), t.sem("tensor")
        dst_t = t.sb("dst_t", [T // 2, 2 * TS], I32)
        dst_f = t.sb("dst_f", [T // 2, 2 * TS])
        dst_i = t.sb("dst_i", [P, EC], I32)
        hi_t, lo_t = t.sb("hi_t", [T // 2, 2]), t.sb("lo_t", [T // 2, 2])
        first_id, next_id = g.block_first, t.sb("next_id", [P, NB])
        rank, back = t.sb("rank", [P, 2]), t.sb("back", [P, 2])
        keys = t.sb("keys", [T // 2, 2, 2, NB])
        tb_f, pb_i, s_tb = t.sb("pair_range", [T // 2, 3]), t.sb("pair_blocks", [T // 2, 1], I32), t.sem("pair_blocks")
        dst16 = t.sb("dst16", [T // 2, 2 * TS], F16)
        key = t.sb("key", [T // 2, 2 * NB])
        best, bounds = t.sb("best", [2 * NB, 1]), t.sb("bounds", [1, 2 * NB])
        ids = g.ids
        pk, pb = t.ps("pk", [2 * NB, P]), t.ps("pb", [1, 2 * NB])
        with nc.Block() as block:
            @block.sync
            def _(e):
                e.dma_start(g.src_i[:, :], a["src"]).then_inc(s_load, 16)
                e.dma_start(dst_i[:, :], a["dst"]).then_inc(s_load, 16)
                e.dma_start(dst_t[:, :], a["dst_rows"].rearrange("(p c) n -> p (c n)", c=2)).then_inc(s_load, 16)
                e.wait_ge(s_tb, 1)
                e.dma_start(dr["pair_blocks"], pb_i[:, :]).then_inc(s_load, 16)
                e.dma_start(dr["dst16"], dst16[:, :]).then_inc(s_load, 16)
                e.wait_ge(s_load, 80)
                e.dma_start(g.pair_blocks[:, :], dr["pair_blocks"].rearrange("t a -> a t")).then_inc(s_load, 16)
                e.wait_ge(s_load, 96)

            @block.gpsimd
            def _(e):
                e.iota(ids[:, :], [[1, NP]], base=-HALF, channel_multiplier=0,
                       allow_small_or_imprecise_dtypes=True).then_inc(s_pool, 1)
                e.iota(g.pcol[:, :], [[1, 1]], base=0, channel_multiplier=1,
                       allow_small_or_imprecise_dtypes=True).then_inc(s_pool, 1)
                e.iota(g.node_id[:, :], [[P, NB]], base=0, channel_multiplier=1,
                       allow_small_or_imprecise_dtypes=True).then_inc(s_pool, 1)
                e.iota(g.iota[:, :], [[1, P]], base=0, channel_multiplier=0,
                       allow_small_or_imprecise_dtypes=True).then_inc(s_pool, 1)
                e.iota(first_id[:, :], [[P, NB + 1]], base=0, channel_multiplier=0,
                       allow_small_or_imprecise_dtypes=True).then_inc(s_pool, 1)
                e.iota(next_id[:, :], [[P, NB]], base=P, channel_multiplier=0,
                       allow_small_or_imprecise_dtypes=True).then_inc(s_pool, 1)
                e.iota(rank[:, :], [[1, 2]], base=1, channel_multiplier=2,
                       allow_small_or_imprecise_dtypes=True).then_inc(s_pool, 1)
                e.iota(back[:, :], [[-1, 2]], base=T, channel_multiplier=-2,
                       allow_small_or_imprecise_dtypes=True).then_inc(s_pool, 1)

            @block.vector
            def _(e):
                c = Chain(e, s_v)
                c(e.memset(g.ones[:, :], 1.0))
                e.wait_ge(s_pool, 8)
                c(e.tensor_copy(g.ids16[:, :], ids[:, :]))
                c(e.tensor_scalar(g.ident[:, :], g.iota[:, :], g.pcol[:, 0:1], None, ALU.is_equal))
                c(e.tensor_copy(g.ident16[:, :], g.ident[:, :]))
                e.wait_ge(s_load, 48)
                c(e.tensor_scalar(g.dst_c[:, :], dst_i[:, :], -float(HALF), None, ALU.add))
                c(e.tensor_copy(g.src_f[:, :], g.src_i[:, :]))
                c(e.tensor_scalar(g.src_f[:, :], g.src_f[:, :], -float(HALF), None, ALU.add))
                c(e.tensor_copy(dst_f[:, :], dst_t[:, :]))
                rows = dst_f[:, :].rearrange("p (c n) -> p c n", c=2)
                c(e.tensor_reduce(hi_t[:, :], rows, X, ALU.max))
                c(e.tensor_reduce(lo_t[:, :], rows, X, ALU.min))
                n2 = T // 2
                for k in range(2):
                    c(e.tensor_scalar(keys[:, 0, k, :], first_id[0:n2, 0:NB], hi_t[:, k:k + 1], back[0:n2, k:k + 1],
                                      ALU.is_le, ALU.mult))
                    c(e.tensor_scalar(keys[:, 1, k, :], next_id[0:n2, :], lo_t[:, k:k + 1], rank[0:n2, k:k + 1],
                                      ALU.is_gt, ALU.mult))
                c(e.tensor_tensor(key[:, :].rearrange("p (a b) -> p a b", a=2), keys[:, :, 0, :], keys[:, :, 1, :],
                                  ALU.max))
                e.wait_ge(s_pe, 1)
                c(e.tensor_reduce(best[:, :], pk[:, 0:n2], X, ALU.max))
                e.wait_ge(s_pe, 2)
                c(e.tensor_scalar(bounds[:, 0:NB], pb[:, 0:NB], -1.0, float(T), ALU.mult, ALU.add))
                c(e.tensor_copy(bounds[:, NB:], pb[:, NB:]))
                c(e.tensor_copy(g.bounds[:, :], bounds[:, :]))
                c(e.tensor_reduce(tb_f[:, 0:1], lo_t[:, :], X, ALU.min))
                c(e.tensor_reduce(tb_f[:, 1:2], hi_t[:, :], X, ALU.max))
                c(e.tensor_scalar(keys[:, 0, 0, :], next_id[0:n2, :], tb_f[:, 0:1], None, ALU.is_le))
                c(e.tensor_scalar(keys[:, 0, 1, :], first_id[0:n2, 0:NB], tb_f[:, 1:2], 32.0, ALU.is_le, ALU.mult))
                c(e.tensor_reduce(tb_f[:, 2:3], keys[:, 0, :, :].rearrange("p k b -> p (k b)"), X, ALU.add))
                c(e.tensor_copy(pb_i[:, :], tb_f[:, 2:3]))
                c(e.tensor_scalar(dst16[:, :], dst_f[:, :], -float(HALF), None, ALU.add))
                c(e.tensor_scalar(g.node_c[:, :], g.node_id[:, :], -float(HALF), None, ALU.add))
                e.sem_inc(s_tb, 1)

            @block.tensor
            def _(e):
                e.wait_ge(s_v, 15)
                e.transpose(pk[:, 0:T // 2], key[:, :], g.ident[0:T // 2, 0:T // 2]).then_inc(s_pe, 1)
                e.wait_ge(s_v, 16)
                e.transpose(pb[:, :], best[:, :], g.ident[0:2 * NB, 0:2 * NB]).then_inc(s_pe, 1)


def layernorm_relu(e, c, wait_scalar, t, x, h, s_root):
    m, v, sq = t
    c(e.tensor_reduce(m[:, :], x, X, ALU.add))
    c(e.tensor_scalar(m[:, :], m[:, :], 1.0 / D, None, ALU.mult))
    c(e.tensor_tensor(h, x, bcast(m[:, :].unsqueeze(2), [P, NB, D]), ALU.subtract))
    c(e.tensor_tensor(sq, h, h, ALU.mult))
    c(e.tensor_reduce(v[:, :], sq, X, ALU.add))
    c(e.tensor_scalar(v[:, :], v[:, :], 1.0 / D, EPS, ALU.mult, ALU.add))
    wait_scalar()
    c(e.reciprocal(v[:, :], v[:, :]))
    c(e.tensor_tensor(h, h, bcast(v[:, :].unsqueeze(2), [P, NB, D]), ALU.mult))
    c(e.tensor_scalar(h, h, 0.0, None, ALU.max))


def table0(nc, g, a, dr):
    with stage_tools(nc, "table0") as t:
        s_load, s_v, s_a, s_out = t.sem("loaded"), t.sem("vector"), t.sem("scalar"), t.sem("stored")
        m, v = t.sb("mean", [P, NB]), t.sb("var", [P, NB])
        h, sq = t.sb("h", [P, NB, D]), t.sb("sq", [P, NB, D])
        z, w = t.sb("z", [P, NB, D, K8]), t.sb("w", [P, D * K8])
        grid, wl = t.sb("grid", [P, K8]), t.sb("wl", [P, K8])
        ba, bl = t.sb("ba", [P, 1]), t.sb("bl", [P, 1])
        cnt, zc = t.sb("cnt", [P, NB]), t.sb("zc", [P, NB, K8])
        u, ua, ul = t.sb("u", [P, NB]), t.sb("ua", [P, NB]), t.sb("ul", [P, NB])
        tab = t.sb("tab", [P, NB, AW])
        with nc.Block() as block:
            @block.vector
            def _(e):
                c = Chain(e, s_v)
                e.wait_ge(s_load, 16 * 7)
                c(e.memset(tab[:, :, :], 0.0))
                layernorm_relu(e, c, lambda: e.wait_ge(s_a, 1), (m, v, sq[:, :, :]), g.x[:, :, :], h[:, :, :], None)
                gz = grid[:, :].unsqueeze(1).unsqueeze(1)
                c(e.tensor_tensor(z[:, :, :, :], bcast(h[:, :, :].unsqueeze(3), [P, NB, D, K8]),
                                  bcast(gz, [P, NB, D, K8]), ALU.subtract))
                c(e.tensor_tensor(z[:, :, :, :], z[:, :, :, :], z[:, :, :, :], ALU.mult))
                c(e.tensor_tensor(zc[:, :, :], bcast(cnt[:, :].unsqueeze(2), [P, NB, K8]),
                                  bcast(grid[:, :].unsqueeze(1), [P, NB, K8]), ALU.subtract))
                g.t0_exp = c(e.tensor_tensor(zc[:, :, :], zc[:, :, :], zc[:, :, :], ALU.mult))
                e.wait_ge(s_a, 3)
                wz = w[:, :].rearrange("p (f k) -> p f k", k=K8).unsqueeze(1)
                c(e.tensor_tensor(z[:, :, :, :], z[:, :, :, :], bcast(wz, [P, NB, D, K8]), ALU.mult))
                c(e.tensor_reduce(u[:, :], z[:, :, :, :].rearrange("p b f k -> p b (f k)"), X, ALU.add))
                c(e.tensor_scalar(tab[:, :, D], u[:, :], ba[:, 0:1], None, ALU.add))
                c(e.tensor_tensor(zc[:, :, :], zc[:, :, :], bcast(wl[:, :].unsqueeze(1), [P, NB, K8]), ALU.mult))
                c(e.tensor_reduce(u[:, :], zc[:, :, :], X, ALU.add))
                c(e.tensor_scalar(u[:, :], u[:, :], bl[:, 0:1], None, ALU.add))
                c(e.tensor_scalar(ua[:, :], u[:, :], -1.0, None, ALU.mult))
                g.t0_abs = c(e.tensor_tensor(ua[:, :], ua[:, :], u[:, :], ALU.min))
                e.wait_ge(s_a, 5)
                c(e.tensor_scalar(u[:, :], u[:, :], 0.0, None, ALU.max))
                c(e.tensor_tensor(ul[:, :], ul[:, :], u[:, :], ALU.add))
                g.t0_done = c(e.tensor_tensor(tab[:, :, 0:D], h[:, :, :],
                                              bcast(ul[:, :].unsqueeze(2), [P, NB, D]), ALU.mult))

            @block.sync
            def _(e):
                e.dma_start(g.x[:, :, :], a["x"].rearrange("(b p) f -> p b f", p=P)).then_inc(s_load, 16)
                e.dma_start(cnt[:, :], a["node_vec"]).then_inc(s_load, 16)
                e.dma_start(w[:, :], a["W_att"][0:1, D * K8:].partition_broadcast(P)).then_inc(s_load, 16)
                e.dma_start(wl[:, :], a["W_lar"][0:1, :].partition_broadcast(P)).then_inc(s_load, 16)
                e.dma_start(ba[:, :], a["b_att"].unsqueeze(0).partition_broadcast(P)).then_inc(s_load, 16)
                e.dma_start(bl[:, :], a["b_lar"].unsqueeze(0).partition_broadcast(P)).then_inc(s_load, 16)
                e.dma_start(grid[:, :], a["grid"][0:1, :].partition_broadcast(P)).then_inc(s_load, 16)
                e.wait_ge(s_v, g.t0_done)
                e.dma_start(dr["table0"].rearrange("(b p) f -> p b f", p=P), tab[:, :, :]).then_inc(s_out, 16)
                e.wait_ge(s_out, 16)

            @block.scalar
            def _(e):
                e.wait_ge(s_v, 7)
                e.activation(v[:, :], v[:, :], ACT.Sqrt).then_inc(s_a, 1)
                e.wait_ge(s_v, g.t0_exp)
                e.activation(z[:, :, :, :], z[:, :, :, :], ACT.Exp, scale=-1.0 / DENOM ** 2).then_inc(s_a, 1)
                e.activation(zc[:, :, :], zc[:, :, :], ACT.Exp, scale=-1.0 / DENOM ** 2).then_inc(s_a, 1)
                e.wait_ge(s_v, g.t0_abs)
                e.activation(ul[:, :], ua[:, :], ACT.Exp).then_inc(s_a, 1)
                e.wait_ge(s_a, 4)
                e.activation(ul[:, :], ul[:, :], ACT.Ln, bias=1.0).then_inc(s_a, 1)



def edge_logits(nc, g, a, dr):
    with stage_tools(nc, "logit") as t:
        s_load, s_w = t.sem("loaded"), t.sem("weights")
        s_p1, s_sq1, s_r1 = t.sem("spread"), t.sem("squared1"), t.sem("bases1")
        s_z2, s_sq2, s_r2 = t.sem("features"), t.sem("squared2"), t.sem("bases2")
        s_wr, s_wd, s_at, s_ev = t.sem("half_weighed"), t.sem("weighed"), t.sem("summed"), t.sem("copied")
        s_out, s_st = t.sem("landed"), t.sem("stored")
        ea = t.sb("ea", [4 * QT, QN * TS])
        spread, bias1 = t.sb("spread", [4 * QT, P]), t.sb("bias1", [P, 1])
        w_edge, watt = t.sb("w_edge", [P, QT, 2 * P]), t.sb("watt", [P, 2])
        bias2, gcol, brep = t.sb("bias2", [P, 2]), t.sb("gcol", [P, 1]), t.sb("brep", [P, 2])
        pick = t.sb("pick", [P, QT, QT])
        r1, r2 = t.sb("r1", [P, 2, TS]), t.sb("r2", [P, 2, 2, TS])
        wr, wd = t.sb("wr", [P, 2, TS]), t.sb("wd", [P, 2, TS])
        el = t.sb("el", [QT, 2, TS])
        p1, pa = t.ps("p1", [P, TS]), [t.ps(f"pa{i}", [QT, TS]) for i in range(2)]
        z2 = [t.ps(f"z2_{i}", [P, 2, TS]) for i in range(2)]
        with nc.Block() as block:
            def steps(eng, step):
                with eng.Fori(0, QN // 2, 1) as k:
                    step(2 * k, 0)
                    step(2 * k + 1, 1)
                step(QN - 1, 0)

            @block.sync
            def _(e):
                for dst_ap, src_ap in ((spread[:, :], a["spread"]), (bias1[:, :], a["bias1"]), (w_edge[:, :, :], a["W_edge"]),
                                       (watt[:, :], a["W_att_edge"]), (brep[:, :], a["b_edge"]), (gcol[:, :], a["grid_col"]),
                                       (ea[:, :], a["edge_attr_4"])):
                    e.dma_start(dst_ap, src_ap).then_inc(s_load, 16)

                def step(i, par):
                    e.wait_ge(s_ev, i + 3)
                    e.dma_start(dr["edge_logit"][ds(i * QT, QT), :], el[:, par, :]).then_inc(s_out, 16)
                    e.wait_ge(s_out, 16 * (i + 1))
                    e.sem_inc(s_st, 1)
                e.sem_inc(s_st, 2)
                steps(e, step)

            @block.vector
            def _(e):
                c = Chain(e, s_w)
                e.wait_ge(s_load, 16 * 7)
                c(e.memset(pick[:, :, :], 0.0))
                for q in range(QT):
                    c(e.memset(pick[:, q, q:q + 1], 1.0))
                c(e.tensor_tensor(bias2[:, :], brep[:, :], bcast(gcol[:, 0:1], [P, 2]), ALU.subtract))
                c(e.tensor_scalar(bias2[:, :], bias2[:, :], 1.0 / DENOM, None, ALU.mult))

                e.sem_inc(s_wd, 2)
                e.sem_inc(s_ev, 2)

                def step(i, par):
                    for q in range(QT):
                        n, s = i * QT + q, q % 2
                        e.wait_ge(s_r2, n + 3)
                        e.tensor_scalar(wr[:, s, :], r2[:, s, 0, :], watt[:, 0:1], None, ALU.mult).then_inc(s_wr, 1)
                        e.wait_ge(s_wr, n + 1)
                        e.wait_ge(s_at, n + 1)
                        e.scalar_tensor_tensor(wd[:, s, :], r2[:, s, 1, :], watt[:, 1:2], wr[:, s, :],
                                               ALU.mult, ALU.add).then_inc(s_wd, 1)
                    e.wait_ge(s_at, i * QT + QT + 2)
                    e.wait_ge(s_st, i + 1)
                    e.tensor_copy(el[:, par, :], pa[par][:, :]).then_inc(s_ev, 1)
                steps(e, step)

            @block.scalar
            def _(e):
                e.wait_ge(s_w, 7)
                e.sem_inc(s_r2, 2)

                def bases1(i, par):
                    e.wait_ge(s_p1, i + 1)
                    e.activation(r1[:, par, :], p1[:, :], ACT.Square, bias=bias1[:, 0:1]).then_inc(s_sq1, 1)
                    e.wait_ge(s_sq1, i + 1)
                    e.activation(r1[:, par, :], r1[:, par, :], ACT.Exp, scale=-1.0).then_inc(s_r1, 1)

                def step(i, par, last=False):
                    for q in range(QT):
                        n, s = i * QT + q, q % 2
                        e.wait_ge(s_z2, n + 1)
                        e.wait_ge(s_wd, n + 1)
                        for h in range(2):
                            e.activation(r2[:, s, h, :], z2[s][:, h, :], ACT.Square, bias=bias2[:, h:h + 1],
                                         scale=1.0 / DENOM).then_inc(s_sq2, 1)
                        e.wait_ge(s_sq2, 2 * n + 2)
                        e.activation(r2[:, s, :, :], r2[:, s, :, :], ACT.Exp, scale=-1.0).then_inc(s_r2, 1)
                        if q == 1 and not last:
                            bases1(i + 1, 1 - par)
                bases1(0, 0)
                with e.Fori(0, QN // 2, 1) as k:
                    step(2 * k, 0)
                    step(2 * k + 1, 1)
                step(QN - 1, 0, True)

            @block.tensor
            def _(e):
                e.wait_ge(s_w, 7)
                e.sem_inc(s_at, 2)

                def expand(i):
                    e.matmul(p1[:, :], spread[:, :], ea[:, ds(i * TS, TS)], start=True, stop=True).then_inc(s_p1, 1)

                def features(n, par, q):
                    for h in range(2):
                        m = e.matmul(z2[q % 2][:, h, :], w_edge[:, q, h * P:(h + 1) * P],
                                     r1[:, par, :], start=True, stop=True)
                    m.then_inc(s_z2, 1)

                def weigh(n, par, q):
                    e.wait_ge(s_wd, n + 3)
                    e.matmul(pa[par][:, :], pick[:, q, :], wd[:, q % 2, :], start=(q == 0), stop=(q == QT - 1)).then_inc(s_at, 1)

                def step(i, par, last=False):
                    for q in range(QT):
                        n = i * QT + q
                        if q == 0:
                            e.wait_ge(s_r1, i + 1)
                        e.wait_ge(s_r2, n + 1)
                        features(n, par, q)
                        if q == 0 and not last:
                            e.wait_ge(s_sq1, i + 1)
                            expand(i + 1)
                        if q == 0:
                            e.wait_ge(s_ev, i + 1)
                        if q > 0:
                            weigh(n - 1, par, q - 1)
                    weigh(i * QT + QT - 1, par, QT - 1)
                expand(0)
                with e.Fori(0, QN // 2, 1) as k:
                    step(2 * k, 0)
                    step(2 * k + 1, 1)
                step(QN - 1, 0, True)


def node_gather(e, t, g, table, width, slots, everything, s_slot, s_claim, s_kept):
    idx = t.sb("idx", [P, 2, GC], I32)
    s_idx = t.sem("idx")

    def fetch(c, k, h):
        e.wait_ge(s_slot[h][1], k + 1)
        e.sem_inc(s_claim, 1)
        e.tensor_copy(idx[:, h, :], g.src_i[:, ds(c * GC, GC)]).then_inc(s_idx, 1)
        e.wait_ge(s_idx, c + 1)
        e.sem_inc(s_claim, 1)
        for j in range(GC):
            e.indirect_dma_start(slots[:, h, j, :], None, table,
                                 bass.IndirectOffsetOnAxis(ap=idx[:, h, j:j + 1].bitcast(U32), axis=0)).then_inc(s_slot[h][0], 16)

    def keep(c, k, h):
        e.wait_ge(s_slot[h][0], 16 * GC * (k + 1))
        e.sem_inc(s_claim, 1)
        e.tensor_copy(everything[:, ds(c * GC, GC), :], slots[:, h, :, 0:width]).then_inc(s_kept, 2)
        e.wait_ge(s_kept, 2 * (c + 1))
        e.sem_inc(s_slot[h][1], 1)

    e.sem_inc(s_slot[0][1], 1)
    e.sem_inc(s_slot[1][1], 1)
    fetch(0, 0, 0)
    fetch(1, 0, 1)
    with e.Fori(1, GN, 1) as i:
        keep(2 * i - 2, i - 1, 0)
        fetch(2 * i, i, 0)
        keep(2 * i - 1, i - 1, 1)
        fetch(2 * i + 1, i, 1)
    keep(2 * GN - 2, GN - 1, 0)
    keep(2 * GN - 1, GN - 1, 1)


def tile_range(e, g, b):
    return (e.value_load(g.bounds[0:1, ds(b, 1)], min_val=0, max_val=T - 1),
            e.value_load(g.bounds[0:1, ds(b + NB, 1)], min_val=0, max_val=T))


class Count:

    def __init__(self, e, name, most):
        self.e, self.most = e, most
        self.reg = e.alloc_register(name)
        e.reg_mov(self.reg, 0)

    def now(self):
        return self.e.snap(self.reg, min_val=0, max_val=self.most)

    def up(self):
        self.e.reg_add(self.reg, self.reg, 1)


VISITS = NB * T
CB = -(-NP // 512)


def count_and_gather(nc, g, a, dr, G):
    with stage_tools(nc, "count") as t:
        s_slot = [(g.rows_landed[0][h], t.sem(f"free{h}")) for h in range(2)]
        s_claim, s_kept = t.sem("claim"), t.sem("kept")
        s_oh, s_used, s_sum, s_ev, s_out, s_st = (t.sem(n) for n in (
            "onehot", "used", "summed", "copied", "landed", "stored"))
        s_z, s_turn = t.sem("zeros"), t.sem("turn")
        slots = t.sb("slots", [P, 2, GC, AW])
        ohs = t.sb("ohs", [P, J, NP], F16)
        ohd = t.sb("ohd", [P, J, P], F16)
        zero = t.sb("zero", [1, 512], F16)
        row = t.sb("row", [P, 2, NP], F16)
        degc = t.sb("degc", [P, NB, CB])
        acc = t.ps("acc", [P, CB, 512])
        with nc.Block() as block:
            @block.gpsimd
            def _(e):
                node_gather(e, t, g, dr["table0"][:, :], D + 1, slots, G, s_slot, s_claim, s_kept)

            @block.vector
            def _(e):
                e.memset(zero[:, :], 0.0).then_inc(s_z, 1)
                v = Count(e, "v", VISITS)
                with e.Fori(0, NB, 1) as b:
                    lo, hi = tile_range(e, g, b)
                    with e.Fori(lo, hi, 1) as tt:
                        n = v.now()
                        for j in range(J):
                            e.wait_ge(s_used, n * J + j + 1)
                            e.tensor_scalar(ohd[:, j, :], g.ids16[:, ds(b * P, P)], g.dst_c[:, ds(tt * J + j, 1)], None, ALU.is_equal).then_inc(s_oh, 1)
                            e.tensor_scalar(ohs[:, j, :], g.ids16[:, :], g.src_f[:, ds(tt * J + j, 1)], None, ALU.is_equal).then_inc(s_oh, 1)
                        v.up()

            @block.tensor
            def _(e):
                e.wait_ge(s_z, 1)
                e.sem_inc(s_used, J)
                v = Count(e, "v", VISITS)
                with e.Fori(0, NB, 1) as b:
                    lo, hi = tile_range(e, g, b)
                    e.wait_ge(s_ev, CB * b + 1)
                    for k in range(CB):
                        if k:
                            e.wait_ge(s_ev, CB * b + k + 1)
                        w = min(512, NP - 512 * k)
                        e.matmul(acc[:, k, 0:w], zero[0:1, 0:P], zero[0:1, 0:w], start=True, stop=False, skip_group_check=True)
                    with e.Fori(lo, hi, 1) as tt:
                        n = v.now()
                        for j in range(J):
                            e.wait_ge(s_oh, (n * J + j) * 2 + 2)
                            for k in range(CB):
                                w = min(512, NP - 512 * k)
                                m = e.matmul(acc[:, k, 0:w], ohd[:, j, :], ohs[:, j, 512 * k:512 * k + w],
                                             start=False, stop=False, skip_group_check=True)
                            m.then_inc(s_used, 1)
                        v.up()
                    e.matmul(acc[:, CB - 1, 0:P], zero[0:1, 0:P], zero[0:1, 0:P], start=False, stop=True,
                             skip_group_check=True).then_inc(s_sum, 1)

            @block.scalar
            def _(e):
                e.sem_inc(s_ev, CB)
                with e.Fori(0, NB, 1) as b:
                    e.wait_ge(s_sum, b + 1)
                    e.wait_ge(s_st, b + 1)
                    for k in range(CB):
                        w = min(512, NP - 512 * k)
                        e.activation(row[:, ds(b % 2, 1), 512 * k:512 * k + w].rearrange("p a n -> p (a n)"), acc[:, k, 0:w],
                                     ACT.Copy, accum_out=degc[:, ds(b, 1), k:k + 1].rearrange("p a n -> p (a n)")).then_inc(s_ev, 1)

            @block.sync
            def _(e):
                e.sem_inc(s_st, 2)
                with e.Fori(0, NB, 1) as b:
                    e.wait_ge(s_ev, CB * (b + 2))
                    e.dma_start(dr["counts"][ds(b * P, P), :], row[:, ds(b % 2, 1), :].rearrange("p a n -> p (a n)")).then_inc(s_out, 16)
                    e.wait_ge(s_out, 16 * (b + 1))
                    e.sem_inc(s_st, 1)
        s_d = t.sem("degree")
        with nc.Block() as block:
            @block.vector
            def _(e):
                e.tensor_reduce(g.deg[:, :], degc[:, :, :], X, ALU.add).then_inc(s_d, 1)
                e.wait_ge(s_d, 1)


def pair_range(e, g, b):
    lo, hi = tile_range(e, g, b)
    return e.snap(lo // 2, min_val=0, max_val=T // 2 - 1), e.snap((hi + 1) // 2, min_val=0, max_val=T // 2)


def raw_logits(nc, g, a, dr, G, raw):
    bf = mybir.dt.bfloat16
    R = EC // 7
    with stage_tools(nc, "attn") as t:
        s_load, s_pe, s_v, s_a, s_out = (t.sem(n) for n in ("loaded", "tensor", "vector", "scalar", "stored"))
        cols, back = t.sb("cols", [R, 7, P]), t.sb("back", [R, 7, P])
        pc = t.ps("pc", [P, 2, 512])
        pr = t.ps("pr", [R, 2, 512])
        with nc.Block() as block:
            @block.sync
            def _(e):
                e.dma_start(cols[:, :, :], dr["edge_logit"].rearrange("t (j n) -> (t j) n", n=P)
                            .rearrange("(c r) n -> r c n", r=R)).then_inc(s_load, 16)
                e.wait_ge(s_a, 2)
                e.dma_start(dr["raw"].rearrange("t (j n) -> (t j) n", n=P).rearrange("(c r) n -> r c n", r=R),
                            back[:, :, :]).then_inc(s_out, 16)
                e.wait_ge(s_out, 16)

            @block.tensor
            def _(e):
                e.wait_ge(s_load, 16)
                for c in range(7):
                    m = e.transpose(pc[:, c // 4, (c % 4) * R:(c % 4 + 1) * R], cols[:, c, :], g.ident[0:R, 0:R])
                m.then_inc(s_pe, 1)
                e.wait_ge(s_v, 2)
                for c in range(7):
                    m = e.transpose(pr[:, c // 4, (c % 4) * P:(c % 4 + 1) * P], raw[:, c * R:(c + 1) * R], g.ident[:, :])
                m.then_inc(s_pe, 1)

            @block.vector
            def _(e):
                e.wait_ge(s_pe, 1)
                e.tensor_tensor(raw[:, 0:4 * R], pc[:, 0, 0:4 * R], G[:, 0:4 * R, D], ALU.add).then_inc(s_v, 1)
                e.tensor_tensor(raw[:, 4 * R:], pc[:, 1, 0:3 * R], G[:, 4 * R:, D], ALU.add).then_inc(s_v, 1)
                e.wait_ge(s_v, 2)
                e.memset(G[:, :, D:D + 1], 1.0).then_inc(s_v, 1)

            @block.scalar
            def _(e):
                e.wait_ge(s_pe, 2)
                e.activation(back[:, 0:4, :], pr[:, 0, :].rearrange("p (c n) -> p c n", n=P), ACT.Copy).then_inc(s_a, 1)
                e.activation(back[:, 4:7, :], pr[:, 1, 0:3 * P].rearrange("p (c n) -> p c n", n=P), ACT.Copy).then_inc(s_a, 1)



def block_range(e, g, pair, turn):
    e.sem_inc(turn, 1)
    both = e.value_load(g.pair_blocks[0:1, ds(pair, 1)], min_val=0, max_val=32 * NB + NB - 1)
    return e.snap(both % 32, min_val=0, max_val=NB - 1), e.snap(both // 32, min_val=0, max_val=NB)


def pairs(eng, step):
    with eng.Fori(0, PN // SL - 1, 1) as i:
        for s in range(SL):
            step(i, s, False)
    for s in range(SL):
        step(PN // SL - 1, s, True)


def maxima(nc, g, dr, best):
    with stage_tools(nc, "amax") as t:
        s_in = [t.sem(f"inputs{s}") for s in range(SL)]
        s_free = [t.sem(f"free{s}") for s in range(SL)]
        s_z, s_v, s_turn = t.sem("start"), t.sem("steps"), t.sem("turn")
        raw_b, dstb = t.sb("raw_b", [P, SL, PS]), t.sb("dstb", [P, SL, PS], F16)
        pen, dump, top = t.sb("pen", [P, 2, PS], mybir.dt.bfloat16), t.sb("dump", [P, PS]), t.sb("top", [P, 1])
        with nc.Block() as block:
            @block.sync
            def _(e):
                for s in range(SL):
                    e.sem_inc(s_free[s], 1)

                def step(i, s, last):
                    tt = i * SL + s
                    e.wait_ge(s_free[s], i + 1)
                    e.dma_start(raw_b[:, s, :], dr["raw"][ds(tt, 1), :].partition_broadcast(P)).then_inc(s_in[s], 16)
                    e.dma_start(dstb[:, s, :], dr["dst16"][ds(tt, 1), :].partition_broadcast(P)).then_inc(s_in[s], 16)
                pairs(e, step)

            @block.vector
            def _(e):
                e.memset(best[:, :], -0.1 * BIG).then_inc(s_z, 1)
                e.memset(top[:, :], -BIG).then_inc(s_z, 1)
                e.wait_ge(s_z, 2)
                v = Count(e, "amax_v", VISITS)

                def step(i, s, last):
                    lo, hi = block_range(e, g, i * SL + s, s_turn)
                    e.wait_ge(s_in[s], i * 32 + 32)
                    e.sem_inc(s_turn, 1)
                    with e.Fori(lo, hi, 1) as b:
                        n = v.now()
                        e.tensor_scalar(pen[:, s % 2, :], dstb[:, s, :], g.node_c[:, ds(b, 1)], -BIG,
                                        ALU.not_equal, ALU.mult).then_inc(s_v, 1)
                        e.wait_ge(s_v, n * 3 + 1)
                        e.sem_inc(s_turn, 1)
                        e.tensor_tensor_reduce(dump[:, :], raw_b[:, s, :], pen[:, s % 2, :], 1.0, -BIG,
                                               ALU.add, ALU.max, top[:, :]).then_inc(s_v, 1)
                        e.wait_ge(s_v, n * 3 + 2)
                        e.tensor_tensor(best[:, ds(b, 1)], best[:, ds(b, 1)], top[:, :], ALU.max).then_inc(s_v, 1)
                        e.wait_ge(s_v, n * 3 + 3)
                        e.sem_inc(s_turn, 1)
                        v.up()
                    e.sem_inc(s_free[s], 1)
                pairs(e, step)


def weighted_sums(nc, g, dr, raw, G, best, sums):
    bf = mybir.dt.bfloat16
    SB = -(-NB * HID // 512)
    with stage_tools(nc, "weigh") as t:
        s_in = [t.sem(f"inputs{s}") for s in range(SL)]
        s_free = [t.sem(f"free{s}") for s in range(SL)]
        s_z, s_p, s_mask, s_mused, s_pm, s_w, s_wf, s_exp, s_oh, s_oused, s_sum, s_ev, s_turn = (t.sem(n) for n in (
            "zeros", "parts", "mask", "mask_used", "picked", "difference", "steps", "weights", "onehot", "onehot_used",
            "summed", "copied", "turn"))
        zero, part, rest = t.sb("zero", [1, 512], bf), t.sb("part", [P, NB, 3], bf), t.sb("rest", [P, NB])
        dstb, mask = t.sb("dstb", [P, SL, PS], F16), t.sb("mask", [P, JP, P], bf)
        me, w = t.sb("me", [P, 2, JP]), t.sb("w", [P, SL, JP])
        oh = t.sb("oh", [P, JP, P])
        pm = [t.ps(f"pm{i}", [P, JP, 4]) for i in range(2)]
        acc = t.ps("acc", [P, SB * 512])

        def after(i, s, n):
            return (i, s + n) if s + n < SL else (i + 1, s + n - SL)

        with nc.Block() as block:
            @block.sync
            def _(e):
                for s in range(SL):
                    e.sem_inc(s_free[s], 1)

                def step(i, s, last):
                    e.wait_ge(s_free[s], i + 1)
                    e.dma_start(dstb[:, s, :], dr["dst16"][ds(i * SL + s, 1), :].partition_broadcast(P)).then_inc(s_in[s], 16)
                pairs(e, step)

            @block.vector
            def _(e):
                e.memset(zero[:, :], 0.0).then_inc(s_z, 1)
                c = Chain(e, s_p)
                c(e.tensor_copy(part[:, :, 0], best[:, :]))
                c(e.tensor_tensor(rest[:, :], best[:, :], part[:, :, 0], ALU.subtract))
                c(e.tensor_copy(part[:, :, 1], rest[:, :]))
                c(e.tensor_tensor(rest[:, :], rest[:, :], part[:, :, 1], ALU.subtract))
                c(e.tensor_copy(part[:, :, 2], rest[:, :]))
                e.sem_inc(s_wf, 4)
                vm, vo = Count(e, "weigh_masks", VISITS), Count(e, "weigh_onehots", VISITS)

                def masks(i, s):
                    lo, hi = block_range(e, g, i * SL + s, s_turn)
                    e.wait_ge(s_in[s], i * 16 + 16)
                    e.sem_inc(s_turn, 1)
                    with e.Fori(lo, hi, 1) as b:
                        n = vm.now()
                        e.wait_ge(s_mused, n + 1)
                        e.tensor_scalar(mask[:, :, :], dstb[:, s, :].rearrange("p (j n) -> p j n", j=JP), g.node_c[:, ds(b, 1)],
                                        None, ALU.is_equal).then_inc(s_mask, 1)
                        vm.up()
                    e.wait_ge(s_mask, vm.now())
                    e.sem_inc(s_free[s], 1)

                def difference(i, s):
                    tt = i * SL + s
                    e.wait_ge(s_pm, tt + 1)
                    e.tensor_reduce(me[:, s % 2, :], pm[s % 2][:, :, 0:3], X, ALU.add).then_inc(s_wf, 1)
                    e.wait_ge(s_wf, tt * 2 + 5)
                    e.tensor_tensor(w[:, s, :], raw[:, ds(tt * JP, JP)], me[:, s % 2, :], ALU.subtract).then_inc(s_wf, 1)
                    e.wait_ge(s_wf, tt * 2 + 6)
                    e.tensor_scalar(w[:, s, :], w[:, s, :], 0.0, None, ALU.min).then_inc(s_w, 1)

                def step(i, s, last):
                    tt = i * SL + s
                    if not last:
                        masks(*after(i, s, 2))
                    if not last or s < SL - 1:
                        difference(*after(i, s, 1))
                    lo, hi = block_range(e, g, tt, s_turn)
                    e.wait_ge(s_exp, tt + 1)
                    e.sem_inc(s_turn, 1)
                    with e.Fori(lo, hi, 1) as b:
                        n = vo.now()
                        e.wait_ge(s_oused, n + 1)
                        for j in range(JP):
                            m = e.tensor_scalar(oh[:, j, :], g.ids[:, ds(b * P, P)], g.dst_c[:, ds(tt * JP + j, 1)],
                                                w[:, s, j:j + 1], ALU.is_equal, ALU.mult)
                        m.then_inc(s_oh, 1)
                        vo.up()
                masks(0, 0)
                masks(0, 1)
                difference(0, 0)
                pairs(e, step)

            @block.scalar
            def _(e):
                def step(i, s, last):
                    e.wait_ge(s_w, i * SL + s + 1)
                    e.activation(w[:, s, :], w[:, s, :], ACT.Exp).then_inc(s_exp, 1)
                pairs(e, step)
                e.wait_ge(s_sum, 1)
                e.activation(sums[:, :, :], acc[:, 0:NB * HID].rearrange("p (b f) -> p b f", f=HID)[:, :, 0:D + 1],
                             ACT.Copy).then_inc(s_ev, 1)
                e.wait_ge(s_ev, 1)

            @block.tensor
            def _(e):
                e.wait_ge(s_z, 1)
                e.wait_ge(s_p, 5)
                e.sem_inc(s_mused, 1)
                e.sem_inc(s_oused, 1)
                for k in range(SB):
                    e.matmul(acc[:, 512 * k:512 * k + 512], zero[0:1, 0:P], zero[0:1, :], start=True, stop=False,
                             skip_group_check=True)
                vm, vo = Count(e, "weigh_picks", VISITS), Count(e, "weigh_sums", VISITS)

                def picks(i, s):
                    tt = i * SL + s
                    lo, hi = block_range(e, g, tt, s_turn)
                    e.wait_ge(s_wf, tt * 2 + 2)
                    e.matmul(pm[s % 2][:, :, :], zero[0:1, 0:P], zero[0:1, 0:4 * JP], start=True, stop=False, skip_group_check=True)
                    with e.Fori(lo, hi, 1) as b:
                        n = vm.now()
                        e.wait_ge(s_mask, n + 1)
                        for j in range(JP):
                            m = e.matmul(pm[s % 2][:, j, 0:3], mask[:, j, :], part[:, ds(b, 1), :].rearrange("p a k -> p (a k)"),
                                         start=False, stop=False, skip_group_check=True)
                        m.then_inc(s_mused, 1)
                        vm.up()
                    e.matmul(pm[s % 2][:, 0, 3:4], zero[0:1, 0:P], zero[0:1, 0:1], start=False, stop=True,
                             skip_group_check=True).then_inc(s_pm, 1)

                def step(i, s, last):
                    tt = i * SL + s
                    if not last:
                        picks(*after(i, s, 2))
                    lo, hi = block_range(e, g, tt, s_turn)
                    with e.Fori(lo, hi, 1) as b:
                        n = vo.now()
                        e.wait_ge(s_oh, n + 1)
                        for j in range(JP):
                            m = e.matmul(acc[:, ds(b * HID, D + 1)], oh[:, j, :],
                                         G[:, ds(tt * JP + j, 1), :].rearrange("p a f -> p (a f)"), start=False, stop=False,
                                         skip_group_check=True)
                        m.then_inc(s_oused, 1)
                        vo.up()
                picks(0, 0)
                picks(0, 1)
                pairs(e, step)
                e.matmul(acc[:, 0:1], zero[0:1, 0:P], zero[0:1, 0:1], start=False, stop=True,
                         skip_group_check=True).then_inc(s_sum, 1)


H9 = 9
BW = 96


def scatter(nc, g, dr, G, sums, harmonics=None, table=None):
    width = H9 * D if harmonics is not None else D + 1
    with stage_tools(nc, "scatter1" if harmonics is not None else "scatter0") as t:
        s_oh = [t.sem(f"onehot{s}") for s in range(2)]
        s_used = [t.sem(f"used{s}") for s in range(2)]
        s_z, s_sum, s_ev, s_load, s_turn = (t.sem(n) for n in (
            "zeros", "summed", "copied", "loaded", "turn"))
        s_slot = [(g.rows_landed[1][h], t.sem(f"free{h}")) for h in range(2)]
        s_claim, s_kept = t.sem("claim"), t.sem("kept")
        oh = t.sb("oh", [P, 2, J, P])
        zero = t.sb("zero", [1, 512], F16)
        if harmonics is not None:
            prod = t.sb("prod", [P, 2, J, H9, D])
            sh = t.sb("sh", [P, EC, H9])
            slots = t.sb("slots", [P, 2, GC, D])
        acc = t.ps("acc", [P, 512])
        with nc.Block() as block:
            if harmonics is not None:
                @block.sync
                def _(e):
                    e.dma_start(sh[:, :, :], harmonics).then_inc(s_load, 16)

                @block.gpsimd
                def _(e):
                    node_gather(e, t, g, table, D, slots, G, s_slot, s_claim, s_kept)

            @block.vector
            def _(e):
                e.memset(zero[:, :], 0.0).then_inc(s_z, 1)
                if harmonics is not None:
                    e.wait_ge(s_load, 16)
                v = Count(e, f"{t.stage}_v", VISITS)
                with e.Fori(0, NB, 1) as b:
                    lo, hi = pair_range(e, g, b)
                    with e.Fori(lo, hi, 1) as u:
                        n = v.now()
                        for s in range(2):
                            e.wait_ge(s_used[s], n + 1)
                            for j in range(J):
                                m = e.tensor_scalar(oh[:, s, j, :], g.ids[:, ds(b * P, P)], g.dst_c[:, ds((u * 2 + s) * J + j, 1)], None,
                                                    ALU.is_equal)
                                if harmonics is None and j == J - 1:
                                    m.then_inc(s_oh[s], 1)
                            if harmonics is not None:
                                if s == 0:
                                    e.wait_ge(s_kept, u * 2 + 2)
                                c0 = (u * 2 + s) * J
                                e.tensor_tensor(prod[:, s, :, :, :],
                                                bcast(G[:, ds(c0, J), :].unsqueeze(2), [P, J, H9, D]),
                                                bcast(sh[:, ds(c0, J), :].unsqueeze(3), [P, J, H9, D]),
                                                ALU.mult).then_inc(s_oh[s], 1)
                        v.up()

            @block.tensor
            def _(e):
                e.wait_ge(s_z, 1)
                e.sem_inc(s_used[0], 1)
                e.sem_inc(s_used[1], 1)
                v = Count(e, f"{t.stage}_pe", VISITS)
                with e.Fori(0, NB, 1) as b:
                    lo, hi = pair_range(e, g, b)
                    e.wait_ge(s_ev, b + 1)
                    e.matmul(acc[:, 0:width], zero[0:1, 0:P], zero[0:1, 0:width], start=True, stop=False, skip_group_check=True)
                    with e.Fori(lo, hi, 1) as u:
                        n = v.now()
                        for s in range(2):
                            e.wait_ge(s_oh[s], n + 1)
                            for j in range(J):
                                if harmonics is not None:
                                    rows = prod[:, s, j, :, :].rearrange("p c f -> p (c f)")
                                else:
                                    rows = G[:, ds((u * 2 + s) * J + j, 1), :].rearrange("p a f -> p (a f)")
                                m = e.matmul(acc[:, 0:width], oh[:, s, j, :], rows, start=False, stop=False, skip_group_check=True)
                            m.then_inc(s_used[s], 1)
                        v.up()
                    e.matmul(acc[:, 0:1], zero[0:1, 0:P], zero[0:1, 0:1], start=False, stop=True,
                             skip_group_check=True).then_inc(s_sum, 1)

            @block.scalar
            def _(e):
                e.sem_inc(s_ev, 1)
                with e.Fori(0, NB, 1) as b:
                    e.wait_ge(s_sum, b + 1)
                    e.activation(sums[:, ds(b, 1), :].rearrange("p a f -> p (a f)"), acc[:, 0:width], ACT.Copy).then_inc(s_ev, 1)


def next_layer(nc, g, a, stage, table, sums=None, mixed=None):
    with stage_tools(nc, stage) as t:
        s_v, s_a, s_out = t.sem("vector"), t.sem("scalar"), t.sem("stored")
        m, v, sq = t.sb("mean", [P, NB]), t.sb("var", [P, NB]), t.sb("sq", [P, NB, D])
        den, mix = t.sb("den", [P, NB]), t.sb("mix", [P, NB, D])
        with nc.Block() as block:
            root = [0, 0]

            @block.vector
            def _(e):
                c = Chain(e, s_v)
                if sums is not None:
                    c(e.tensor_scalar(den[:, :], sums[:, :, D], 1e-8, None, ALU.add))
                    c(e.reciprocal(den[:, :], den[:, :]))
                    c(e.tensor_tensor(mix[:, :, :], sums[:, :, 0:D], bcast(den[:, :].unsqueeze(2), [P, NB, D]), ALU.mult))
                    c(e.tensor_tensor(g.x[:, :, :], g.x[:, :, :], mix[:, :, :], ALU.add))
                if mixed is not None:
                    c(e.tensor_tensor(g.x[:, :, :], g.x[:, :, :], mixed[:, :, :], ALU.add))
                root[0] = c.n + 6
                layernorm_relu(e, c, lambda: e.wait_ge(s_a, 1), (m, v, sq[:, :, :]), g.x[:, :, :], g.h[:, :, :], None)
                root[1] = c.n

            @block.scalar
            def _(e):
                e.wait_ge(s_v, root[0])
                e.activation(v[:, :], v[:, :], ACT.Sqrt).then_inc(s_a, 1)

            @block.sync
            def _(e):
                if table is not None:
                    e.wait_ge(s_v, root[1])
                    e.dma_start(table.rearrange("(b p) f -> p b f", p=P), g.h[:, :, :]).then_inc(s_out, 16)
                    e.wait_ge(s_out, 16)


def mix_products(nc, g, a, sums, mixed):
    with stage_tools(nc, "mix") as t:
        s_load, s_w, s_pe, s_a, s_out, s_v = (t.sem(n) for n in ("loaded", "weights", "turned", "copied", "mixed", "kept"))
        wrep, cg = t.sb("wrep", [BW, 3, D]), t.sb("cg", [BW, 3, D])
        turned = t.sb("turned", [BW, 2, 3, P])
        pt = [t.ps(f"pt{i}", [BW, 3 * P]) for i in range(2)]
        po = [t.ps(f"po{i}", [P, D]) for i in range(2)]
        with nc.Block() as block:
            @block.sync
            def _(e):
                e.dma_start(wrep[:, :, :], a["W1_rep"].rearrange("(q r) o -> r q o", r=BW)).then_inc(s_load, 16)
                e.dma_start(cg[:, :, :], a["cg"].rearrange("(q r) o -> r q o", r=BW)).then_inc(s_load, 16)

            @block.vector
            def _(e):
                e.wait_ge(s_load, 32)
                e.tensor_tensor(wrep[:, :, :], wrep[:, :, :], cg[:, :, :], ALU.mult).then_inc(s_w, 1)
                for b in range(NB):
                    e.wait_ge(s_out, b + 1)
                    e.tensor_copy(mixed[:, b, :], po[b % 2][:, :]).then_inc(s_v, 1)

            @block.scalar
            def _(e):
                for b in range(NB):
                    e.wait_ge(s_pe, b + 1)
                    if b >= 2:
                        e.wait_ge(s_out, b - 1)
                    e.activation(turned[:, b % 2, :, :].rearrange("p q n -> p (q n)"), pt[b % 2][:, :], ACT.Copy).then_inc(s_a, 1)

            @block.tensor
            def _(e):
                e.wait_ge(s_w, 1)

                def mix(b):
                    e.wait_ge(s_a, b + 1)
                    if b >= 2:
                        e.wait_ge(s_v, b - 1)
                    for q in range(3):
                        m = e.matmul(po[b % 2][:, :], turned[:, b % 2, q, :], wrep[:, q, :], start=(q == 0), stop=(q == 2))
                    m.then_inc(s_out, 1)
                for b in range(NB):
                    if b >= 2:
                        e.wait_ge(s_a, b - 1)
                    for q in range(3):
                        m = e.transpose(pt[b % 2][:, q * P:(q + 1) * P], sums[:, b, q * BW:(q + 1) * BW], g.ident[:, :])
                    m.then_inc(s_pe, 1)
                    if b:
                        mix(b - 1)
                mix(NB - 1)


HID = 64
LOW = 4096.0
DC = [min(512, N - c) for c in range(0, N, 512)]
TAIL = N - (NB - 1) * P


def turn_counts(nc, g, dr, CT):
    SG = [(s, min(8, NB - s)) for s in range(0, NB, 8)]
    with stage_tools(nc, "turn") as t:
        s_ld = [t.sem(f"loaded{i}") for i in range(2)]
        s_t, s_ea, s_ev, s_one, s_deg, s_id = (t.sem(n) for n in ("turned", "copied_a", "copied_v", "ones", "degree", "diagonal"))
        row = t.sb("row", [P, 2, NP], F16)
        one = t.sb("one", [P, 1], F16)
        pt = [t.ps(f"pt{i}", [P, 8, P], F16) for i in range(4)]
        pd = t.ps("pd", [P, NB])
        zero = t.sb("zero", [1, P], F16)
        with nc.Block() as block:
            @block.sync
            def _(e):
                for b in range(NB):
                    if b >= 2:
                        e.wait_ge(s_t, 4 * (b - 1))
                    e.dma_start(row[:, b % 2, :], dr["counts"][b * P:(b + 1) * P, :]).then_inc(s_ld[b % 2], 16)

            @block.tensor
            def _(e):
                e.wait_ge(s_one, 2)
                e.matmul(pd[:, :], zero[0:1, :], zero[0:1, 0:NB], start=True, stop=False, skip_group_check=True)
                for b in range(NB):
                    e.wait_ge(s_ld[b % 2], 16 * (b // 2 + 1))
                    for k, (s0, n) in enumerate(SG):
                        if b:
                            e.wait_ge(s_ea if k % 2 else s_ev, 2 * b if k >= 2 else 2 * b - 1)
                        for s in range(s0, s0 + n):
                            e.matmul(pd[:, s:s + 1], row[:, b % 2, s * P:(s + 1) * P], one[:, :], start=False,
                                     stop=(b == NB - 1), skip_group_check=True)
                        for s in range(s0, s0 + n):
                            m = e.transpose(pt[k][:, s - s0, :], row[:, b % 2, s * P:(s + 1) * P], g.ident16[:, :])
                        m.then_inc(s_t, 1)

            @block.vector
            def _(e):
                e.memset(zero[:, :], 0.0).then_inc(s_one, 1)
                e.memset(one[:, :], 1.0).then_inc(s_one, 1)
                for b in range(NB):
                    w = min(P, N - b * P)
                    for k in (0, 2):
                        s0, n = SG[k]
                        e.wait_ge(s_t, 4 * b + k + 1)
                        e.tensor_copy(CT[:, s0:s0 + n, b * P:b * P + w], pt[k][:, 0:n, 0:w]).then_inc(s_ev, 1)
                e.wait_ge(s_ev, 2 * NB)
                e.wait_ge(s_ea, 2 * NB)
                for s in range(NB):
                    w = min(P, N - s * P)
                    d = CT[:, s, s * P:s * P + w]
                    e.tensor_tensor(d, d, g.ident16[:, 0:w], ALU.add).then_inc(s_id, 1)
                e.tensor_copy(g.deg_out[:, :], pd[:, :]).then_inc(s_id, 1)
                e.tensor_scalar(g.dis[:, :], g.deg[:, :], 1.0, None, ALU.add).then_inc(s_deg, 1)
                e.wait_ge(s_deg, 2)
                e.reciprocal(g.dis[:, :], g.dis[:, :]).then_inc(s_deg, 1)
                e.wait_ge(s_id, NB + 1)

            @block.scalar
            def _(e):
                for b in range(NB):
                    w = min(P, N - b * P)
                    for k in (1, 3):
                        s0, n = SG[k]
                        e.wait_ge(s_t, 4 * b + k + 1)
                        e.activation(CT[:, s0:s0 + n, b * P:b * P + w], pt[k][:, 0:n, 0:w], ACT.Copy).then_inc(s_ea, 1)
                e.wait_ge(s_deg, 1)
                e.activation(g.dis[:, :], g.dis[:, :], ACT.Sqrt).then_inc(s_deg, 1)


def gcn(nc, g, stage, CT, z, fin, weights, outs):
    fo = sum(w.shape[1] for w in weights)
    with stage_tools(nc, stage) as t:
        s_v, s_a, s_w, s_agg, s_ev, s_y, s_yv, s_b = (t.sem(n) for n in (
            "vector", "scalar", "weights", "aggregated", "copied", "mixed", "used", "bias"))
        zs = t.sb("zs", [P, NB, fin])
        parts = t.sb("parts", [P, NB, 2 * fin], F16)
        W = t.sb("W", [2 * fin, fo])
        bias = t.sb("bias", [P, fo])
        agg = t.sb("agg", [2 * fin, 2, 512])
        pa = [t.ps(f"pa{i}", [2 * fin, 512]) for i in range(2)]
        py = [t.ps(f"py{i}", [P, 4, fo]) for i in range(2)]
        yv = t.sb("yv", [P, 2, 4, fo])
        nload = 3 * len(weights)
        with nc.Block() as block:
            @block.sync
            def _(e):
                c = 0
                for w, (b, _, _) in zip(weights, outs):
                    n = w.shape[1]
                    e.dma_start(W[0:fin, c:c + n], w).then_inc(s_w, 16)
                    e.dma_start(W[fin:2 * fin, c:c + n], w).then_inc(s_w, 16)
                    e.dma_start(bias[:, c:c + n], b.unsqueeze(0).partition_broadcast(P)).then_inc(s_w, 16)
                    c += n

            @block.vector
            def _(e):
                c = Chain(e, s_v)
                c(e.tensor_tensor(zs[:, :, :], z, bcast(g.dis[:, :].unsqueeze(2), [P, NB, fin]), ALU.mult))
                e.wait_ge(s_a, 1)
                c(e.tensor_tensor(zs[:, :, :], zs[:, :, :], parts[:, :, 0:fin], ALU.subtract))
                e.wait_ge(s_w, 16 * nload)
                c(e.tensor_scalar(W[fin:2 * fin, :], W[fin:2 * fin, :], 1.0 / LOW, None, ALU.mult))
                for _, h, add in outs:
                    if not add:
                        c(e.memset(h[:, NB - 1, :], 0.0))
                for k, n in enumerate(DC):
                    rows, nb = (P, n // P) if n >= P else (n, 1)
                    e.wait_ge(s_y, k + 1)
                    y = yv[0:rows, k % 2, 0:nb, :]
                    e.tensor_tensor(y, py[k % 2][0:rows, 0:nb, :],
                                    bcast(g.dis[0:rows, 4 * k:4 * k + nb].unsqueeze(2), [rows, nb, fo]), ALU.mult).then_inc(s_yv, 1)
                    e.wait_ge(s_yv, k + 1)
                    o = 0
                    for _, h, add in outs:
                        w = h.shape[2]
                        d = h[0:rows, 4 * k:4 * k + nb, :]
                        if add:
                            c(e.tensor_tensor(d, d, yv[0:rows, k % 2, 0:nb, o:o + w], ALU.add))
                            c(e.tensor_tensor(d, d, bcast(bias[0:rows, o:o + w].unsqueeze(1), [rows, nb, w]), ALU.add))
                        else:
                            c(e.tensor_tensor(d, yv[0:rows, k % 2, 0:nb, o:o + w],
                                              bcast(bias[0:rows, o:o + w].unsqueeze(1), [rows, nb, w]), ALU.add))
                        o += w

            @block.scalar
            def _(e):
                e.wait_ge(s_v, 1)
                e.activation(parts[:, :, 0:fin], zs[:, :, :], ACT.Copy).then_inc(s_a, 1)
                e.wait_ge(s_v, 2)
                e.activation(parts[:, :, fin:], zs[:, :, :], ACT.Copy, scale=LOW).then_inc(s_a, 1)
                for k, n in enumerate(DC):
                    e.wait_ge(s_agg, k + 1)
                    if k >= 2:
                        e.wait_ge(s_y, k - 1)
                    e.activation(agg[:, k % 2, 0:n], pa[k % 2][:, 0:n], ACT.Copy).then_inc(s_ev, 1)

            @block.tensor
            def _(e):
                e.wait_ge(s_a, 2)
                e.wait_ge(s_v, 3)

                def mix(k):
                    n = DC[k]
                    rows, nb = (P, n // P) if n >= P else (n, 1)
                    e.wait_ge(s_ev, k + 1)
                    if k >= 2:
                        e.wait_ge(s_yv, k - 1)
                    for i in range(nb):
                        m = e.matmul(py[k % 2][0:rows, i, :], agg[:, k % 2, i * P:i * P + rows], W[:, :], start=True, stop=True)
                    m.then_inc(s_y, 1)
                for k, n in enumerate(DC):
                    if k >= 2:
                        e.wait_ge(s_ev, k - 1)
                    for s in range(NB):
                        m = e.matmul(pa[k % 2][:, 0:n], parts[:, s, :], CT[:, s, 512 * k:512 * k + n],
                                     start=(s == 0), stop=(s == NB - 1))
                    m.then_inc(s_agg, 1)
                    if k:
                        mix(k - 1)
                mix(len(DC) - 1)


def batchnorm(nc, g, stage, h, w, gamma, beta, into, add):
    with stage_tools(nc, stage) as t:
        s_v, s_a, s_pe, s_ld = t.sem("vector"), t.sem("scalar"), t.sem("tensor"), t.sem("loaded")
        part, part2 = t.sb("part", [P, w]), t.sb("part2", [P, w])
        mean, var = t.sb("mean", [P, w]), t.sb("var", [P, w])
        ga, be = t.sb("gamma", [P, w]), t.sb("beta", [P, w])
        sq = t.sb("sq", [P, NB, w])
        pm, pv = t.ps("pm", [P, w]), t.ps("pv", [P, w])
        with nc.Block() as block:
            @block.sync
            def _(e):
                e.dma_start(ga[:, :], gamma.unsqueeze(0).partition_broadcast(P)).then_inc(s_ld, 16)
                e.dma_start(be[:, :], beta.unsqueeze(0).partition_broadcast(P)).then_inc(s_ld, 16)

            @block.vector
            def _(e):
                c = Chain(e, s_v)
                full = lambda v: bcast(v[:, :].unsqueeze(1), [P, NB, w])
                c(e.tensor_reduce(part[:, :], h.rearrange("p b f -> p f b"), X, ALU.add))
                e.wait_ge(s_pe, 1)
                c(e.tensor_scalar(mean[:, :], pm[:, :], 1.0 / N, None, ALU.mult))
                c(e.tensor_tensor(h, h, full(mean), ALU.subtract))
                c(e.tensor_tensor(sq[:, :, :], h, h, ALU.mult))
                c(e.tensor_reduce(part2[:, :], sq[:, 0:NB - 1, :].rearrange("p b f -> p f b"), X, ALU.add))
                e.wait_ge(s_pe, 2)
                c(e.tensor_scalar(var[:, :], pv[:, :], 1.0 / N, EPS, ALU.mult, ALU.add))
                e.wait_ge(s_a, 1)
                e.wait_ge(s_ld, 32)
                c(e.reciprocal(var[:, :], var[:, :]))
                c(e.tensor_tensor(var[:, :], var[:, :], ga[:, :], ALU.mult))
                c(e.tensor_tensor(h, h, full(var), ALU.mult))
                c(e.tensor_tensor(h, h, full(be), ALU.add))
                c(e.scalar_tensor_tensor(into, h, 0.0, add, ALU.max, ALU.add))

            @block.scalar
            def _(e):
                e.wait_ge(s_v, 6)
                e.activation(var[:, :], var[:, :], ACT.Sqrt).then_inc(s_a, 1)

            @block.tensor
            def _(e):
                e.wait_ge(s_v, 1)
                e.matmul(pm[:, :], g.ones[:, :], part[:, :], start=True, stop=True).then_inc(s_pe, 1)
                e.wait_ge(s_v, 5)
                e.matmul(pv[:, :], g.ones[:, :], part2[:, :], start=True, stop=False)
                e.matmul(pv[:, :], g.ones[0:TAIL, :], sq[0:TAIL, NB - 1, :], start=False, stop=True).then_inc(s_pe, 1)


def linear(nc, g, stage, z, fin, w, b, res):
    fo = w.shape[1]
    nload = 16 if b is None else 32
    with stage_tools(nc, stage) as t:
        s_ld, s_t, s_a, s_y, s_v = (t.sem(n) for n in ("loaded", "turned", "copied", "mixed", "vector"))
        W, bias = t.sb("W", [fin, fo]), t.sb("bias", [P, fo])
        zt = t.sb("zt", [fin, 2, P])
        pt = [t.ps(f"pt{i}", [fin, P]) for i in range(2)]
        py = [t.ps(f"py{i}", [P, fo]) for i in range(2)]
        with nc.Block() as block:
            @block.sync
            def _(e):
                e.dma_start(W[:, :], w).then_inc(s_ld, 16)
                if b is not None:
                    e.dma_start(bias[:, :], b.unsqueeze(0).partition_broadcast(P)).then_inc(s_ld, 16)

            @block.tensor
            def _(e):
                e.wait_ge(s_ld, nload)

                def mix(k):
                    e.wait_ge(s_a, k + 1)
                    if k >= 2:
                        e.wait_ge(s_v, k - 1)
                    e.matmul(py[k % 2][:, :], zt[:, k % 2, :], W[:, :], start=True, stop=True).then_inc(s_y, 1)
                for k in range(NB):
                    if k >= 2:
                        e.wait_ge(s_a, k - 1)
                    e.transpose(pt[k % 2][:, :], z[:, k, :], g.ident[:, :]).then_inc(s_t, 1)
                    if k:
                        mix(k - 1)
                mix(NB - 1)

            @block.scalar
            def _(e):
                for k in range(NB):
                    e.wait_ge(s_t, k + 1)
                    if k >= 2:
                        e.wait_ge(s_y, k - 1)
                    e.activation(zt[:, k % 2, :], pt[k % 2][:, :], ACT.Copy).then_inc(s_a, 1)

            @block.vector
            def _(e):
                e.wait_ge(s_ld, nload)
                for k in range(NB):
                    e.wait_ge(s_y, k + 1)
                    if b is None:
                        e.tensor_copy(res[:, k, :], py[k % 2][:, :]).then_inc(s_v, 1)
                    else:
                        e.tensor_tensor(res[:, k, :], py[k % 2][:, :], bias[:, :], ALU.add).then_inc(s_v, 1)


def residual_gcn(nc, g, a, dr):
    with stage_tools(nc, "l2") as t:
        CT = t.sb("CT", [P, NB, N], F16)
        turn_counts(nc, g, dr, CT)
        A, B, M = t.sb("A", [P, NB, HID]), t.sb("B", [P, NB, HID]), t.sb("M", [P, NB, HID])
        Av, Bv, Mv = A[:, :, :], B[:, :, :], M[:, :, :]
        W, gm, bt = a["W_hid"], a["gamma_hid"], a["beta_hid"]
        bh = a["b_hid"]
        h = g.h[:, :, :]
        linear(nc, g, "enc1_res", h, D, a["Wres_enc1"], a["bres_enc1"], Bv)
        gcn(nc, g, "enc1", CT, h, D, [a["W_enc1"]], [(a["b_enc1"], Av, False)])
        batchnorm(nc, g, "enc1_bn", Av, HID, gm[0], bt[0], Bv, Bv)
        gcn(nc, g, "enc2", CT, Bv, HID, [W[0], W[2]], [(bh[0], Av, False), (bh[2], Mv, False)])
        batchnorm(nc, g, "enc2_bn", Av, HID, gm[1], bt[1], Bv, Bv)
        gcn(nc, g, "enc3", CT, Bv, HID, [W[1], W[3]], [(bh[1], Av, False), (bh[3], Mv, True)])
        batchnorm(nc, g, "enc3_bn", Av, HID, gm[2], bt[2], Bv, Bv)
        gcn(nc, g, "mid", CT, Bv, HID, [W[4]], [(bh[4], Mv, True)])
        gcn(nc, g, "dec1", CT, Mv, HID, [W[5]], [(bh[5], Av, False)])
        batchnorm(nc, g, "dec1_bn", Av, HID, gm[3], bt[3], Mv, Mv)
        linear(nc, g, "dec2_res", Mv, HID, a["Wres_dec2"], a["bres_dec2"], B[:, :, 0:D])
        gcn(nc, g, "dec2", CT, Mv, HID, [a["W_dec2"]], [(a["b_dec2"], A[:, :, 0:D], False)])
        batchnorm(nc, g, "dec2_bn", A[:, :, 0:D], D, a["gamma_out"][0], a["beta_out"][0], B[:, :, 0:D], B[:, :, 0:D])
        gcn(nc, g, "dec3", CT, B[:, :, 0:D], D, [a["W_dec3"]], [(a["b_dec3"], A[:, :, 0:D], False)])
        batchnorm(nc, g, "dec3_bn", A[:, :, 0:D], D, a["gamma_out"][1], a["beta_out"][1], A[:, :, HID - D:], B[:, :, 0:D])
        next_layer(nc, g, a, "layer3", dr["table1"], mixed=A[:, :, HID - D:])


ED = 16
FH = 2 * HID


def edge_flows(nc, g, a, dr, sums):
    bf = mybir.dt.bfloat16
    with stage_tools(nc, "flow") as t:
        s_in = [t.sem(f"inputs{s}") for s in range(SL)]
        s_pre = [t.sem(f"added{s}") for s in range(SL)]
        s_ph, s_mask, s_mused, s_oh, s_oused, s_act, s_lo = (t.sem(n) for n in (
            "parts", "mask", "mask_used", "onehot", "onehot_used", "relu", "low"))
        s_hfree, s_st, s_stf, s_idx, s_claim, s_z, s_sum, s_ev, s_ld = (t.sem(n) for n in (
            "hidden_used", "stored", "place", "idx", "claim", "zeros", "summed", "copied", "weights"))
        s_turn = t.sem("turn")
        idx = t.sb("idx", [P, SL, JP], I32)
        rows = t.sb("rows", [P, SL, JP, FH])
        dstb, xin = t.sb("dstb", [P, SL, PS], F16), t.sb("xin", [P, SL, JP, P])
        W, zero = t.sb("W", [P, FH]), t.sb("zero", [1, 512], bf)
        mask, oh = t.sb("mask", [P, JP, P], bf), t.sb("oh", [P, JP, P])
        pre, hid, r2 = t.sb("pre", [P, 2, JP, FH]), t.sb("hid", [P, 2, JP, HID]), t.sb("r2", [P, 2, JP, HID])
        hl = t.sb("hl", [P, 2, JP, FH], F16)
        ph = [t.ps(f"ph{i}", [P, JP, FH]) for i in range(2)]
        SB = -(-NB * HID // 512)
        acc = t.ps("acc", [P, SB * 512])
        with nc.Block() as block:
            @block.gpsimd
            def _(e):
                def step(i, s, last):
                    e.wait_ge(s_pre[s], i + 1)
                    e.sem_inc(s_claim, 1)
                    e.tensor_copy(idx[:, s, :], g.src_i[:, ds((i * SL + s) * JP, JP)]).then_inc(s_idx, 1)
                    e.wait_ge(s_idx, i * SL + s + 1)
                    e.sem_inc(s_claim, 1)
                    for j in range(JP):
                        e.indirect_dma_start(rows[:, s, j, :], None, dr["table3"],
                                             bass.IndirectOffsetOnAxis(ap=idx[:, s, j:j + 1].bitcast(U32), axis=0)
                                             ).then_inc(g.rows_landed[2][s], 16)
                pairs(e, step)

            @block.sync
            def _(e):
                e.wait_ge(s_z, 3)
                e.dma_start(W[0:ED, :], a["Wf1_edge"]).then_inc(s_ld, 16)

                def load(tt, s):
                    e.dma_start(dstb[:, s, :], dr["dst16"][ds(tt, 1), :].partition_broadcast(P)).then_inc(s_in[s], 16)
                    e.dma_start(xin[0:ED, s, :, :], a["edge_attr_16"][ds(tt, 1), :, :, :]
                                .rearrange("a k j p -> (a k) j p")).then_inc(s_in[s], 16)

                def store(tt, s):
                    e.wait_ge(s_lo, tt + 3)
                    e.dma_start(dr["hidden"][ds(tt, 1), :, :].rearrange("a p n -> (a p) n"),
                                hl[:, s % 2, :, :].rearrange("p j f -> p (j f)")).then_inc(s_st, 16)

                def stored(tt):
                    e.wait_ge(s_st, 16 * (tt + 1))
                    e.sem_inc(s_stf, 1)
                e.sem_inc(s_stf, 2)
                for s in range(SL):
                    load(s, s)
                with e.Fori(0, PN // SL - 1, 1) as i:
                    for s in range(SL):
                        store(i * SL + s, s)
                        load((i + 1) * SL + s, s)
                        stored(i * SL + s)
                for s in range(SL):
                    store(PN - SL + s, s)
                    stored(PN - SL + s)

            @block.vector
            def _(e):
                e.memset(zero[:, :], 0.0).then_inc(s_z, 1)
                e.memset(xin[:, :, :, :], 0.0).then_inc(s_z, 1)
                e.memset(W[:, :], 0.0).then_inc(s_z, 1)
                for s in range(SL):
                    e.sem_inc(s_pre[s], 1)
                e.sem_inc(s_lo, 2)
                vm, vo = Count(e, "flow_masks", VISITS), Count(e, "flow_onehots", VISITS)

                def masks(i, s):
                    e.wait_ge(s_in[s], i * 32 + 32)
                    lo, hi = block_range(e, g, i * SL + s, s_turn)
                    with e.Fori(lo, hi, 1) as b:
                        n = vm.now()
                        e.wait_ge(s_mused, n + 1)
                        e.tensor_scalar(mask[:, :, :], dstb[:, s, :].rearrange("p (j n) -> p j n", j=JP), g.node_c[:, ds(b, 1)],
                                        None, ALU.is_equal).then_inc(s_mask, 1)
                        vm.up()

                def step(i, s, last):
                    tt = i * SL + s
                    if not last or s < SL - 1:
                        masks(*((i, s + 1) if s < SL - 1 else (i + 1, 0)))
                    e.wait_ge(s_ph, tt + 1)
                    e.wait_ge(g.rows_landed[2][s], 16 * JP * (i + 1))
                    e.wait_ge(s_act, tt * 3 + 3)
                    e.tensor_tensor(pre[:, s % 2, :, :], ph[s % 2][:, :, :], rows[:, s, :, :], ALU.add).then_inc(s_pre[s], 1)
                    lo, hi = block_range(e, g, tt, s_turn)
                    with e.Fori(lo, hi, 1) as b:
                        n = vo.now()
                        e.wait_ge(s_oused, n + 1)
                        for j in range(JP):
                            m = e.tensor_scalar(oh[:, j, :], g.ids[:, ds(b * P, P)], g.dst_c[:, ds(tt * JP + j, 1)],
                                                None, ALU.is_equal)
                        m.then_inc(s_oh, 1)
                        vo.up()
                    e.wait_ge(s_act, tt * 3 + 9)
                    e.scalar_tensor_tensor(hl[:, s % 2, :, HID:], hl[:, s % 2, :, 0:HID], -LOW, r2[:, s % 2, :, :],
                                           ALU.mult, ALU.add).then_inc(s_lo, 1)
                masks(0, 0)
                pairs(e, step)

            @block.scalar
            def _(e):
                e.sem_inc(s_act, 6)

                def step(i, s, last):
                    tt = i * SL + s
                    e.wait_ge(s_stf, tt + 1)
                    e.wait_ge(s_lo, tt + 1)
                    e.wait_ge(s_hfree, tt + 1)
                    e.wait_ge(s_pre[s], i + 2)
                    e.activation(hl[:, s % 2, :, 0:HID], pre[:, s % 2, :, HID:], ACT.Relu).then_inc(s_act, 1)
                    e.activation(r2[:, s % 2, :, :], pre[:, s % 2, :, HID:], ACT.Relu, scale=LOW).then_inc(s_act, 1)
                    e.activation(hid[:, s % 2, :, :], pre[:, s % 2, :, 0:HID], ACT.Relu).then_inc(s_act, 1)
                pairs(e, step)
                e.wait_ge(s_sum, 1)
                e.activation(sums[:, :, :], acc[:, 0:NB * HID].rearrange("p (b f) -> p b f", f=HID), ACT.Copy).then_inc(s_ev, 1)
                e.wait_ge(s_ev, 1)

            @block.tensor
            def _(e):
                e.wait_ge(s_z, 3)
                e.wait_ge(s_ld, 16)
                e.sem_inc(s_mused, 1)
                e.sem_inc(s_oused, 1)
                e.sem_inc(s_hfree, 2)
                for k in range(SB):
                    e.matmul(acc[:, 512 * k:512 * k + 512], zero[0:1, 0:P], zero[0:1, :], start=True, stop=False,
                             skip_group_check=True)
                vm, vo = Count(e, "flow_picks", VISITS), Count(e, "flow_sums", VISITS)

                def parts(i, s):
                    e.wait_ge(s_in[s], i * 32 + 32)
                    e.wait_ge(s_pre[s], i + 1)
                    for k in range(2):
                        e.matmul(ph[s % 2][:, k * J:(k + 1) * J, :], zero[0:1, 0:P], zero[0:1, :], start=True, stop=False,
                                 skip_group_check=True)
                    for j in range(JP):
                        e.matmul(ph[s % 2][:, j, :], xin[:, s, j, :], W[:, :], start=False, stop=False, skip_group_check=True)
                    lo, hi = block_range(e, g, i * SL + s, s_turn)
                    with e.Fori(lo, hi, 1) as b:
                        n = vm.now()
                        e.wait_ge(s_mask, n + 1)
                        for j in range(JP):
                            for k in range(3):
                                m = e.matmul(ph[s % 2][:, j, :], mask[:, j, :],
                                             g.pd3[:, ds(b, 1), k, :].rearrange("p a f -> p (a f)"),
                                             start=False, stop=False, skip_group_check=True)
                        m.then_inc(s_mused, 1)
                        vm.up()
                    e.matmul(ph[s % 2][:, JP - 1, 0:1], zero[0:1, 0:P], zero[0:1, 0:1], start=False, stop=True,
                             skip_group_check=True).then_inc(s_ph, 1)

                def step(i, s, last):
                    tt = i * SL + s
                    if not last or s < SL - 1:
                        parts(*((i, s + 1) if s < SL - 1 else (i + 1, 0)))
                    e.wait_ge(s_act, tt * 3 + 9)
                    lo, hi = block_range(e, g, tt, s_turn)
                    with e.Fori(lo, hi, 1) as b:
                        n = vo.now()
                        e.wait_ge(s_oh, n + 1)
                        for j in range(JP):
                            m = e.matmul(acc[:, ds(b * HID, HID)], oh[:, j, :], hid[:, s % 2, j, :], start=False, stop=False,
                                         skip_group_check=True)
                        m.then_inc(s_oused, 1)
                        vo.up()
                    e.wait_ge(s_oused, vo.now() + 1)
                    e.sem_inc(s_hfree, 1)
                parts(0, 0)
                pairs(e, step)
                e.matmul(acc[:, 0:1], zero[0:1, 0:P], zero[0:1, 0:1], start=False, stop=True,
                         skip_group_check=True).then_inc(s_sum, 1)


def backward_sums(nc, g, a, dr, back):
    with stage_tools(nc, "back") as t:
        s_ld = [t.sem(f"loaded{i}") for i in range(SL)]
        s_free = [t.sem(f"free{i}") for i in range(SL)]
        s_oh, s_used, s_z, s_sum, s_ev = (t.sem(n) for n in ("onehot", "used", "zeros", "summed", "copied"))
        hl = t.sb("hl", [P, SL, JP * FH], F16)
        ohs = t.sb("ohs", [P, J, NP], F16)
        zero = t.sb("zero", [1, 512], F16)
        acc = t.ps("acc", [P, CB, 512])
        with nc.Block() as block:
            @block.sync
            def _(e):
                def step(i, s, last):
                    e.wait_ge(s_free[s], i + 1)
                    e.dma_start(hl[:, s, :], dr["hidden"][ds(i * SL + s, 1), :, :].rearrange("a p n -> (a p) n")).then_inc(s_ld[s], 16)
                pairs(e, step)

            @block.vector
            def _(e):
                e.memset(zero[:, :], 0.0).then_inc(s_z, 1)

                def step(i, s, last):
                    for j in range(JP):
                        c = (i * SL + s) * JP + j
                        e.wait_ge(s_used, c + 1)
                        e.tensor_scalar(ohs[:, j % J, 0:N + 1], g.ids16[:, 0:N + 1], g.src_f[:, ds(c, 1)], None,
                                        ALU.is_equal).then_inc(s_oh, 1)
                pairs(e, step)
                e.memset(back[:, N:NP], 0.0).then_inc(s_z, 1)

            @block.tensor
            def _(e):
                e.wait_ge(s_z, 1)
                for s in range(SL):
                    e.sem_inc(s_free[s], 1)
                e.sem_inc(s_used, J)
                for k, w in enumerate(DC):
                    e.matmul(acc[:, k, 0:w], zero[0:1, 0:P], zero[0:1, 0:w], start=True, stop=False, skip_group_check=True)

                def step(i, s, last):
                    e.wait_ge(s_ld[s], 16 * i + 16)
                    for j in range(JP):
                        c = (i * SL + s) * JP + j
                        e.wait_ge(s_oh, c + 1)
                        for k, w in enumerate(DC):
                            m = e.matmul(acc[:, k, 0:w], hl[:, s, j * FH:(j + 1) * FH], ohs[:, j % J, 512 * k:512 * k + w],
                                         start=False, stop=False, skip_group_check=True)
                        m.then_inc(s_used, 1)
                    e.wait_ge(s_used, (i * SL + s) * JP + JP + J)
                    e.sem_inc(s_free[s], 1)
                pairs(e, step)
                e.matmul(acc[:, CB - 1, 0:1], zero[0:1, 0:P], zero[0:1, 0:1], start=False, stop=True,
                         skip_group_check=True).then_inc(s_sum, 1)

            @block.scalar
            def _(e):
                e.wait_ge(s_sum, 1)
                for k, w in enumerate(DC):
                    e.activation(back[:, 512 * k:512 * k + w], acc[:, k, 0:w], ACT.Copy).then_inc(s_ev, 1)
                e.wait_ge(s_ev, CB)


def node_flows(nc, g, a, fwd, back, res):
    with stage_tools(nc, "node_flow") as t:
        s_ld, s_t, s_a, s_y, s_v, s_w = (t.sem(n) for n in ("loaded", "turned", "copied", "mixed", "vector", "weights"))
        W, bias = t.sb("W", [FH, HID]), t.sb("bias", [P, HID])
        deg = t.sb("deg", [P, NB])
        zt = t.sb("zt", [HID, 2, P])
        pt = [t.ps(f"pt{i}", [HID, P]) for i in range(2)]
        py = [t.ps(f"py{i}", [P, HID]) for i in range(2)]
        with nc.Block() as block:
            @block.sync
            def _(e):
                e.dma_start(W[0:HID, :], a["Wf2"]).then_inc(s_ld, 16)
                e.dma_start(W[HID:, :], a["Wf2"]).then_inc(s_ld, 16)
                e.dma_start(bias[:, :], a["bf2"].unsqueeze(0).partition_broadcast(P)).then_inc(s_ld, 16)

            @block.vector
            def _(e):
                e.wait_ge(s_ld, 48)
                e.tensor_scalar(W[HID:, :], W[HID:, :], 1.0 / LOW, None, ALU.mult).then_inc(s_w, 1)
                e.tensor_tensor(deg[:, :], g.deg[:, :], g.deg_out[:, :], ALU.add).then_inc(s_w, 1)
                e.wait_ge(s_w, 2)
                for k in range(NB):
                    e.wait_ge(s_y, k + 1)
                    e.scalar_tensor_tensor(res[:, k, :], bias[:, :], deg[:, k:k + 1], py[k % 2][:, :], ALU.mult, ALU.add).then_inc(s_v, 1)

            @block.tensor
            def _(e):
                e.wait_ge(s_w, 1)

                def mix(k):
                    e.wait_ge(s_a, k + 1)
                    if k >= 2:
                        e.wait_ge(s_v, k - 1)
                    e.matmul(py[k % 2][:, :], zt[:, k % 2, :], W[0:HID, :], start=True, stop=False)
                    e.matmul(py[k % 2][:, :], back[:, k * P:(k + 1) * P], W[:, :], start=False, stop=True).then_inc(s_y, 1)
                for k in range(NB):
                    if k >= 2:
                        e.wait_ge(s_a, k - 1)
                    e.transpose(pt[k % 2][:, :], fwd[:, k, :], g.ident[:, :]).then_inc(s_t, 1)
                    if k:
                        mix(k - 1)
                mix(NB - 1)

            @block.scalar
            def _(e):
                for k in range(NB):
                    e.wait_ge(s_t, k + 1)
                    if k >= 2:
                        e.wait_ge(s_y, k - 1)
                    e.activation(zt[:, k % 2, :], pt[k % 2][:, :], ACT.Copy).then_inc(s_a, 1)


def pointwise(nc, stage, ins):
    with stage_tools(nc, stage) as t:
        s_v = t.sem("vector")
        with nc.Block() as block:
            @block.vector
            def _(e):
                ins(e).then_inc(s_v, 1)
                e.wait_ge(s_v, 1)


def flow_layer(nc, g, a, dr):
    bf = mybir.dt.bfloat16
    with stage_tools(nc, "l3") as t:
        s_ld, s_v, s_ids, s_st = t.sem("loaded"), t.sem("vector"), t.sem("ids"), t.sem("stored")
        g.src_i, g.dst_c, g.src_f = t.sb("src_i", [P, EC], I32), t.sb("dst_c", [P, EC]), t.sb("src_f", [P, EC])
        g.ids, g.ids16, g.pd3 = t.sb("ids", [P, NP]), t.sb("ids16", [P, NP], F16), t.sb("pd3", [P, NB, 3, FH], bf)
        sums, res = t.sb("sums", [P, NB, HID]), t.sb("res", [P, NB, HID])
        with ExitStack() as c1:
            t1 = Tools(nc, c1, "l3a")
            PD, src_part, pad = t1.sb("PD", [P, NB, FH]), t1.sb("src_part", [P, NB, FH]), t1.sb("pad", [P, EC])
            dst_i = t1.sb("dst_i", [P, EC], I32)
            linear(nc, g, "flow_src", g.h[:, :, :], D, a["Wf1_src"], None, src_part)
            linear(nc, g, "flow_dst", g.h[:, :, :], D, a["Wf1_dst"], a["bf1_twice"], PD)
            with nc.Block() as block:
                @block.sync
                def _(e):
                    e.dma_start(g.src_i[:, :], a["src"]).then_inc(s_ld, 16)
                    e.dma_start(dst_i[:, :], a["dst"]).then_inc(s_ld, 16)
                    e.dma_start(dr["table3"].rearrange("(b p) f -> p b f", p=P), src_part[:, :, :]).then_inc(s_st, 16)
                    e.wait_ge(s_st, 16)

                @block.gpsimd
                def _(e):
                    e.iota(g.ids[:, :], [[1, NP]], base=-HALF, channel_multiplier=0,
                           allow_small_or_imprecise_dtypes=True).then_inc(s_ids, 1)

                @block.vector
                def _(e):
                    c = Chain(e, s_v)
                    e.wait_ge(s_ld, 32)
                    c(e.tensor_copy(g.dst_c[:, :], dst_i[:, :]))
                    c(e.tensor_scalar(g.dst_c[:, :], g.dst_c[:, :], -float(HALF), None, ALU.add))
                    c(e.tensor_copy(g.src_f[:, :], g.src_i[:, :]))
                    c(e.tensor_scalar(g.src_f[:, :], g.src_f[:, :], -float(HALF), None, ALU.add))
                    e.wait_ge(s_ids, 1)
                    c(e.tensor_copy(g.ids16[:, :], g.ids[:, :]))
                    c(e.tensor_scalar(pad[:, :], g.dst_c[:, :], float(HALF), 2.0 * NP, ALU.is_ge, ALU.mult))
                    c(e.tensor_tensor(g.src_f[:, :], g.src_f[:, :], pad[:, :], ALU.add))
                    c(e.tensor_copy(g.pd3[:, :, 0, :], PD[:, :, :]))
                    c(e.tensor_tensor(PD[:, :, :], PD[:, :, :], g.pd3[:, :, 0, :], ALU.subtract))
                    c(e.tensor_copy(g.pd3[:, :, 1, :], PD[:, :, :]))
                    c(e.tensor_tensor(PD[:, :, :], PD[:, :, :], g.pd3[:, :, 1, :], ALU.subtract))
                    c(e.tensor_copy(g.pd3[:, :, 2, :], PD[:, :, :]))
        edge_flows(nc, g, a, dr, sums)
        with ExitStack() as c2:
            back = Tools(nc, c2, "l3b").sb("back", [P, NP])
            backward_sums(nc, g, a, dr, back)
            node_flows(nc, g, a, sums, back, res)
        linear(nc, g, "node1", res[:, :, :], HID, a["Wn1"], a["bn1"], sums)
        pointwise(nc, "node_relu", lambda e: e.tensor_scalar(sums[:, :, :], sums[:, :, :], 0.0, None, ALU.max))
        linear(nc, g, "node2", sums[:, :, :], HID, a["Wn2"], a["bn2"], res[:, :, 0:D])
        pointwise(nc, "last_add", lambda e: e.tensor_tensor(g.x[:, :, :], g.x[:, :, :], res[:, :, 0:D], ALU.add))


def cg_tables():
    import math
    combos = [(0, 0, 0), (0, 1, 1), (1, 0, 1), (1, 1, 0), (1, 1, 1), (2, 1, 1)]

    def coeff(j1, m1, j2, m2, j3, m3):
        if m3 != m1 + m2:
            return 0.0
        f = math.factorial
        pref = (2 * j3 + 1) * f(j3 + j1 - j2) * f(j3 - j1 + j2) * f(j1 + j2 - j3) / f(j1 + j2 + j3 + 1)
        pref *= f(j3 + m3) * f(j3 - m3) * f(j1 - m1) * f(j1 + m1) * f(j2 - m2) * f(j2 + m2)
        s = 0.0
        for v in range(max(0, j2 - j3 - m1, j1 + m2 - j3), min(j1 + j2 - j3, j1 - m1, j2 + m2) + 1):
            s += (-1) ** v / (f(v) * f(j1 + j2 - j3 - v) * f(j1 - m1 - v) * f(j2 + m2 - v) * f(j3 - j2 + m1 + v) * f(j3 - j1 - m2 + v))
        return math.sqrt(pref) * s

    def qmat(l):
        q = np.zeros((2 * l + 1, 2 * l + 1), dtype=np.complex128)
        for m in range(-l, 0):
            q[l + m, l + abs(m)] = 1 / np.sqrt(2)
            q[l + m, l - abs(m)] = -1j / np.sqrt(2)
        q[l, l] = 1.0
        for m in range(1, l + 1):
            q[l + m, l + abs(m)] = (-1) ** m / np.sqrt(2)
            q[l + m, l - abs(m)] = 1j * (-1) ** m / np.sqrt(2)
        return (-1j) ** l * q

    M = 8
    cg = np.zeros((H9 * D, D), np.float32)
    which = np.zeros((H9 * D, D, 3), np.int64)
    first = {0: 0, 1: 1, 2: 4}
    for idx, (le, ln, lo) in enumerate(combos):
        C = np.zeros((2 * le + 1, 2 * ln + 1, 2 * lo + 1), dtype=np.complex128)
        for m1 in range(-le, le + 1):
            for m2 in range(-ln, ln + 1):
                if -lo <= m1 + m2 <= lo:
                    C[m1 + le, m2 + ln, m1 + m2 + lo] = coeff(le, m1, ln, m2, lo, m1 + m2)
        C = np.einsum('ij,kl,mn,ikn->jlm', qmat(le), qmat(ln), np.conj(qmat(lo)).T, C).real
        C = (C / np.linalg.norm(C)).astype(np.float32)
        for i in range(2 * le + 1):
            for m in range(M):
                for j in range(2 * ln + 1):
                    for o in range(M):
                        for k in range(2 * lo + 1):
                            r = (first[le] + i) * D + (m if ln == 0 else M + 3 * m + j)
                            q = o if lo == 0 else M + 3 * o + k
                            cg[r, q] = C[i, j, k]
                            which[r, q] = (idx, m, o)
    return cg, which


def program(nc, a, out, upto):
    dr = {n: nc.dram_tensor(n, s, d).ap() for n, s, d in [
        ("table0", (NP, AW), F32), ("table1", (NP, D), F32), ("edge_logit", (T, TS), F32), ("raw", (PN, PS), F32),
        ("counts", (NP, NP), F16),
        ("hidden", (PN, P, JP * FH), F16), ("table3", (NP, FH), F32), ("dst16", (PN, PS), F16),
        ("pair_blocks", (PN, 1), I32)]}
    with ExitStack() as ctx:
        t = Tools(nc, ctx, "keep")

        class Kept:
            pass
        g = Kept()
        g.rows_landed = [[t.sem(f"rows_landed{k}{h}") for h in range(2)] for k in range(3)]
        g.bounds = t.sb("bounds", [1, 2 * NB], I32)
        g.pair_blocks = t.sb("pair_blocks", [1, PN], I32)
        g.node_c = t.sb("node_c", [P, NB])
        g.pcol, g.node_id, g.iota = t.sb("pcol", [P, 1]), t.sb("node_id", [P, NB]), t.sb("iota", [P, P])
        g.block_first = t.sb("block_first", [P, NB + 1])
        g.ident, g.ident16 = t.sb("ident", [P, P]), t.sb("ident16", [P, P], F16)
        g.x, g.h, g.deg = t.sb("x", [P, NB, D]), t.sb("h", [P, NB, D]), t.sb("deg", [P, NB])
        g.deg_out, g.dis, g.ones = t.sb("deg_out", [P, NB]), t.sb("dis", [P, NB]), t.sb("ones", [P, P])
        g.t0_done = g.t0_exp = g.t0_abs = 0
        edges = ExitStack()
        te = Tools(nc, edges, "edges")
        g.src_i, g.dst_c, g.src_f = te.sb("src_i", [P, EC], I32), te.sb("dst_c", [P, EC]), te.sb("src_f", [P, EC])
        g.ids = te.sb("ids", [P, NP])
        with ExitStack() as early:
            g.ids16 = Tools(nc, early, "early").sb("ids16", [P, NP], F16)
            setup(nc, g, a, dr)
            table0(nc, g, a, dr)
            edge_logits(nc, g, a, dr)
            with ExitStack() as l0:
                G = Tools(nc, l0, "l0").sb("G", [P, EC, D + 1])
                if upto >= 1:
                    count_and_gather(nc, g, a, dr, G)
                if upto >= 2:
                    raw, best = (Tools(nc, l0, "l0").sb(n, [P, w]) for n, w in (("raw", EC), ("best", NB)))
                    raw_logits(nc, g, a, dr, G, raw)
                    maxima(nc, g, dr, best)
                if upto >= 3:
                    sums = Tools(nc, l0, "l0b").sb("sums", [P, NB, D + 1])
                    weighted_sums(nc, g, dr, raw, G, best, sums)
                    next_layer(nc, g, a, "layer1", dr["table1"], sums=sums)
        if upto >= 4:
            with ExitStack() as l1:
                t1 = Tools(nc, l1, "l1")
                sums = t1.sb("sums", [P, NB, H9 * D])
                mixed = t1.sb("mixed", [P, NB, D])
                G = t1.sb("G", [P, EC, D])
                scatter(nc, g, dr, G, sums, a["harmonics"], dr["table1"])
                mix_products(nc, g, a, sums, mixed)
                next_layer(nc, g, a, "layer2", None, mixed=mixed)
        edges.close()
        if upto >= 5:
            residual_gcn(nc, g, a, dr)
        if upto >= 6:
            flow_layer(nc, g, a, dr)
        with ExitStack() as fin:
            s_out = Tools(nc, fin, "fin").sem("stored")
            with nc.Block() as block:
                @block.sync
                def _(e):
                    full = N // P
                    e.dma_start(out[0:full * P, :].rearrange("(b p) f -> p b f", p=P), g.x[:, 0:full, :]).then_inc(s_out, 16)
                    e.dma_start(out[full * P:N, :], g.x[0:N - full * P, full, :]).then_inc(s_out, 16)
                    e.wait_ge(s_out, 32)


def layouts(inp):
    def rows(v, n, fill=0):
        return np.concatenate([v, np.full((n - v.shape[0],) + v.shape[1:], fill, v.dtype)])

    def columns(v):
        return np.ascontiguousarray(v.reshape(EC, P, -1).transpose(1, 0, 2))
    i = {k: np.asarray(v) for k, v in inp.items()}
    ep = T * TS
    src, dst = rows(i["src"], ep), rows(i["dst"], ep, NP)
    off = np.array([0.0, 0.0, 0.0, -1.0], np.float32)
    per = np.array([1 / 50.0, 1.0, 1.0, 1 / 10.0], np.float32)
    spread = np.zeros((QT, 4, QT, 4, K8), np.float32)
    for q in range(QT):
        for c in range(4):
            spread[q, c, q, c, :] = per[c] / DENOM
    bias1 = np.tile(((off[:, None] - GRID[None, :]) / DENOM).reshape(-1), QT).astype(np.float32)
    w_edge = np.zeros((QT, 4 * K8, QT, 2 * P), np.float32)
    for q in range(QT):
        w_edge[q, :, q, :] = np.repeat(i["L0_gnn_W_edge"].T, K8, axis=1)
    w_edge = w_edge.reshape(P, QT, 2 * P)
    cg, which = cg_tables()
    w1 = i["L1_gnn_W"][which[..., 0], which[..., 1], which[..., 2]]
    return {
        "x": rows(i["x"], NP), "src": columns(src)[:, :, 0], "dst": columns(dst)[:, :, 0], "dst_rows": dst.reshape(T, TS),
        "node_vec": np.ascontiguousarray(rows(i["node_vec"], NP).reshape(NB, P).T),
        "edge_attr_4": np.ascontiguousarray(rows(i["edge_attr_4"], ep).reshape(QN, QT, TS, 4).transpose(1, 3, 0, 2)
                                            .reshape(4 * QT, QN * TS)),
        "harmonics": columns(rows(np.concatenate([i["edge_weight1"], i["edge_attr_3"], i["edge_attr_5"]], axis=1), ep)),
        "W_att": i["L0_gnn_W_att"], "W_lar": i["L0_gnn_W_lar"], "b_att": i["L0_gnn_b_att"], "b_lar": i["L0_gnn_b_lar"],
        "grid": GRID[None, :], "grid_col": np.tile(GRID, P // K8)[:, None].copy(),
        "spread": spread.reshape(4 * QT, P), "bias1": bias1[:, None], "W_edge": w_edge,
        "W_att_edge": np.ascontiguousarray(i["L0_gnn_W_att"][0, :D * K8].reshape(2, P).T),
        "b_edge": np.ascontiguousarray(np.repeat(i["L0_gnn_b_edge"], K8).reshape(2, P).T),
        "cg": cg, "W1_rep": w1,
        "gamma_hid": i["L2_gnn_bn_gamma_hid"], "beta_hid": i["L2_gnn_bn_beta_hid"],
        "gamma_out": i["L2_gnn_bn_gamma_out"], "beta_out": i["L2_gnn_bn_beta_out"],
        "edge_attr_16": rows(i["edge_attr_16"], ep).reshape(PN, JP, P, ED).transpose(0, 3, 1, 2),
        "Wf1_dst": np.concatenate([i["L3_gnn_Wf1"][0:D], i["L3_gnn_Wf1"][D:2 * D]], axis=1),
        "Wf1_src": np.concatenate([i["L3_gnn_Wf1"][D:2 * D], i["L3_gnn_Wf1"][0:D]], axis=1),
        "Wf1_edge": np.concatenate([i["L3_gnn_Wf1"][2 * D:], i["L3_gnn_Wf1"][2 * D:]], axis=1),
        "bf1_twice": np.concatenate([i["L3_gnn_bf1"], i["L3_gnn_bf1"]]),
        **{k: i["L3_gnn_" + k] for k in ("Wf2", "bf2", "Wn1", "bn1", "Wn2", "bn2")},
        **{k: i["L2_gnn_" + k] for k in ("W_enc1", "b_enc1", "W_hid", "b_hid", "W_dec2", "b_dec2", "W_dec3", "b_dec3",
                                         "Wres_enc1", "bres_enc1", "Wres_dec2", "bres_dec2")},
    }


def kernel(**inputs):
    import concourse.bacc as bacc
    from concourse.bass_utils import run_bass_kernel_spmd as run

    nc = bacc.Bacc("TRN2", target_bir_lowering=False, num_devices=1)
    arrays, a = {}, {}
    for name, v in layouts(inputs).items():
        v = np.ascontiguousarray(v)
        arrays[f"in_{name}_dram"] = v
        a[name] = nc.dram_tensor(f"in_{name}_dram", v.shape, mybir.dt.from_np(v.dtype), kind="ExternalInput").ap()
    out = nc.dram_tensor("out_0_dram", (N, D), F32, kind="ExternalOutput").ap()
    program(nc, a, out, PHASES)
    r = run(nc, [arrays], core_ids=[0])
    return r.results[0]["out_0_dram"]
```

```python
from contextlib import ExitStack, contextmanager

import concourse.bass as bass
import numpy as np
from concourse import mybir

F32 = mybir.dt.float32
F16 = mybir.dt.float16
I32 = mybir.dt.int32
U32 = mybir.dt.uint32
ALU = mybir.AluOpType
ACT = mybir.ActivationFunctionType
X = mybir.AxisListType.X
ds = bass.ds

P = 128
N = 3125
NB = -(-N // P)
NP = NB * P
E = 100000
J = 4
TS = J * P
T = -(-E // TS)
EC = T * J
D = 32
K8 = 8
HALF = NP // 2
BIG = 1.0e30
EPS = 1e-5
GRID = np.linspace(-2.0, 2.0, K8, dtype=np.float32)
DENOM = float(GRID[1] - GRID[0])
LOW = 4096.0
QT = 4
QN = T // QT
AW = 36
GC = 8
GN = EC // GC // 2
JP = 2 * J
PS = JP * P
PN = T // 2
SL = 2
ML = 7
assert PN % ML == 0 and PN % SL == 0 and T % QT == 0 and EC % (2 * GC) == 0 and T % 2 == 0


class Tools:

    def __init__(self, nc, ctx, stage):
        self.nc, self.ctx, self.stage, self.sems = nc, ctx, stage, []

    def sb(self, name, shape, dt=F32):
        return self.ctx.enter_context(self.nc.sbuf_tensor(f"{self.stage}_{name}", shape, dt))

    def ps(self, name, shape, dt=F32):
        return self.ctx.enter_context(self.nc.psum_tensor(f"{self.stage}_{name}", shape, dt))

    def sem(self, name):
        self.sems.append(self.ctx.enter_context(self.nc.semaphore(f"{self.stage}_{name}")))
        return self.sems[-1]


@contextmanager
def stage_tools(nc, stage):
    with ExitStack() as ctx:
        t = Tools(nc, ctx, stage)
        yield t
        with nc.Block() as block:
            @block.sync
            def _(e):
                for s in t.sems:
                    e.sem_clear(s)


class Chain:

    def __init__(self, eng, sem):
        self.eng, self.sem, self.n = eng, sem, 0

    def __call__(self, ins):
        ins.then_inc(self.sem, 1)
        self.n += 1
        self.eng.wait_ge(self.sem, self.n)
        return self.n


def bcast(ap, shape):
    return ap.broadcast_to(shape)


def setup(nc, g, a, dr):
    with stage_tools(nc, "setup") as t:
        s_load, s_pool, s_v, s_pe = t.sem("loaded"), t.sem("pool"), t.sem("vector"), t.sem("tensor")
        dst_t = t.sb("dst_t", [T // 2, 2 * TS], I32)
        dst_f = t.sb("dst_f", [T // 2, 2 * TS])
        dst_i = t.sb("dst_i", [P, EC], I32)
        hi_t, lo_t = t.sb("hi_t", [PN, JP]), t.sb("lo_t", [PN, JP])
        first_id, next_id = g.block_first, t.sb("next_id", [P, NB])
        rank, back = t.sb("rank", [P, JP]), t.sb("back", [P, JP])
        keys = t.sb("keys", [PN, 2, JP, NB])
        tb_f, pb_i, s_tb = t.sb("pair_range", [T // 2, 3]), t.sb("pair_blocks", [T // 2, 1], I32), t.sem("pair_blocks")
        dst16 = t.sb("dst16", [T // 2, 2 * TS], F16)
        key = t.sb("key", [T // 2, 2 * NB])
        best, bounds = t.sb("best", [2 * NB, 1]), t.sb("bounds", [1, 2 * NB])
        ids = g.ids
        pk, pb = t.ps("pk", [2 * NB, P]), t.ps("pb", [1, 2 * NB])
        found = [0]
        with nc.Block() as block:
            @block.sync
            def _(e):
                e.dma_start(g.src_i[:, :], a["src"]).then_inc(s_load, 16)
                e.dma_start(dst_i[:, :], a["dst"]).then_inc(s_load, 16)
                e.dma_start(dst_t[:, :], a["dst_rows"].rearrange("(p c) n -> p (c n)", c=2)).then_inc(s_load, 16)
                e.wait_ge(s_tb, 1)
                e.dma_start(dr["pair_blocks"], pb_i[:, :]).then_inc(s_load, 16)
                e.dma_start(dr["dst16"], dst16[:, :]).then_inc(s_load, 16)
                e.wait_ge(s_load, 80)
                e.dma_start(g.pair_blocks[:, :], dr["pair_blocks"].rearrange("t a -> a t")).then_inc(s_load, 16)
                e.wait_ge(s_load, 96)

            @block.gpsimd
            def _(e):
                e.iota(ids[:, :], [[1, NP]], base=-HALF, channel_multiplier=0,
                       allow_small_or_imprecise_dtypes=True).then_inc(s_pool, 1)
                e.iota(g.pcol[:, :], [[1, 1]], base=0, channel_multiplier=1,
                       allow_small_or_imprecise_dtypes=True).then_inc(s_pool, 1)
                e.iota(g.node_id[:, :], [[P, NB]], base=0, channel_multiplier=1,
                       allow_small_or_imprecise_dtypes=True).then_inc(s_pool, 1)
                e.iota(g.iota[:, :], [[1, P]], base=0, channel_multiplier=0,
                       allow_small_or_imprecise_dtypes=True).then_inc(s_pool, 1)
                e.iota(first_id[:, :], [[P, NB + 1]], base=0, channel_multiplier=0,
                       allow_small_or_imprecise_dtypes=True).then_inc(s_pool, 1)
                e.iota(next_id[:, :], [[P, NB]], base=P, channel_multiplier=0,
                       allow_small_or_imprecise_dtypes=True).then_inc(s_pool, 1)
                e.iota(rank[:, :], [[1, JP]], base=1, channel_multiplier=JP,
                       allow_small_or_imprecise_dtypes=True).then_inc(s_pool, 1)
                e.iota(back[:, :], [[-1, JP]], base=EC, channel_multiplier=-JP,
                       allow_small_or_imprecise_dtypes=True).then_inc(s_pool, 1)

            @block.vector
            def _(e):
                c = Chain(e, s_v)
                c(e.memset(g.ones[:, :], 1.0))
                e.wait_ge(s_pool, 8)
                c(e.tensor_copy(g.ids16[:, :], ids[:, :]))
                c(e.tensor_scalar(g.ident[:, :], g.iota[:, :], g.pcol[:, 0:1], None, ALU.is_equal))
                c(e.tensor_copy(g.ident16[:, :], g.ident[:, :]))
                e.wait_ge(s_load, 48)
                c(e.tensor_scalar(g.dst_c[:, :], dst_i[:, :], -float(HALF), None, ALU.add))
                c(e.tensor_copy(g.src_f[:, :], g.src_i[:, :]))
                c(e.tensor_scalar(g.src_f[:, :], g.src_f[:, :], -float(HALF), None, ALU.add))
                c(e.tensor_copy(dst_f[:, :], dst_t[:, :]))
                rows = dst_f[:, :].rearrange("p (c n) -> p c n", c=JP)
                c(e.tensor_reduce(hi_t[:, :], rows, X, ALU.max))
                c(e.tensor_reduce(lo_t[:, :], rows, X, ALU.min))
                n2 = T // 2
                for k in range(JP):
                    c(e.tensor_scalar(keys[:, 0, k, :], first_id[0:n2, 0:NB], hi_t[:, k:k + 1], back[0:n2, k:k + 1],
                                      ALU.is_le, ALU.mult))
                    c(e.tensor_scalar(keys[:, 1, k, :], next_id[0:n2, :], lo_t[:, k:k + 1], rank[0:n2, k:k + 1],
                                      ALU.is_gt, ALU.mult))
                c(e.tensor_reduce(key[:, :].rearrange("p (a b) -> p a b", a=2), keys[:, :, :, :].rearrange("p a k b -> p a b k"),
                                  X, ALU.max))
                found[0] = c.n
                e.wait_ge(s_pe, 1)
                c(e.tensor_reduce(best[:, :], pk[:, 0:n2], X, ALU.max))
                e.wait_ge(s_pe, 2)
                c(e.tensor_scalar(bounds[:, 0:NB], pb[:, 0:NB], -1.0, float(EC), ALU.mult, ALU.add))
                c(e.tensor_copy(bounds[:, NB:], pb[:, NB:]))
                c(e.tensor_copy(g.bounds[:, :], bounds[:, :]))
                c(e.tensor_reduce(tb_f[:, 0:1], lo_t[:, :], X, ALU.min))
                c(e.tensor_reduce(tb_f[:, 1:2], hi_t[:, :], X, ALU.max))
                c(e.tensor_scalar(keys[:, 0, 0, :], next_id[0:n2, :], tb_f[:, 0:1], None, ALU.is_le))
                c(e.tensor_scalar(keys[:, 0, 1, :], first_id[0:n2, 0:NB], tb_f[:, 1:2], 32.0, ALU.is_le, ALU.mult))
                c(e.tensor_reduce(tb_f[:, 2:3], keys[:, 0, 0:2, :].rearrange("p k b -> p (k b)"), X, ALU.add))
                c(e.tensor_copy(pb_i[:, :], tb_f[:, 2:3]))
                c(e.tensor_scalar(dst16[:, :], dst_f[:, :], -float(HALF), None, ALU.add))
                c(e.tensor_scalar(g.node_c[:, :], g.node_id[:, :], -float(HALF), None, ALU.add))
                e.sem_inc(s_tb, 1)

            @block.tensor
            def _(e):
                e.wait_ge(s_v, found[0])
                e.transpose(pk[:, 0:T // 2], key[:, :], g.ident[0:T // 2, 0:T // 2]).then_inc(s_pe, 1)
                e.wait_ge(s_v, found[0] + 1)
                e.transpose(pb[:, :], best[:, :], g.ident[0:2 * NB, 0:2 * NB]).then_inc(s_pe, 1)


def layernorm_relu(e, c, wait_scalar, t, x, h):
    m, v, sq = t
    c(e.tensor_reduce(m[:, :], x, X, ALU.add))
    c(e.tensor_scalar(m[:, :], m[:, :], 1.0 / D, None, ALU.mult))
    c(e.tensor_tensor(h, x, bcast(m[:, :].unsqueeze(2), [P, NB, D]), ALU.subtract))
    c(e.tensor_tensor(sq, h, h, ALU.mult))
    c(e.tensor_reduce(v[:, :], sq, X, ALU.add))
    c(e.tensor_scalar(v[:, :], v[:, :], 1.0 / D, EPS, ALU.mult, ALU.add))
    wait_scalar()
    c(e.reciprocal(v[:, :], v[:, :]))
    c(e.tensor_tensor(h, h, bcast(v[:, :].unsqueeze(2), [P, NB, D]), ALU.mult))
    c(e.tensor_scalar(h, h, 0.0, None, ALU.max))


def table0(nc, g, a, dr):
    with stage_tools(nc, "table0") as t:
        s_load, s_v, s_a, s_out = t.sem("loaded"), t.sem("vector"), t.sem("scalar"), t.sem("stored")
        m, v = t.sb("mean", [P, NB]), t.sb("var", [P, NB])
        h, sq = t.sb("h", [P, NB, D]), t.sb("sq", [P, NB, D])
        z, w = t.sb("z", [P, NB, D, K8]), t.sb("w", [P, D * K8])
        grid, wl = t.sb("grid", [P, K8]), t.sb("wl", [P, K8])
        ba, bl = t.sb("ba", [P, 1]), t.sb("bl", [P, 1])
        cnt, zc = t.sb("cnt", [P, NB]), t.sb("zc", [P, NB, K8])
        u, ua, ul = t.sb("u", [P, NB]), t.sb("ua", [P, NB]), t.sb("ul", [P, NB])
        tab = t.sb("tab", [P, NB, AW])
        with nc.Block() as block:
            @block.vector
            def _(e):
                c = Chain(e, s_v)
                e.wait_ge(s_load, 16 * 7)
                c(e.memset(tab[:, :, :], 0.0))
                layernorm_relu(e, c, lambda: e.wait_ge(s_a, 1), (m, v, sq[:, :, :]), g.x[:, :, :], h[:, :, :])
                gz = grid[:, :].unsqueeze(1).unsqueeze(1)
                c(e.tensor_tensor(z[:, :, :, :], bcast(h[:, :, :].unsqueeze(3), [P, NB, D, K8]),
                                  bcast(gz, [P, NB, D, K8]), ALU.subtract))
                c(e.tensor_tensor(z[:, :, :, :], z[:, :, :, :], z[:, :, :, :], ALU.mult))
                c(e.tensor_tensor(zc[:, :, :], bcast(cnt[:, :].unsqueeze(2), [P, NB, K8]),
                                  bcast(grid[:, :].unsqueeze(1), [P, NB, K8]), ALU.subtract))
                g.t0_exp = c(e.tensor_tensor(zc[:, :, :], zc[:, :, :], zc[:, :, :], ALU.mult))
                e.wait_ge(s_a, 3)
                wz = w[:, :].rearrange("p (f k) -> p f k", k=K8).unsqueeze(1)
                c(e.tensor_tensor(z[:, :, :, :], z[:, :, :, :], bcast(wz, [P, NB, D, K8]), ALU.mult))
                c(e.tensor_reduce(u[:, :], z[:, :, :, :].rearrange("p b f k -> p b (f k)"), X, ALU.add))
                c(e.tensor_scalar(tab[:, :, D], u[:, :], ba[:, 0:1], None, ALU.add))
                c(e.tensor_tensor(zc[:, :, :], zc[:, :, :], bcast(wl[:, :].unsqueeze(1), [P, NB, K8]), ALU.mult))
                c(e.tensor_reduce(u[:, :], zc[:, :, :], X, ALU.add))
                c(e.tensor_scalar(u[:, :], u[:, :], bl[:, 0:1], None, ALU.add))
                c(e.tensor_scalar(ua[:, :], u[:, :], -1.0, None, ALU.mult))
                g.t0_abs = c(e.tensor_tensor(ua[:, :], ua[:, :], u[:, :], ALU.min))
                e.wait_ge(s_a, 5)
                c(e.tensor_scalar(u[:, :], u[:, :], 0.0, None, ALU.max))
                c(e.tensor_tensor(ul[:, :], ul[:, :], u[:, :], ALU.add))
                g.t0_done = c(e.tensor_tensor(tab[:, :, 0:D], h[:, :, :],
                                              bcast(ul[:, :].unsqueeze(2), [P, NB, D]), ALU.mult))

            @block.sync
            def _(e):
                e.dma_start(g.x[:, :, :], a["x"].rearrange("(b p) f -> p b f", p=P)).then_inc(s_load, 16)
                e.dma_start(cnt[:, :], a["node_vec"]).then_inc(s_load, 16)
                e.dma_start(w[:, :], a["W_att"][0:1, D * K8:].partition_broadcast(P)).then_inc(s_load, 16)
                e.dma_start(wl[:, :], a["W_lar"][0:1, :].partition_broadcast(P)).then_inc(s_load, 16)
                e.dma_start(ba[:, :], a["b_att"].unsqueeze(0).partition_broadcast(P)).then_inc(s_load, 16)
                e.dma_start(bl[:, :], a["b_lar"].unsqueeze(0).partition_broadcast(P)).then_inc(s_load, 16)
                e.dma_start(grid[:, :], a["grid"][0:1, :].partition_broadcast(P)).then_inc(s_load, 16)
                e.wait_ge(s_v, g.t0_done)
                e.dma_start(dr["table0"].rearrange("(b p) f -> p b f", p=P), tab[:, :, :]).then_inc(s_out, 16)
                e.wait_ge(s_out, 16)

            @block.scalar
            def _(e):
                e.wait_ge(s_v, 7)
                e.activation(v[:, :], v[:, :], ACT.Sqrt).then_inc(s_a, 1)
                e.wait_ge(s_v, g.t0_exp)
                e.activation(z[:, :, :, :], z[:, :, :, :], ACT.Exp, scale=-1.0 / DENOM ** 2).then_inc(s_a, 1)
                e.activation(zc[:, :, :], zc[:, :, :], ACT.Exp, scale=-1.0 / DENOM ** 2).then_inc(s_a, 1)
                e.wait_ge(s_v, g.t0_abs)
                e.activation(ul[:, :], ua[:, :], ACT.Exp).then_inc(s_a, 1)
                e.wait_ge(s_a, 4)
                e.activation(ul[:, :], ul[:, :], ACT.Ln, bias=1.0).then_inc(s_a, 1)



def edge_logits(nc, g, a, dr):
    with stage_tools(nc, "logit") as t:
        s_load, s_w = t.sem("loaded"), t.sem("weights")
        s_p1, s_sq1, s_r1 = t.sem("spread"), t.sem("squared1"), t.sem("bases1")
        s_z2, s_sq2, s_r2 = t.sem("features"), t.sem("squared2"), t.sem("bases2")
        s_wr, s_wd, s_at, s_ev = t.sem("half_weighed"), t.sem("weighed"), t.sem("summed"), t.sem("copied")
        s_out, s_st = t.sem("landed"), t.sem("stored")
        ea = t.sb("ea", [4 * QT, QN * TS])
        spread, bias1 = t.sb("spread", [4 * QT, P]), t.sb("bias1", [P, 1])
        w_edge, watt = t.sb("w_edge", [P, QT, 2 * P]), t.sb("watt", [P, 2])
        bias2, gcol, brep = t.sb("bias2", [P, 2]), t.sb("gcol", [P, 1]), t.sb("brep", [P, 2])
        pick = t.sb("pick", [P, QT, QT])
        r1, r2 = t.sb("r1", [P, 2, TS]), t.sb("r2", [P, 2, 2, TS])
        wr, wd = t.sb("wr", [P, 2, TS]), t.sb("wd", [P, 2, TS])
        el = t.sb("el", [QT, 2, TS])
        p1, pa = t.ps("p1", [P, TS]), [t.ps(f"pa{i}", [QT, TS]) for i in range(2)]
        z2 = [t.ps(f"z2_{i}", [P, 2, TS]) for i in range(2)]
        with nc.Block() as block:
            def steps(eng, step):
                with eng.Fori(0, QN // 2, 1) as k:
                    step(2 * k, 0)
                    step(2 * k + 1, 1)
                step(QN - 1, 0)

            def lagging(eng, step):
                step(0, 0, "first")
                with eng.Fori(1, QN // 2, 1) as k:
                    step(2 * k - 1, 1, None)
                    step(2 * k, 0, None)
                step(QN - 2, 1, None)
                step(QN - 1, 0, "last")

            @block.sync
            def _(e):
                for dst_ap, src_ap in ((spread[:, :], a["spread"]), (bias1[:, :], a["bias1"]), (w_edge[:, :, :], a["W_edge"]),
                                       (watt[:, :], a["W_att_edge"]), (brep[:, :], a["b_edge"]), (gcol[:, :], a["grid_col"]),
                                       (ea[:, :], a["edge_attr_4"])):
                    e.dma_start(dst_ap, src_ap).then_inc(s_load, 16)

                def step(i, par):
                    e.wait_ge(s_ev, i + 3)
                    e.dma_start(dr["edge_logit"][ds(i * QT, QT), :], el[:, par, :]).then_inc(s_out, 16)
                    e.wait_ge(s_out, 16 * (i + 1))
                    e.sem_inc(s_st, 1)
                e.sem_inc(s_st, 2)
                steps(e, step)

            @block.vector
            def _(e):
                c = Chain(e, s_w)
                e.wait_ge(s_load, 16 * 7)
                c(e.memset(pick[:, :, :], 0.0))
                for q in range(QT):
                    c(e.memset(pick[:, q, q:q + 1], 1.0))
                c(e.tensor_tensor(bias2[:, :], brep[:, :], bcast(gcol[:, 0:1], [P, 2]), ALU.subtract))
                c(e.tensor_scalar(bias2[:, :], bias2[:, :], 1.0 / DENOM, None, ALU.mult))

                e.sem_inc(s_wd, 2)
                e.sem_inc(s_ev, 2)

                def copy(i, par):
                    e.wait_ge(s_at, i * QT + QT + 2)
                    e.wait_ge(s_st, i + 1)
                    e.tensor_copy(el[:, par, :], pa[par][:, :]).then_inc(s_ev, 1)

                def step(i, par, end):
                    for q in range(QT):
                        n, s = i * QT + q, q % 2
                        if q == 2 and end != "first":
                            copy(i - 1, 1 - par)
                        e.wait_ge(s_r2, n + 1)
                        e.tensor_scalar(wr[:, s, :], r2[:, s, 0, :], watt[:, 0:1], None, ALU.mult).then_inc(s_wr, 1)
                        e.wait_ge(s_wr, n + 1)
                        e.wait_ge(s_at, n + 1)
                        e.scalar_tensor_tensor(wd[:, s, :], r2[:, s, 1, :], watt[:, 1:2], wr[:, s, :],
                                               ALU.mult, ALU.add).then_inc(s_wd, 1)
                lagging(e, step)
                copy(QN - 1, 0)

            @block.scalar
            def _(e):
                e.wait_ge(s_w, 7)
                e.sem_inc(s_sq2, 4)

                def bases1(i, par):
                    e.wait_ge(s_p1, i + 1)
                    e.activation(r1[:, par, :], p1[:, :], ACT.Square, bias=bias1[:, 0:1]).then_inc(s_sq1, 1)
                    e.wait_ge(s_sq1, i + 1)
                    e.activation(r1[:, par, :], r1[:, par, :], ACT.Exp, scale=-1.0).then_inc(s_r1, 1)

                def step(i, par, last=False):
                    for q in range(QT):
                        n, s = i * QT + q, q % 2
                        e.wait_ge(s_z2, n + 1)
                        e.wait_ge(s_wd, n + 1)
                        for h in range(2):
                            e.activation(r2[:, s, h, :], z2[s][:, h, :], ACT.Square, bias=bias2[:, h:h + 1],
                                         scale=1.0 / DENOM).then_inc(s_sq2, 1)
                        e.wait_ge(s_sq2, 2 * n + 6)
                        e.activation(r2[:, s, :, :], r2[:, s, :, :], ACT.Exp, scale=-1.0).then_inc(s_r2, 1)
                        if q == 1 and not last:
                            bases1(i + 1, 1 - par)
                bases1(0, 0)
                with e.Fori(0, QN // 2, 1) as k:
                    step(2 * k, 0)
                    step(2 * k + 1, 1)
                step(QN - 1, 0, True)

            @block.tensor
            def _(e):
                e.wait_ge(s_w, 7)
                e.sem_inc(s_at, 2)

                def expand(i):
                    e.matmul(p1[:, :], spread[:, :], ea[:, ds(i * TS, TS)], start=True, stop=True).then_inc(s_p1, 1)

                def features(n, par, q):
                    for h in range(2):
                        m = e.matmul(z2[q % 2][:, h, :], w_edge[:, q, h * P:(h + 1) * P],
                                     r1[:, par, :], start=True, stop=True)
                    m.then_inc(s_z2, 1)

                def weigh(n, par, q):
                    e.wait_ge(s_wd, n + 3)
                    e.matmul(pa[par][:, :], pick[:, q, :], wd[:, q % 2, :], start=(q == 0), stop=(q == QT - 1)).then_inc(s_at, 1)

                def step(i, par, end):
                    for q in range(QT):
                        n = i * QT + q
                        if q == 0:
                            e.wait_ge(s_r1, i + 1)
                        e.wait_ge(s_sq2, 2 * n + 2)
                        features(n, par, q)
                        if q == 0 and end != "last":
                            e.wait_ge(s_sq1, i + 1)
                            expand(i + 1)
                        if q == 2:
                            e.wait_ge(s_ev, i + 1)
                        if q >= 2:
                            weigh(n - 2, par, q - 2)
                        elif end != "first":
                            weigh(n - 2, 1 - par, q + 2)
                expand(0)
                lagging(e, step)
                weigh(QN * QT - 2, 0, QT - 2)
                weigh(QN * QT - 1, 0, QT - 1)


def node_gather(e, t, g, table, slots, s_slot, s_claim, keep=None):
    idx = t.sb("idx", [P, 2, GC], I32)
    s_idx = t.sem("idx")

    def fetch(i, h):
        c = 2 * i + h
        e.wait_ge(s_slot[h][1], i + 1)
        e.sem_inc(s_claim, 1)
        e.tensor_copy(idx[:, h, :], g.src_i[:, ds(c * GC, GC)]).then_inc(s_idx, 1)
        e.wait_ge(s_idx, c + 1)
        e.sem_inc(s_claim, 1)
        for j in range(GC):
            e.indirect_dma_start(slots[:, h, j, :], None, table,
                                 bass.IndirectOffsetOnAxis(ap=idx[:, h, j:j + 1].bitcast(U32), axis=0)).then_inc(s_slot[h][0], 16)

    fetch(0, 0)
    fetch(0, 1)
    with e.Fori(1, GN, 1) as i:
        for h in range(2):
            if keep is not None:
                keep(i - 1, h)
            fetch(i, h)
    if keep is not None:
        keep(GN - 1, 0)
        keep(GN - 1, 1)


def column_range(e, g, b):
    return (e.value_load(g.bounds[0:1, ds(b, 1)], min_val=0, max_val=EC - 1),
            e.value_load(g.bounds[0:1, ds(b + NB, 1)], min_val=0, max_val=EC))


class Count:

    def __init__(self, e, name, most):
        self.e, self.most = e, most
        self.reg = e.alloc_register(name)
        e.reg_mov(self.reg, 0)

    def now(self):
        return self.e.snap(self.reg, min_val=0, max_val=self.most)

    def up(self):
        self.e.reg_add(self.reg, self.reg, 1)


class Range:

    def __init__(self, e, name):
        self.e, self.lo, self.hi = e, e.alloc_register(f"{name}_lo"), e.alloc_register(f"{name}_hi")

    def load(self, g, pair, turn):
        lo, hi = block_range(self.e, g, pair, turn)
        self.e.reg_mov(self.lo, lo)
        self.e.reg_mov(self.hi, hi)

    def blocks(self):
        return self.e.Fori(self.e.snap(self.lo, min_val=0, max_val=NB - 1), self.e.snap(self.hi, min_val=0, max_val=NB), 1)


VISITS = NB * T
DC = [min(512, N - c) for c in range(0, N, 512)]
CB = len(DC)
CG = [(0, 1), (1, 3), (3, 5), (5, CB)]


def count_and_gather(nc, g, a, dr, G):
    with stage_tools(nc, "count") as t:
        s_slot = [(g.rows_landed[0][h], t.sem(f"free{h}")) for h in range(2)]
        s_claim, s_kept = t.sem("claim"), t.sem("kept")
        s_oh, s_used, s_sum, s_ev, s_out, s_st = (t.sem(n) for n in (
            "onehot", "used", "summed", "copied", "landed", "stored"))
        s_z = t.sem("zeros")
        slots = t.sb("slots", [P, 2, GC, AW])
        ohs = t.sb("ohs", [P, J, NP], F16)
        ohd = t.sb("ohd", [P, J, P], F16)
        zero = t.sb("zero", [1, 512], F16)
        row = t.sb("row", [P, 2, NP], F16)
        degc = t.sb("degc", [P, NB, len(CG)])
        acc = t.ps("acc", [P, CB * 512])
        with nc.Block() as block:
            @block.gpsimd
            def _(e):
                def keep(i, h):
                    e.wait_ge(s_slot[h][0], 16 * GC * (i + 1))
                    e.sem_inc(s_claim, 1)
                    e.tensor_copy(G[:, ds((2 * i + h) * GC, GC), :], slots[:, h, :, 0:D + 1]).then_inc(s_kept, 1)
                    e.wait_ge(s_kept, 2 * i + h + 1)
                    e.sem_inc(s_slot[h][1], 1)
                e.sem_inc(s_slot[0][1], 1)
                e.sem_inc(s_slot[1][1], 1)
                node_gather(e, t, g, dr["table0"][:, :], slots, s_slot, s_claim, keep)

            @block.vector
            def _(e):
                e.memset(zero[:, :], 0.0).then_inc(s_z, 1)
                e.memset(row[:, :, N:NP], 0.0).then_inc(s_z, 1)
                v = Count(e, "v", NB * EC)
                with e.Fori(0, NB, 1) as b:
                    lo, hi = column_range(e, g, b)
                    with e.Fori(lo, hi, 1) as c:
                        n = v.now()
                        j = e.snap(n % J, min_val=0, max_val=J - 1)
                        e.wait_ge(s_used, n + 1)
                        e.tensor_scalar(ohd[:, ds(j, 1), :].rearrange("p a n -> p (a n)"), g.ids16[:, ds(b * P, P)],
                                        g.dst_c[:, ds(c, 1)], None, ALU.is_equal).then_inc(s_oh, 1)
                        e.tensor_scalar(ohs[:, ds(j, 1), 0:N + 1].rearrange("p a n -> p (a n)"), g.ids16[:, 0:N + 1],
                                        g.src_f[:, ds(c, 1)], None, ALU.is_equal).then_inc(s_oh, 1)
                        v.up()

            @block.tensor
            def _(e):
                e.wait_ge(s_z, 2)
                e.sem_inc(s_used, J)
                v = Count(e, "v", NB * EC)
                with e.Fori(0, NB, 1) as b:
                    lo, hi = column_range(e, g, b)
                    for k, w in enumerate(DC):
                        for m, (k0, _) in enumerate(CG):
                            if k == k0:
                                e.wait_ge(s_ev, len(CG) * b + m + 1)
                        e.matmul(acc[:, 512 * k:512 * k + w], zero[0:1, 0:P], zero[0:1, 0:w], start=True, stop=False,
                                 skip_group_check=True)
                    with e.Fori(lo, hi, 1) as c:
                        n = v.now()
                        j = e.snap(n % J, min_val=0, max_val=J - 1)
                        e.wait_ge(s_oh, n * 2 + 2)
                        for k, w in enumerate(DC):
                            m = e.matmul(acc[:, 512 * k:512 * k + w], ohd[:, ds(j, 1), :].rearrange("p a n -> p (a n)"),
                                         ohs[:, ds(j, 1), 512 * k:512 * k + w].rearrange("p a n -> p (a n)"),
                                         start=False, stop=False, skip_group_check=True)
                        m.then_inc(s_used, 1)
                        v.up()
                    e.matmul(acc[:, 512 * (CB - 1):512 * (CB - 1) + 1], zero[0:1, 0:P], zero[0:1, 0:1], start=False, stop=True,
                             skip_group_check=True).then_inc(s_sum, 1)

            @block.scalar
            def _(e):
                e.sem_inc(s_ev, len(CG))
                with e.Fori(0, NB, 1) as b:
                    e.wait_ge(s_sum, b + 1)
                    e.wait_ge(s_st, b + 1)
                    for k, (k0, k1) in enumerate(CG):
                        n0, n1 = 512 * k0, min(N, 512 * k1)
                        e.activation(row[:, ds(b % 2, 1), n0:n1].rearrange("p a n -> p (a n)"), acc[:, n0:n1],
                                     ACT.Copy, scale=0.5,
                                     accum_out=degc[:, ds(b, 1), k:k + 1].rearrange("p a n -> p (a n)")).then_inc(s_ev, 1)

            @block.sync
            def _(e):
                e.sem_inc(s_st, 2)
                with e.Fori(0, NB, 1) as b:
                    e.wait_ge(s_z, 2)
                    e.wait_ge(s_ev, len(CG) * (b + 2))
                    e.dma_start(dr["counts"][ds(b * P, P), :],
                                row[:, ds(b % 2, 1), :].rearrange("p a n -> p (a n)")).then_inc(s_out, 16)
                    e.wait_ge(s_out, 16 * (b + 1))
                    e.sem_inc(s_st, 1)
        s_d = t.sem("degree")
        with nc.Block() as block:
            @block.vector
            def _(e):
                e.tensor_reduce(g.deg[:, :], degc[:, :, :], X, ALU.add).then_inc(s_d, 1)
                e.wait_ge(s_d, 1)
                e.tensor_scalar(g.deg[:, :], g.deg[:, :], 2.0, None, ALU.mult).then_inc(s_d, 1)
                e.wait_ge(s_d, 2)


def pair_range(e, g, b):
    lo, hi = column_range(e, g, b)
    return e.snap(lo // JP, min_val=0, max_val=PN - 1), e.snap((hi + (JP - 1)) // JP, min_val=0, max_val=PN)


def raw_logits(nc, g, a, dr, G, raw):
    R = EC // 7
    with stage_tools(nc, "attn") as t:
        s_load, s_pe, s_v, s_a, s_out = (t.sem(n) for n in ("loaded", "tensor", "vector", "scalar", "stored"))
        cols, back = t.sb("cols", [R, 7, P]), t.sb("back", [R, 7, P])
        pc = t.ps("pc", [P, 2, 512])
        pr = t.ps("pr", [R, 2, 512])
        with nc.Block() as block:
            @block.sync
            def _(e):
                e.dma_start(cols[:, :, :], dr["edge_logit"].rearrange("t (j n) -> (t j) n", n=P)
                            .rearrange("(c r) n -> r c n", r=R)).then_inc(s_load, 16)
                e.wait_ge(s_a, 2)
                e.dma_start(dr["raw"].rearrange("t (j n) -> (t j) n", n=P).rearrange("(c r) n -> r c n", r=R),
                            back[:, :, :]).then_inc(s_out, 16)
                e.wait_ge(s_out, 16)

            @block.tensor
            def _(e):
                e.wait_ge(s_load, 16)
                for c in range(7):
                    m = e.transpose(pc[:, c // 4, (c % 4) * R:(c % 4 + 1) * R], cols[:, c, :], g.ident[0:R, 0:R])
                m.then_inc(s_pe, 1)
                e.wait_ge(s_v, 2)
                for c in range(7):
                    m = e.transpose(pr[:, c // 4, (c % 4) * P:(c % 4 + 1) * P], raw[:, c * R:(c + 1) * R], g.ident[:, :])
                m.then_inc(s_pe, 1)

            @block.vector
            def _(e):
                e.wait_ge(s_pe, 1)
                e.tensor_tensor(raw[:, 0:4 * R], pc[:, 0, 0:4 * R], G[:, 0:4 * R, D], ALU.add).then_inc(s_v, 1)
                e.tensor_tensor(raw[:, 4 * R:], pc[:, 1, 0:3 * R], G[:, 4 * R:, D], ALU.add).then_inc(s_v, 1)
                e.wait_ge(s_v, 2)
                e.memset(G[:, :, D:D + 1], 1.0).then_inc(s_v, 1)

            @block.scalar
            def _(e):
                e.wait_ge(s_pe, 2)
                e.activation(back[:, 0:4, :], pr[:, 0, :].rearrange("p (c n) -> p c n", n=P), ACT.Copy).then_inc(s_a, 1)
                e.activation(back[:, 4:7, :], pr[:, 1, 0:3 * P].rearrange("p (c n) -> p c n", n=P), ACT.Copy).then_inc(s_a, 1)



def block_range(e, g, pair, turn):
    e.sem_inc(turn, 1)
    both = e.value_load(g.pair_blocks[0:1, ds(pair, 1)], min_val=0, max_val=32 * NB + NB - 1)
    return e.snap(both % 32, min_val=0, max_val=NB - 1), e.snap(both // 32, min_val=0, max_val=NB)


def pairs(eng, step, places=SL):
    with eng.Fori(0, PN // places - 1, 1) as i:
        for s in range(places):
            step(i, s, False)
    for s in range(places):
        step(PN // places - 1, s, True)


def maxima(nc, g, dr, best):
    with stage_tools(nc, "amax") as t:
        s_in = [t.sem(f"inputs{s}") for s in range(ML)]
        s_free = [t.sem(f"free{s}") for s in range(ML)]
        s_z, s_v, s_turn = t.sem("start"), t.sem("steps"), t.sem("turn")
        raw_b, dstb = t.sb("raw_b", [P, ML, PS]), t.sb("dstb", [P, ML, PS], F16)
        pen, dump, top = t.sb("pen", [P, 2, PS], mybir.dt.bfloat16), t.sb("dump", [P, PS]), t.sb("top", [P, 1])
        with nc.Block() as block:
            @block.sync
            def _(e):
                for s in range(ML):
                    e.sem_inc(s_free[s], 1)

                def step(i, s, last):
                    tt = i * ML + s
                    e.wait_ge(s_free[s], i + 1)
                    e.dma_start(raw_b[:, s, :], dr["raw"][ds(tt, 1), :].partition_broadcast(P)).then_inc(s_in[s], 16)
                    e.dma_start(dstb[:, s, :], dr["dst16"][ds(tt, 1), :].partition_broadcast(P)).then_inc(s_in[s], 16)
                pairs(e, step, ML)

            @block.vector
            def _(e):
                e.memset(best[:, :], -0.1 * BIG).then_inc(s_z, 1)
                e.memset(top[:, :], -BIG).then_inc(s_z, 1)
                e.wait_ge(s_z, 2)
                v = Count(e, "amax_v", VISITS)

                def step(i, s, last):
                    lo, hi = block_range(e, g, i * ML + s, s_turn)
                    e.wait_ge(s_in[s], i * 32 + 32)
                    e.sem_inc(s_turn, 1)
                    with e.Fori(lo, hi, 1) as b:
                        n = v.now()
                        e.tensor_scalar(pen[:, s % 2, :], dstb[:, s, :], g.node_c[:, ds(b, 1)], -BIG,
                                        ALU.not_equal, ALU.mult).then_inc(s_v, 1)
                        e.wait_ge(s_v, n * 3 + 1)
                        e.sem_inc(s_turn, 1)
                        e.tensor_tensor_reduce(dump[:, :], raw_b[:, s, :], pen[:, s % 2, :], 1.0, -BIG,
                                               ALU.add, ALU.max, top[:, :]).then_inc(s_v, 1)
                        e.wait_ge(s_v, n * 3 + 2)
                        e.tensor_tensor(best[:, ds(b, 1)], best[:, ds(b, 1)], top[:, :], ALU.max).then_inc(s_v, 1)
                        v.up()
                    e.sem_inc(s_free[s], 1)
                pairs(e, step, ML)


def weighted_sums(nc, g, dr, raw, G, best, sums):
    bf = mybir.dt.bfloat16
    SB = -(-NB * 2 * D // 512)
    with stage_tools(nc, "weigh") as t:
        s_in, s_free, s_mask, s_mused, s_oh, s_oused = ([t.sem(f"{n}{s}") for s in range(SL)] for n in (
            "inputs", "free", "mask", "mask_used", "onehot", "onehot_used"))
        s_z, s_p, s_pm, s_w, s_wf, s_exp, s_wg, s_hi, s_lo, s_rfree, s_sum, s_ev, s_turn = (t.sem(n) for n in (
            "zeros", "parts", "picked", "difference", "steps", "weights", "weighed", "high", "low", "rows_used",
            "summed", "copied", "turn"))
        zero, part, rest = t.sb("zero", [1, 512], bf), t.sb("part", [P, NB, 3], bf), t.sb("rest", [P, NB])
        dstb, mask = t.sb("dstb", [P, SL, PS], F16), t.sb("mask", [P, SL, JP, P], bf)
        me, w = t.sb("me", [P, SL, JP]), t.sb("w", [P, SL, JP])
        wg, scaled = t.sb("wg", [P, JP, D + 1]), t.sb("scaled", [P, JP, D + 1])
        rows = t.sb("rows", [P, SL, JP, 2, D + 1], F16)
        oh = t.sb("oh", [P, SL, JP, P], F16)
        high = t.sb("high", [P, NB, 2 * D])
        den = t.sb("den", [P, NB, 2])
        pm = [t.ps(f"pm{i}", [P, JP, 4]) for i in range(SL)]
        acc, acd = t.ps("acc", [P, SB * 512]), t.ps("acd", [P, NB, 2])
        with nc.Block() as block:
            @block.sync
            def _(e):
                for s in range(SL):
                    e.sem_inc(s_free[s], 1)

                def step(i, s, last):
                    e.wait_ge(s_free[s], i + 1)
                    e.dma_start(dstb[:, s, :], dr["dst16"][ds(i * SL + s, 1), :].partition_broadcast(P)).then_inc(s_in[s], 16)
                pairs(e, step)

            @block.vector
            def _(e):
                e.memset(zero[:, :], 0.0).then_inc(s_z, 1)
                c = Chain(e, s_p)
                c(e.tensor_copy(part[:, :, 0], best[:, :]))
                c(e.tensor_tensor(rest[:, :], best[:, :], part[:, :, 0], ALU.subtract))
                c(e.tensor_copy(part[:, :, 1], rest[:, :]))
                c(e.tensor_tensor(rest[:, :], rest[:, :], part[:, :, 1], ALU.subtract))
                c(e.tensor_copy(part[:, :, 2], rest[:, :]))
                e.sem_inc(s_wf, 4)
                e.sem_inc(s_lo, 1)
                vm, vo = ([Count(e, f"weigh_{n}{s}", VISITS) for s in range(SL)] for n in ("masks", "onehots"))
                own = [Range(e, f"weigh_v{s}") for s in range(SL)]

                def masks(i, s):
                    e.wait_ge(s_in[s], i * 16 + 16)
                    e.sem_inc(s_turn, 1)
                    with own[s].blocks() as b:
                        n = vm[s].now()
                        e.wait_ge(s_mused[s], n + 1)
                        e.tensor_scalar(mask[:, s, :, :], dstb[:, s, :].rearrange("p (j n) -> p j n", j=JP), g.node_c[:, ds(b, 1)],
                                        None, ALU.is_equal).then_inc(s_mask[s], 1)
                        vm[s].up()
                    e.wait_ge(s_mask[s], vm[s].now())
                    e.sem_inc(s_free[s], 1)

                def difference(i, s):
                    tt = i * SL + s
                    e.wait_ge(s_pm, tt + 1)
                    e.tensor_reduce(me[:, s, :], pm[s][:, :, 0:3], X, ALU.add).then_inc(s_wf, 1)
                    e.wait_ge(s_wf, tt * 2 + 5)
                    e.tensor_tensor(w[:, s, :], raw[:, ds(tt * JP, JP)], me[:, s, :], ALU.subtract).then_inc(s_wf, 1)
                    e.wait_ge(s_wf, tt * 2 + 6)
                    e.tensor_scalar(w[:, s, :], w[:, s, :], 0.0, None, ALU.min).then_inc(s_w, 1)

                def weigh(i, s):
                    tt = i * SL + s
                    e.wait_ge(s_exp, tt + 1)
                    e.tensor_tensor(wg[:, :, :], G[:, ds(tt * JP, JP), :], bcast(w[:, s, :].unsqueeze(2), [P, JP, D + 1]),
                                    ALU.mult).then_inc(s_wg, 1)

                def step(i, s, last):
                    tt = i * SL + s
                    following = (i, 1) if s == 0 else (i + 1, 0)
                    e.wait_ge(s_hi, tt * 2 + 2)
                    e.scalar_tensor_tensor(rows[:, s, :, 1, :], rows[:, s, :, 0, :], -LOW, scaled[:, :, :],
                                           ALU.mult, ALU.add).then_inc(s_lo, 1)
                    with own[s].blocks() as b:
                        n = vo[s].now()
                        e.wait_ge(s_oused[s], n + 1)
                        for j in range(JP):
                            m = e.tensor_scalar(oh[:, s, j, :], g.ids16[:, ds(b * P, P)], g.dst_c[:, ds(tt * JP + j, 1)],
                                                None, ALU.is_equal)
                        m.then_inc(s_oh[s], 1)
                        vo[s].up()
                    if not last or s == 0:
                        difference(*following)
                    if not last:
                        own[s].load(g, (i + 1) * SL + s, s_turn)
                    if not last or s == 0:
                        weigh(*following)
                    if not last:
                        masks(i + 1, s)
                for s in range(SL):
                    own[s].load(g, s, s_turn)
                    masks(0, s)
                difference(0, 0)
                weigh(0, 0)
                pairs(e, step)
                e.wait_ge(s_ev, 2)
                e.scalar_tensor_tensor(sums[:, :, 0:D], high[:, :, D:], 1.0 / LOW, high[:, :, 0:D], ALU.mult, ALU.add).then_inc(s_p, 1)
                e.scalar_tensor_tensor(sums[:, :, D], den[:, :, 1], 1.0 / LOW, den[:, :, 0], ALU.mult, ALU.add).then_inc(s_p, 1)
                e.wait_ge(s_p, 7)

            @block.scalar
            def _(e):
                def exp(tt, s):
                    e.wait_ge(s_w, tt + 1)
                    e.activation(w[:, s, :], w[:, s, :], ACT.Exp).then_inc(s_exp, 1)

                def step(i, s, last):
                    tt = i * SL + s
                    e.wait_ge(s_wg, tt + 1)
                    e.wait_ge(s_rfree, tt + 1)
                    e.wait_ge(s_lo, tt + 1)
                    e.activation(rows[:, s, :, 0, :], wg[:, :, :], ACT.Copy).then_inc(s_hi, 1)
                    e.activation(scaled[:, :, :], wg[:, :, :], ACT.Copy, scale=LOW).then_inc(s_hi, 1)
                    if not last or s == 0:
                        exp(tt + 1, 1 - s)
                exp(0, 0)
                pairs(e, step)
                e.wait_ge(s_sum, 1)
                e.activation(high[:, :, :], acc[:, 0:NB * 2 * D].rearrange("p (b f) -> p b f", f=2 * D), ACT.Copy).then_inc(s_ev, 1)
                e.activation(den[:, :, :], acd[:, :, :], ACT.Copy).then_inc(s_ev, 1)

            @block.tensor
            def _(e):
                e.wait_ge(s_z, 1)
                e.wait_ge(s_p, 5)
                for s in range(SL):
                    e.sem_inc(s_mused[s], 1)
                    e.sem_inc(s_oused[s], 1)
                e.sem_inc(s_rfree, 2)
                for k in range(SB):
                    e.matmul(acc[:, 512 * k:512 * k + 512], zero[0:1, 0:P], zero[0:1, :], start=True, stop=False,
                             skip_group_check=True)
                e.matmul(acd[:, :, :], zero[0:1, 0:P], zero[0:1, 0:2 * NB], start=True, stop=False, skip_group_check=True)
                vm, vo = ([Count(e, f"weigh_{n}{s}", VISITS) for s in range(SL)] for n in ("picks", "sums"))
                own = [Range(e, f"weigh_pe{s}") for s in range(SL)]

                def picks(i, s):
                    e.wait_ge(s_wf, (i * SL + s) * 2 + 2)
                    e.matmul(pm[s][:, :, :], zero[0:1, 0:P], zero[0:1, 0:4 * JP], start=True, stop=False, skip_group_check=True)
                    with own[s].blocks() as b:
                        n = vm[s].now()
                        e.wait_ge(s_mask[s], n + 1)
                        for j in range(JP):
                            m = e.matmul(pm[s][:, j, 0:3], mask[:, s, j, :], part[:, ds(b, 1), :].rearrange("p a k -> p (a k)"),
                                         start=False, stop=False, skip_group_check=True)
                        m.then_inc(s_mused[s], 1)
                        vm[s].up()
                    e.matmul(pm[s][:, 0, 3:4], zero[0:1, 0:P], zero[0:1, 0:1], start=False, stop=True,
                             skip_group_check=True).then_inc(s_pm, 1)

                def step(i, s, last):
                    e.wait_ge(s_lo, i * SL + s + 2)
                    with own[s].blocks() as b:
                        n = vo[s].now()
                        e.wait_ge(s_oh[s], n + 1)
                        for j in range(JP):
                            e.matmul(acc[:, ds(b * (2 * D), 2 * D)], oh[:, s, j, :], rows[:, s, j, :, 0:D], start=False,
                                     stop=False, skip_group_check=True)
                            m = e.matmul(acd[:, ds(b, 1), :].rearrange("p a k -> p (a k)"), oh[:, s, j, :], rows[:, s, j, :, D],
                                         start=False, stop=False, skip_group_check=True)
                        m.then_inc(s_oused[s], 1)
                        vo[s].up()
                    if not last:
                        own[s].load(g, (i + 1) * SL + s, s_turn)
                    e.wait_ge(s_oused[s], vo[s].now() + 1)
                    e.sem_inc(s_rfree, 1)
                    if not last:
                        picks(i + 1, s)
                for s in range(SL):
                    own[s].load(g, s, s_turn)
                    picks(0, s)
                pairs(e, step)
                e.matmul(acc[:, 0:1], zero[0:1, 0:P], zero[0:1, 0:1], start=False, stop=True, skip_group_check=True)
                e.matmul(acd[:, 0, 0:1], zero[0:1, 0:P], zero[0:1, 0:1], start=False, stop=True,
                         skip_group_check=True).then_inc(s_sum, 1)


H9 = 9
BW = 96


def product_sums(nc, g, G, sums, harmonics, table):
    width = H9 * D
    with stage_tools(nc, "products") as t:
        s_oh, s_used = ([t.sem(f"{n}{s}") for s in range(2)] for n in ("onehot", "used"))
        s_z, s_sum, s_ev, s_load = (t.sem(n) for n in ("zeros", "summed", "copied", "loaded"))
        s_slot = [(g.rows_landed[1][h], t.sem(f"free{h}")) for h in range(2)]
        s_claim, s_kept = t.sem("claim"), t.sem("kept")
        oh, zero = t.sb("oh", [P, 2, J, P]), t.sb("zero", [1, 512], F16)
        prod, sh = t.sb("prod", [P, 2, J, H9, D]), t.sb("sh", [P, EC, H9])
        slots = t.sb("slots", [P, 2, GC, D])
        acc = t.ps("acc", [P, 512])
        with nc.Block() as block:
            @block.sync
            def _(e):
                e.dma_start(sh[:, :, :], harmonics).then_inc(s_load, 16)

            @block.gpsimd
            def _(e):
                node_gather(e, t, g, table, slots, s_slot, s_claim)

            @block.scalar
            def _(e):
                e.sem_inc(s_slot[0][1], 1)
                e.sem_inc(s_slot[1][1], 1)
                with e.Fori(0, GN, 1) as i:
                    for h in range(2):
                        e.wait_ge(s_slot[h][0], 16 * GC * (i + 1))
                        e.activation(G[:, ds((2 * i + h) * GC, GC), :], slots[:, h, :, :], ACT.Copy).then_inc(s_kept, 1)
                        e.wait_ge(s_kept, 2 * i + h + 1)
                        e.sem_inc(s_slot[h][1], 1)

            @block.vector
            def _(e):
                e.memset(zero[:, :], 0.0).then_inc(s_z, 1)
                e.wait_ge(s_load, 16)
                v = Count(e, "products_v", VISITS)
                e.sem_inc(s_ev, 1)
                with e.Fori(0, NB, 1) as b:
                    lo, hi = pair_range(e, g, b)
                    with e.Fori(lo, hi, 1) as u:
                        n = v.now()
                        for s in range(2):
                            e.wait_ge(s_used[s], n + 1)
                            c0 = u * JP + s * J
                            for j in range(J):
                                e.tensor_scalar(oh[:, s, j, :], g.ids[:, ds(b * P, P)], g.dst_c[:, ds(c0 + j, 1)], None,
                                                ALU.is_equal)
                            if s == 0:
                                e.wait_ge(s_kept, u + 1)
                            e.tensor_tensor(prod[:, s, :, :, :], bcast(G[:, ds(c0, J), :].unsqueeze(2), [P, J, H9, D]),
                                            bcast(sh[:, ds(c0, J), :].unsqueeze(3), [P, J, H9, D]), ALU.mult).then_inc(s_oh[s], 1)
                        v.up()
                    e.wait_ge(s_sum, b + 1)
                    e.tensor_copy(sums[:, ds(b, 1), :].rearrange("p a f -> p (a f)"), acc[:, 0:width]).then_inc(s_ev, 1)

            @block.tensor
            def _(e):
                e.wait_ge(s_z, 1)
                e.sem_inc(s_used[0], 1)
                e.sem_inc(s_used[1], 1)
                v = Count(e, "products_pe", VISITS)
                with e.Fori(0, NB, 1) as b:
                    lo, hi = pair_range(e, g, b)
                    e.wait_ge(s_ev, b + 1)
                    e.matmul(acc[:, 0:width], zero[0:1, 0:P], zero[0:1, 0:width], start=True, stop=False, skip_group_check=True)
                    with e.Fori(lo, hi, 1) as u:
                        n = v.now()
                        for s in range(2):
                            e.wait_ge(s_oh[s], n + 1)
                            for j in range(J):
                                m = e.matmul(acc[:, 0:width], oh[:, s, j, :], prod[:, s, j, :, :].rearrange("p c f -> p (c f)"),
                                             start=False, stop=False, skip_group_check=True)
                            m.then_inc(s_used[s], 1)
                        v.up()
                    e.matmul(acc[:, 0:1], zero[0:1, 0:P], zero[0:1, 0:1], start=False, stop=True,
                             skip_group_check=True).then_inc(s_sum, 1)


def next_layer(nc, g, a, stage, table, sums=None, mixed=None):
    with stage_tools(nc, stage) as t:
        s_v, s_a, s_out = t.sem("vector"), t.sem("scalar"), t.sem("stored")
        m, v, sq = t.sb("mean", [P, NB]), t.sb("var", [P, NB]), t.sb("sq", [P, NB, D])
        den, mix = t.sb("den", [P, NB]), t.sb("mix", [P, NB, D])
        with nc.Block() as block:
            root = [0, 0]

            @block.vector
            def _(e):
                c = Chain(e, s_v)
                if sums is not None:
                    c(e.tensor_scalar(den[:, :], sums[:, :, D], 1e-8, None, ALU.add))
                    c(e.reciprocal(den[:, :], den[:, :]))
                    c(e.tensor_tensor(mix[:, :, :], sums[:, :, 0:D], bcast(den[:, :].unsqueeze(2), [P, NB, D]), ALU.mult))
                    c(e.tensor_tensor(g.x[:, :, :], g.x[:, :, :], mix[:, :, :], ALU.add))
                if mixed is not None:
                    c(e.tensor_tensor(g.x[:, :, :], g.x[:, :, :], mixed[:, :, :], ALU.add))
                root[0] = c.n + 6
                layernorm_relu(e, c, lambda: e.wait_ge(s_a, 1), (m, v, sq[:, :, :]), g.x[:, :, :], g.h[:, :, :])
                root[1] = c.n

            @block.scalar
            def _(e):
                e.wait_ge(s_v, root[0])
                e.activation(v[:, :], v[:, :], ACT.Sqrt).then_inc(s_a, 1)

            @block.sync
            def _(e):
                if table is not None:
                    e.wait_ge(s_v, root[1])
                    e.dma_start(table.rearrange("(b p) f -> p b f", p=P), g.h[:, :, :]).then_inc(s_out, 16)
                    e.wait_ge(s_out, 16)


def mix_products(nc, g, a, sums, mixed):
    with stage_tools(nc, "mix") as t:
        s_load, s_w, s_pe, s_a, s_out, s_v = (t.sem(n) for n in ("loaded", "weights", "turned", "copied", "mixed", "kept"))
        wrep, cg = t.sb("wrep", [BW, 3, D]), t.sb("cg", [BW, 3, D])
        turned = t.sb("turned", [BW, 2, 3, P])
        pt = [t.ps(f"pt{i}", [BW, 3 * P]) for i in range(2)]
        po = [t.ps(f"po{i}", [P, D]) for i in range(2)]
        with nc.Block() as block:
            @block.sync
            def _(e):
                e.dma_start(wrep[:, :, :], a["W1_rep"].rearrange("(q r) o -> r q o", r=BW)).then_inc(s_load, 16)
                e.dma_start(cg[:, :, :], a["cg"].rearrange("(q r) o -> r q o", r=BW)).then_inc(s_load, 16)

            @block.vector
            def _(e):
                e.wait_ge(s_load, 32)
                e.tensor_tensor(wrep[:, :, :], wrep[:, :, :], cg[:, :, :], ALU.mult).then_inc(s_w, 1)
                for b in range(NB):
                    e.wait_ge(s_out, b + 1)
                    e.tensor_copy(mixed[:, b, :], po[b % 2][:, :]).then_inc(s_v, 1)

            @block.scalar
            def _(e):
                for b in range(NB):
                    e.wait_ge(s_pe, b + 1)
                    if b >= 2:
                        e.wait_ge(s_out, b - 1)
                    e.activation(turned[:, b % 2, :, :].rearrange("p q n -> p (q n)"), pt[b % 2][:, :], ACT.Copy).then_inc(s_a, 1)

            @block.tensor
            def _(e):
                e.wait_ge(s_w, 1)

                def mix(b):
                    e.wait_ge(s_a, b + 1)
                    if b >= 2:
                        e.wait_ge(s_v, b - 1)
                    for q in range(3):
                        m = e.matmul(po[b % 2][:, :], turned[:, b % 2, q, :], wrep[:, q, :], start=(q == 0), stop=(q == 2))
                    m.then_inc(s_out, 1)
                for b in range(NB):
                    if b >= 2:
                        e.wait_ge(s_a, b - 1)
                    for q in range(3):
                        m = e.transpose(pt[b % 2][:, q * P:(q + 1) * P], sums[:, b, q * BW:(q + 1) * BW], g.ident[:, :])
                    m.then_inc(s_pe, 1)
                    if b:
                        mix(b - 1)
                mix(NB - 1)


HID = 64
TAIL = N - (NB - 1) * P


def turn_counts(nc, g, dr, CT):
    SG = [(s, min(8, NB - s)) for s in range(0, NB, 8)]
    with stage_tools(nc, "turn") as t:
        s_ld = [t.sem(f"loaded{i}") for i in range(2)]
        s_t, s_ea, s_ev, s_one, s_deg, s_id = (t.sem(n) for n in ("turned", "copied_a", "copied_v", "ones", "degree", "diagonal"))
        row = t.sb("row", [P, 2, NP], F16)
        two = t.sb("two", [P, 1], F16)
        pt = [t.ps(f"pt{i}", [P, 8, P], F16) for i in range(4)]
        pd = t.ps("pd", [P, NB])
        zero = t.sb("zero", [1, P], F16)
        with nc.Block() as block:
            @block.sync
            def _(e):
                for b in range(NB):
                    if b >= 2:
                        e.wait_ge(s_t, 4 * (b - 1))
                    e.dma_start(row[:, b % 2, :], dr["counts"][b * P:(b + 1) * P, :]).then_inc(s_ld[b % 2], 16)

            @block.tensor
            def _(e):
                e.wait_ge(s_one, 2)
                e.matmul(pd[:, :], zero[0:1, :], zero[0:1, 0:NB], start=True, stop=False, skip_group_check=True)
                for b in range(NB):
                    e.wait_ge(s_ld[b % 2], 16 * (b // 2 + 1))
                    for k, (s0, n) in enumerate(SG):
                        if b:
                            e.wait_ge(s_ea if k % 2 else s_ev, 2 * b if k >= 2 else 2 * b - 1)
                        for s in range(s0, s0 + n):
                            e.matmul(pd[:, s:s + 1], row[:, b % 2, s * P:(s + 1) * P], two[:, :], start=False,
                                     stop=(b == NB - 1), skip_group_check=True)
                        for s in range(s0, s0 + n):
                            m = e.transpose(pt[k][:, s - s0, :], row[:, b % 2, s * P:(s + 1) * P], g.ident16[:, :])
                        m.then_inc(s_t, 1)

            @block.vector
            def _(e):
                e.memset(zero[:, :], 0.0).then_inc(s_one, 1)
                e.memset(two[:, :], 2.0).then_inc(s_one, 1)
                for b in range(NB):
                    w = min(P, N - b * P)
                    for k in (0, 2):
                        s0, n = SG[k]
                        e.wait_ge(s_t, 4 * b + k + 1)
                        e.tensor_copy(CT[:, s0:s0 + n, b * P:b * P + w], pt[k][:, 0:n, 0:w]).then_inc(s_ev, 1)
                e.wait_ge(s_ev, 2 * NB)
                e.wait_ge(s_ea, 2 * NB)
                for s in range(NB):
                    w = min(P, N - s * P)
                    d = CT[:, s, s * P:s * P + w]
                    e.scalar_tensor_tensor(d, g.ident16[:, 0:w], 0.5, d, ALU.mult, ALU.add).then_inc(s_id, 1)
                e.tensor_copy(g.deg_out[:, :], pd[:, :]).then_inc(s_id, 1)
                e.tensor_scalar(g.dis[:, :], g.deg[:, :], 1.0, None, ALU.add).then_inc(s_deg, 1)
                e.wait_ge(s_deg, 2)
                e.reciprocal(g.dis[:, :], g.dis[:, :]).then_inc(s_deg, 1)
                e.wait_ge(s_id, NB + 1)

            @block.scalar
            def _(e):
                for b in range(NB):
                    w = min(P, N - b * P)
                    for k in (1, 3):
                        s0, n = SG[k]
                        e.wait_ge(s_t, 4 * b + k + 1)
                        e.activation(CT[:, s0:s0 + n, b * P:b * P + w], pt[k][:, 0:n, 0:w], ACT.Copy).then_inc(s_ea, 1)
                e.wait_ge(s_deg, 1)
                e.activation(g.dis[:, :], g.dis[:, :], ACT.Sqrt).then_inc(s_deg, 1)


def gcn(nc, g, stage, CT, z, fin, weights, outs):
    fo = sum(w.shape[1] for w in weights)
    with stage_tools(nc, stage) as t:
        s_v, s_a, s_w, s_agg, s_ev, s_y, s_yv = (t.sem(n) for n in (
            "vector", "scalar", "weights", "aggregated", "copied", "mixed", "used"))
        zs = t.sb("zs", [P, NB, fin])
        parts = t.sb("parts", [P, NB, 2 * fin], F16)
        W = t.sb("W", [2 * fin, fo])
        bias = t.sb("bias", [P, fo])
        agg = t.sb("agg", [2 * fin, 2, 512])
        pa = [t.ps(f"pa{i}", [2 * fin, 512]) for i in range(2)]
        py = [t.ps(f"py{i}", [P, 4, fo]) for i in range(2)]
        yv = t.sb("yv", [P, 2, 4, fo])
        nload = 3 * len(weights)
        with nc.Block() as block:
            @block.sync
            def _(e):
                c = 0
                for w, (b, _, _) in zip(weights, outs):
                    n = w.shape[1]
                    e.dma_start(W[0:fin, c:c + n], w).then_inc(s_w, 16)
                    e.dma_start(W[fin:2 * fin, c:c + n], w).then_inc(s_w, 16)
                    e.dma_start(bias[:, c:c + n], b.unsqueeze(0).partition_broadcast(P)).then_inc(s_w, 16)
                    c += n

            @block.vector
            def _(e):
                c = Chain(e, s_v)
                c(e.scalar_tensor_tensor(zs[:, :, :], z, 2.0, bcast(g.dis[:, :].unsqueeze(2), [P, NB, fin]), ALU.mult, ALU.mult))
                e.wait_ge(s_a, 1)
                c(e.tensor_tensor(zs[:, :, :], zs[:, :, :], parts[:, :, 0:fin], ALU.subtract))
                e.wait_ge(s_w, 16 * nload)
                c(e.tensor_scalar(W[fin:2 * fin, :], W[fin:2 * fin, :], 1.0 / LOW, None, ALU.mult))
                for _, h, add in outs:
                    if not add:
                        c(e.memset(h[:, NB - 1, :], 0.0))
                for k, n in enumerate(DC):
                    rows, nb = (P, n // P) if n >= P else (n, 1)
                    e.wait_ge(s_y, k + 1)
                    y = yv[0:rows, k % 2, 0:nb, :]
                    e.tensor_tensor(y, py[k % 2][0:rows, 0:nb, :],
                                    bcast(g.dis[0:rows, 4 * k:4 * k + nb].unsqueeze(2), [rows, nb, fo]), ALU.mult).then_inc(s_yv, 1)
                    e.wait_ge(s_yv, k + 1)
                    o = 0
                    for _, h, add in outs:
                        w = h.shape[2]
                        d = h[0:rows, 4 * k:4 * k + nb, :]
                        if add:
                            c(e.tensor_tensor(d, d, yv[0:rows, k % 2, 0:nb, o:o + w], ALU.add))
                            c(e.tensor_tensor(d, d, bcast(bias[0:rows, o:o + w].unsqueeze(1), [rows, nb, w]), ALU.add))
                        else:
                            c(e.tensor_tensor(d, yv[0:rows, k % 2, 0:nb, o:o + w],
                                              bcast(bias[0:rows, o:o + w].unsqueeze(1), [rows, nb, w]), ALU.add))
                        o += w

            @block.scalar
            def _(e):
                e.wait_ge(s_v, 1)
                e.activation(parts[:, :, 0:fin], zs[:, :, :], ACT.Copy).then_inc(s_a, 1)
                e.wait_ge(s_v, 2)
                e.activation(parts[:, :, fin:], zs[:, :, :], ACT.Copy, scale=LOW).then_inc(s_a, 1)
                for k, n in enumerate(DC):
                    e.wait_ge(s_agg, k + 1)
                    if k >= 2:
                        e.wait_ge(s_y, k - 1)
                    e.activation(agg[:, k % 2, 0:n], pa[k % 2][:, 0:n], ACT.Copy).then_inc(s_ev, 1)

            @block.tensor
            def _(e):
                e.wait_ge(s_a, 2)
                e.wait_ge(s_v, 3)

                def mix(k):
                    n = DC[k]
                    rows, nb = (P, n // P) if n >= P else (n, 1)
                    e.wait_ge(s_ev, k + 1)
                    if k >= 2:
                        e.wait_ge(s_yv, k - 1)
                    for i in range(nb):
                        m = e.matmul(py[k % 2][0:rows, i, :], agg[:, k % 2, i * P:i * P + rows], W[:, :], start=True, stop=True)
                    m.then_inc(s_y, 1)
                for k, n in enumerate(DC):
                    if k >= 2:
                        e.wait_ge(s_ev, k - 1)
                    for s in range(NB):
                        m = e.matmul(pa[k % 2][:, 0:n], parts[:, s, :], CT[:, s, 512 * k:512 * k + n],
                                     start=(s == 0), stop=(s == NB - 1))
                    m.then_inc(s_agg, 1)
                    if k:
                        mix(k - 1)
                mix(len(DC) - 1)


def batchnorm(nc, g, stage, h, w, gamma, beta, into, add):
    with stage_tools(nc, stage) as t:
        s_v, s_a, s_pe, s_ld = t.sem("vector"), t.sem("scalar"), t.sem("tensor"), t.sem("loaded")
        part, part2 = t.sb("part", [P, w]), t.sb("part2", [P, w])
        mean, var = t.sb("mean", [P, w]), t.sb("var", [P, w])
        ga, be = t.sb("gamma", [P, w]), t.sb("beta", [P, w])
        sq = t.sb("sq", [P, NB, w])
        pm, pv = t.ps("pm", [P, w]), t.ps("pv", [P, w])
        with nc.Block() as block:
            @block.sync
            def _(e):
                e.dma_start(ga[:, :], gamma.unsqueeze(0).partition_broadcast(P)).then_inc(s_ld, 16)
                e.dma_start(be[:, :], beta.unsqueeze(0).partition_broadcast(P)).then_inc(s_ld, 16)

            @block.vector
            def _(e):
                c = Chain(e, s_v)
                full = lambda v: bcast(v[:, :].unsqueeze(1), [P, NB, w])
                c(e.tensor_reduce(part[:, :], h.rearrange("p b f -> p f b"), X, ALU.add))
                e.wait_ge(s_pe, 1)
                c(e.tensor_scalar(mean[:, :], pm[:, :], 1.0 / N, None, ALU.mult))
                c(e.tensor_tensor(h, h, full(mean), ALU.subtract))
                c(e.tensor_tensor(sq[:, :, :], h, h, ALU.mult))
                c(e.tensor_reduce(part2[:, :], sq[:, 0:NB - 1, :].rearrange("p b f -> p f b"), X, ALU.add))
                e.wait_ge(s_pe, 2)
                c(e.tensor_scalar(var[:, :], pv[:, :], 1.0 / N, EPS, ALU.mult, ALU.add))
                e.wait_ge(s_a, 1)
                e.wait_ge(s_ld, 32)
                c(e.reciprocal(var[:, :], var[:, :]))
                c(e.tensor_tensor(var[:, :], var[:, :], ga[:, :], ALU.mult))
                c(e.tensor_tensor(h, h, full(var), ALU.mult))
                c(e.tensor_tensor(h, h, full(be), ALU.add))
                c(e.scalar_tensor_tensor(into, h, 0.0, add, ALU.max, ALU.add))

            @block.scalar
            def _(e):
                e.wait_ge(s_v, 6)
                e.activation(var[:, :], var[:, :], ACT.Sqrt).then_inc(s_a, 1)

            @block.tensor
            def _(e):
                e.wait_ge(s_v, 1)
                e.matmul(pm[:, :], g.ones[:, :], part[:, :], start=True, stop=True).then_inc(s_pe, 1)
                e.wait_ge(s_v, 5)
                e.matmul(pv[:, :], g.ones[:, :], part2[:, :], start=True, stop=False)
                e.matmul(pv[:, :], g.ones[0:TAIL, :], sq[0:TAIL, NB - 1, :], start=False, stop=True).then_inc(s_pe, 1)


def linear(nc, g, stage, z, fin, w, b, res, relu=False):
    fo = w.shape[1]
    nload = 16 if b is None else 32
    with stage_tools(nc, stage) as t:
        s_ld, s_t, s_a, s_y, s_v = (t.sem(n) for n in ("loaded", "turned", "copied", "mixed", "vector"))
        W, bias = t.sb("W", [fin, fo]), t.sb("bias", [P, fo])
        zt = t.sb("zt", [fin, 2, P])
        pt = [t.ps(f"pt{i}", [fin, P]) for i in range(2)]
        py = [t.ps(f"py{i}", [P, fo]) for i in range(2)]
        with nc.Block() as block:
            @block.sync
            def _(e):
                e.dma_start(W[:, :], w).then_inc(s_ld, 16)
                if b is not None:
                    e.dma_start(bias[:, :], b.unsqueeze(0).partition_broadcast(P)).then_inc(s_ld, 16)

            @block.tensor
            def _(e):
                e.wait_ge(s_ld, nload)

                def mix(k):
                    e.wait_ge(s_a, k + 1)
                    if k >= 2:
                        e.wait_ge(s_v, k - 1)
                    e.matmul(py[k % 2][:, :], zt[:, k % 2, :], W[:, :], start=True, stop=True).then_inc(s_y, 1)
                for k in range(NB):
                    if k >= 2:
                        e.wait_ge(s_a, k - 1)
                    e.transpose(pt[k % 2][:, :], z[:, k, :], g.ident[:, :]).then_inc(s_t, 1)
                    if k:
                        mix(k - 1)
                mix(NB - 1)

            @block.scalar
            def _(e):
                for k in range(NB):
                    e.wait_ge(s_t, k + 1)
                    if k >= 2:
                        e.wait_ge(s_y, k - 1)
                    e.activation(zt[:, k % 2, :], pt[k % 2][:, :], ACT.Relu if relu else ACT.Copy).then_inc(s_a, 1)

            @block.vector
            def _(e):
                e.wait_ge(s_ld, nload)
                for k in range(NB):
                    e.wait_ge(s_y, k + 1)
                    if b is None:
                        e.tensor_copy(res[:, k, :], py[k % 2][:, :]).then_inc(s_v, 1)
                    else:
                        e.tensor_tensor(res[:, k, :], py[k % 2][:, :], bias[:, :], ALU.add).then_inc(s_v, 1)


def residual_gcn(nc, g, a, dr):
    with stage_tools(nc, "l2") as t:
        CT = t.sb("CT", [P, NB, N], F16)
        turn_counts(nc, g, dr, CT)
        A, B, M = t.sb("A", [P, NB, HID]), t.sb("B", [P, NB, HID]), t.sb("M", [P, NB, HID])
        Av, Bv, Mv = A[:, :, :], B[:, :, :], M[:, :, :]
        W, gm, bt = a["W_hid"], a["gamma_hid"], a["beta_hid"]
        bh = a["b_hid"]
        h = g.h[:, :, :]
        linear(nc, g, "enc1_res", h, D, a["Wres_enc1"], a["bres_enc1"], Bv)
        gcn(nc, g, "enc1", CT, h, D, [a["W_enc1"]], [(a["b_enc1"], Av, False)])
        batchnorm(nc, g, "enc1_bn", Av, HID, gm[0], bt[0], Bv, Bv)
        gcn(nc, g, "enc2", CT, Bv, HID, [W[0], W[2]], [(bh[0], Av, False), (bh[2], Mv, False)])
        batchnorm(nc, g, "enc2_bn", Av, HID, gm[1], bt[1], Bv, Bv)
        gcn(nc, g, "enc3", CT, Bv, HID, [W[1], W[3]], [(bh[1], Av, False), (bh[3], Mv, True)])
        batchnorm(nc, g, "enc3_bn", Av, HID, gm[2], bt[2], Bv, Bv)
        gcn(nc, g, "mid", CT, Bv, HID, [W[4]], [(bh[4], Mv, True)])
        gcn(nc, g, "dec1", CT, Mv, HID, [W[5]], [(bh[5], Av, False)])
        batchnorm(nc, g, "dec1_bn", Av, HID, gm[3], bt[3], Mv, Mv)
        linear(nc, g, "dec2_res", Mv, HID, a["Wres_dec2"], a["bres_dec2"], B[:, :, 0:D])
        gcn(nc, g, "dec2", CT, Mv, HID, [a["W_dec2"]], [(a["b_dec2"], A[:, :, 0:D], False)])
        batchnorm(nc, g, "dec2_bn", A[:, :, 0:D], D, a["gamma_out"][0], a["beta_out"][0], B[:, :, 0:D], B[:, :, 0:D])
        gcn(nc, g, "dec3", CT, B[:, :, 0:D], D, [a["W_dec3"]], [(a["b_dec3"], A[:, :, 0:D], False)])
        batchnorm(nc, g, "dec3_bn", A[:, :, 0:D], D, a["gamma_out"][1], a["beta_out"][1], A[:, :, HID - D:], B[:, :, 0:D])
        next_layer(nc, g, a, "layer3", dr["table1"], mixed=A[:, :, HID - D:])


ED = 16
FH = 2 * HID


def edge_flows(nc, g, a, dr, sums):
    bf = mybir.dt.bfloat16
    with stage_tools(nc, "flow") as t:
        s_in = [t.sem(f"inputs{s}") for s in range(SL)]
        s_pre = [t.sem(f"added{s}") for s in range(SL)]
        s_mask, s_mused, s_oh, s_oused = ([t.sem(f"{n}{s}") for s in range(SL)] for n in (
            "mask", "mask_used", "onehot", "onehot_used"))
        s_ph, s_act, s_lo = (t.sem(n) for n in ("parts", "relu", "low"))
        s_hfree, s_st, s_stf, s_idx, s_claim, s_z, s_sum, s_ev, s_ld = (t.sem(n) for n in (
            "hidden_used", "stored", "place", "idx", "claim", "zeros", "summed", "copied", "weights"))
        s_turn = t.sem("turn")
        idx = t.sb("idx", [P, SL, JP], I32)
        rows = t.sb("rows", [P, SL, JP, FH])
        dstb, xin = t.sb("dstb", [P, SL, PS], F16), t.sb("xin", [P, SL, JP, P])
        W, zero = t.sb("W", [P, FH]), t.sb("zero", [1, 512], bf)
        mask, oh = t.sb("mask", [P, SL, JP, P], bf), t.sb("oh", [P, SL, JP, P])
        pre, hid, r2 = t.sb("pre", [P, 2, JP, FH]), t.sb("hid", [P, 2, JP, HID]), t.sb("r2", [P, 2, JP, HID])
        hl = t.sb("hl", [P, 2, JP, FH], F16)
        ph = [t.ps(f"ph{i}", [P, JP, FH]) for i in range(2)]
        SB = -(-NB * HID // 512)
        acc = t.ps("acc", [P, SB * 512])
        with nc.Block() as block:
            @block.gpsimd
            def _(e):
                def step(i, s, last):
                    e.wait_ge(s_pre[s], i + 1)
                    e.sem_inc(s_claim, 1)
                    e.tensor_copy(idx[:, s, :], g.src_i[:, ds((i * SL + s) * JP, JP)]).then_inc(s_idx, 1)
                    e.wait_ge(s_idx, i * SL + s + 1)
                    e.sem_inc(s_claim, 1)
                    for j in range(JP):
                        e.indirect_dma_start(rows[:, s, j, :], None, dr["table3"],
                                             bass.IndirectOffsetOnAxis(ap=idx[:, s, j:j + 1].bitcast(U32), axis=0)
                                             ).then_inc(g.rows_landed[2][s], 16)
                pairs(e, step)

            @block.sync
            def _(e):
                e.wait_ge(s_z, 3)
                e.dma_start(W[0:ED, :], a["Wf1_edge"]).then_inc(s_ld, 16)

                def load(tt, s):
                    e.dma_start(dstb[:, s, :], dr["dst16"][ds(tt, 1), :].partition_broadcast(P)).then_inc(s_in[s], 16)
                    e.dma_start(xin[0:ED, s, :, :], a["edge_attr_16"][ds(tt, 1), :, :, :]
                                .rearrange("a k j p -> (a k) j p")).then_inc(s_in[s], 16)

                def store(tt, s):
                    e.wait_ge(s_lo, tt + 3)
                    e.dma_start(dr["hidden"][ds(tt, 1), :, :].rearrange("a p n -> (a p) n"),
                                hl[:, s % 2, :, :].rearrange("p j f -> p (j f)")).then_inc(s_st, 16)

                def stored(tt):
                    e.wait_ge(s_st, 16 * (tt + 1))
                    e.sem_inc(s_stf, 1)
                e.sem_inc(s_stf, 2)
                for s in range(SL):
                    load(s, s)

                def step(i, s, last):
                    if not last:
                        e.wait_ge(s_ph, i * SL + s + 1)
                        load((i + 1) * SL + s, s)
                    store(i * SL + s, s)
                    stored(i * SL + s)
                pairs(e, step)

            @block.vector
            def _(e):
                e.memset(zero[:, :], 0.0).then_inc(s_z, 1)
                e.memset(xin[:, :, :, :], 0.0).then_inc(s_z, 1)
                e.memset(W[:, :], 0.0).then_inc(s_z, 1)
                for s in range(SL):
                    e.sem_inc(s_pre[s], 1)
                e.sem_inc(s_lo, 2)
                vm, vo = ([Count(e, f"flow_{n}{s}", VISITS) for s in range(SL)] for n in ("masks", "onehots"))
                own = [Range(e, f"flow_v{s}") for s in range(SL)]

                def masks(i, s):
                    e.wait_ge(s_in[s], i * 32 + 32)
                    with own[s].blocks() as b:
                        n = vm[s].now()
                        e.wait_ge(s_mused[s], n + 1)
                        e.tensor_scalar(mask[:, s, :, :], dstb[:, s, :].rearrange("p (j n) -> p j n", j=JP), g.node_c[:, ds(b, 1)],
                                        None, ALU.is_equal).then_inc(s_mask[s], 1)
                        vm[s].up()

                def step(i, s, last):
                    tt = i * SL + s
                    if not last or s < SL - 1:
                        masks(*((i, s + 1) if s < SL - 1 else (i + 1, 0)))
                    e.wait_ge(s_ph, tt + 1)
                    e.wait_ge(g.rows_landed[2][s], 16 * JP * (i + 1))
                    e.wait_ge(s_act, tt * 3 + 3)
                    e.tensor_tensor(pre[:, s % 2, :, :], ph[s % 2][:, :, :], rows[:, s, :, :], ALU.add).then_inc(s_pre[s], 1)
                    with own[s].blocks() as b:
                        n = vo[s].now()
                        e.wait_ge(s_oused[s], n + 1)
                        for j in range(JP):
                            m = e.tensor_scalar(oh[:, s, j, :], g.ids[:, ds(b * P, P)], g.dst_c[:, ds(tt * JP + j, 1)],
                                                None, ALU.is_equal)
                        m.then_inc(s_oh[s], 1)
                        vo[s].up()
                    if not last:
                        own[s].load(g, (i + 1) * SL + s, s_turn)
                    e.wait_ge(s_act, tt * 3 + 9)
                    e.scalar_tensor_tensor(hl[:, s % 2, :, HID:], hl[:, s % 2, :, 0:HID], -LOW, r2[:, s % 2, :, :],
                                           ALU.mult, ALU.add).then_inc(s_lo, 1)
                for s in range(SL):
                    own[s].load(g, s, s_turn)
                masks(0, 0)
                pairs(e, step)

            @block.scalar
            def _(e):
                e.sem_inc(s_act, 6)

                def step(i, s, last):
                    tt = i * SL + s
                    e.wait_ge(s_stf, tt + 1)
                    e.wait_ge(s_lo, tt + 1)
                    e.wait_ge(s_hfree, tt + 1)
                    e.wait_ge(s_pre[s], i + 2)
                    e.activation(hl[:, s % 2, :, 0:HID], pre[:, s % 2, :, HID:], ACT.Relu).then_inc(s_act, 1)
                    e.activation(r2[:, s % 2, :, :], pre[:, s % 2, :, HID:], ACT.Relu, scale=LOW).then_inc(s_act, 1)
                    e.activation(hid[:, s % 2, :, :], pre[:, s % 2, :, 0:HID], ACT.Relu).then_inc(s_act, 1)
                pairs(e, step)
                e.wait_ge(s_sum, 1)
                e.activation(sums[:, :, :], acc[:, 0:NB * HID].rearrange("p (b f) -> p b f", f=HID), ACT.Copy).then_inc(s_ev, 1)
                e.wait_ge(s_ev, 1)

            @block.tensor
            def _(e):
                e.wait_ge(s_z, 3)
                e.wait_ge(s_ld, 16)
                for s in range(SL):
                    e.sem_inc(s_mused[s], 1)
                    e.sem_inc(s_oused[s], 1)
                e.sem_inc(s_hfree, 2)
                for k in range(SB):
                    e.matmul(acc[:, 512 * k:512 * k + 512], zero[0:1, 0:P], zero[0:1, :], start=True, stop=False,
                             skip_group_check=True)
                vm, vo = ([Count(e, f"flow_{n}{s}", VISITS) for s in range(SL)] for n in ("picks", "sums"))
                own = [Range(e, f"flow_pe{s}") for s in range(SL)]

                def parts(i, s):
                    e.wait_ge(s_in[s], i * 32 + 32)
                    e.wait_ge(s_pre[s], i + 1)
                    for j in range(JP):
                        e.matmul(ph[s % 2][:, j, :], xin[:, s, j, :], W[:, :], start=(j % J == 0), stop=False, skip_group_check=True)
                    with own[s].blocks() as b:
                        n = vm[s].now()
                        e.wait_ge(s_mask[s], n + 1)
                        for j in range(JP):
                            for k in range(3):
                                m = e.matmul(ph[s % 2][:, j, :], mask[:, s, j, :],
                                             g.pd3[:, ds(b, 1), k, :].rearrange("p a f -> p (a f)"),
                                             start=False, stop=False, skip_group_check=True)
                        m.then_inc(s_mused[s], 1)
                        vm[s].up()
                    e.matmul(ph[s % 2][:, JP - 1, 0:1], zero[0:1, 0:P], zero[0:1, 0:1], start=False, stop=True,
                             skip_group_check=True).then_inc(s_ph, 1)

                def step(i, s, last):
                    tt = i * SL + s
                    if not last or s < SL - 1:
                        parts(*((i, s + 1) if s < SL - 1 else (i + 1, 0)))
                    e.wait_ge(s_act, tt * 3 + 9)
                    with own[s].blocks() as b:
                        n = vo[s].now()
                        e.wait_ge(s_oh[s], n + 1)
                        for j in range(JP):
                            m = e.matmul(acc[:, ds(b * HID, HID)], oh[:, s, j, :], hid[:, s % 2, j, :], start=False, stop=False,
                                         skip_group_check=True)
                        m.then_inc(s_oused[s], 1)
                        vo[s].up()
                    if not last:
                        own[s].load(g, (i + 1) * SL + s, s_turn)
                    e.wait_ge(s_oused[s], vo[s].now() + 1)
                    e.sem_inc(s_hfree, 1)
                for s in range(SL):
                    own[s].load(g, s, s_turn)
                parts(0, 0)
                pairs(e, step)
                e.matmul(acc[:, 0:1], zero[0:1, 0:P], zero[0:1, 0:1], start=False, stop=True,
                         skip_group_check=True).then_inc(s_sum, 1)


def backward_sums(nc, g, a, dr, back):
    with stage_tools(nc, "back") as t:
        s_ld = [t.sem(f"loaded{i}") for i in range(SL)]
        s_free = [t.sem(f"free{i}") for i in range(SL)]
        s_oh, s_used, s_z, s_sum, s_ev = (t.sem(n) for n in ("onehot", "used", "zeros", "summed", "copied"))
        hl = t.sb("hl", [P, SL, JP * FH], F16)
        ohs = t.sb("ohs", [P, J, NP], F16)
        zero = t.sb("zero", [1, 512], F16)
        acc = t.ps("acc", [P, CB, 512])
        with nc.Block() as block:
            @block.sync
            def _(e):
                def step(i, s, last):
                    e.wait_ge(s_free[s], i + 1)
                    e.dma_start(hl[:, s, :], dr["hidden"][ds(i * SL + s, 1), :, :].rearrange("a p n -> (a p) n")).then_inc(s_ld[s], 16)
                pairs(e, step)

            @block.vector
            def _(e):
                e.memset(zero[:, :], 0.0).then_inc(s_z, 1)

                def step(i, s, last):
                    for j in range(JP):
                        c = (i * SL + s) * JP + j
                        e.wait_ge(s_used, c + 1)
                        e.tensor_scalar(ohs[:, j % J, 0:N + 1], g.ids16[:, 0:N + 1], g.src_f[:, ds(c, 1)], None,
                                        ALU.is_equal).then_inc(s_oh, 1)
                pairs(e, step)
                e.memset(back[:, N:NP], 0.0).then_inc(s_z, 1)

            @block.tensor
            def _(e):
                e.wait_ge(s_z, 1)
                for s in range(SL):
                    e.sem_inc(s_free[s], 1)
                e.sem_inc(s_used, J)
                for k, w in enumerate(DC):
                    e.matmul(acc[:, k, 0:w], zero[0:1, 0:P], zero[0:1, 0:w], start=True, stop=False, skip_group_check=True)

                def step(i, s, last):
                    e.wait_ge(s_ld[s], 16 * i + 16)
                    for j in range(JP):
                        c = (i * SL + s) * JP + j
                        e.wait_ge(s_oh, c + 1)
                        for k, w in enumerate(DC):
                            m = e.matmul(acc[:, k, 0:w], hl[:, s, j * FH:(j + 1) * FH], ohs[:, j % J, 512 * k:512 * k + w],
                                         start=False, stop=False, skip_group_check=True)
                        m.then_inc(s_used, 1)
                    e.wait_ge(s_used, (i * SL + s) * JP + JP + J)
                    e.sem_inc(s_free[s], 1)
                pairs(e, step)
                e.matmul(acc[:, CB - 1, 0:1], zero[0:1, 0:P], zero[0:1, 0:1], start=False, stop=True,
                         skip_group_check=True).then_inc(s_sum, 1)

            @block.scalar
            def _(e):
                e.wait_ge(s_sum, 1)
                for k, w in enumerate(DC):
                    e.activation(back[:, 512 * k:512 * k + w], acc[:, k, 0:w], ACT.Copy).then_inc(s_ev, 1)
                e.wait_ge(s_ev, CB)


def node_flows(nc, g, a, fwd, back, res):
    with stage_tools(nc, "node_flow") as t:
        s_ld, s_t, s_a, s_y, s_v, s_w = (t.sem(n) for n in ("loaded", "turned", "copied", "mixed", "vector", "weights"))
        W, bias = t.sb("W", [FH, HID]), t.sb("bias", [P, HID])
        deg = t.sb("deg", [P, NB])
        zt = t.sb("zt", [HID, 2, P])
        pt = [t.ps(f"pt{i}", [HID, P]) for i in range(2)]
        py = [t.ps(f"py{i}", [P, HID]) for i in range(2)]
        with nc.Block() as block:
            @block.sync
            def _(e):
                e.dma_start(W[0:HID, :], a["Wf2"]).then_inc(s_ld, 16)
                e.dma_start(W[HID:, :], a["Wf2"]).then_inc(s_ld, 16)
                e.dma_start(bias[:, :], a["bf2"].unsqueeze(0).partition_broadcast(P)).then_inc(s_ld, 16)

            @block.vector
            def _(e):
                e.wait_ge(s_ld, 48)
                e.tensor_scalar(W[HID:, :], W[HID:, :], 1.0 / LOW, None, ALU.mult).then_inc(s_w, 1)
                e.tensor_tensor(deg[:, :], g.deg[:, :], g.deg_out[:, :], ALU.add).then_inc(s_w, 1)
                e.wait_ge(s_w, 2)
                for k in range(NB):
                    e.wait_ge(s_y, k + 1)
                    e.scalar_tensor_tensor(res[:, k, :], bias[:, :], deg[:, k:k + 1], py[k % 2][:, :], ALU.mult, ALU.add).then_inc(s_v, 1)

            @block.tensor
            def _(e):
                e.wait_ge(s_w, 1)

                def mix(k):
                    e.wait_ge(s_a, k + 1)
                    if k >= 2:
                        e.wait_ge(s_v, k - 1)
                    e.matmul(py[k % 2][:, :], zt[:, k % 2, :], W[0:HID, :], start=True, stop=False)
                    e.matmul(py[k % 2][:, :], back[:, k * P:(k + 1) * P], W[:, :], start=False, stop=True).then_inc(s_y, 1)
                for k in range(NB):
                    if k >= 2:
                        e.wait_ge(s_a, k - 1)
                    e.transpose(pt[k % 2][:, :], fwd[:, k, :], g.ident[:, :]).then_inc(s_t, 1)
                    if k:
                        mix(k - 1)
                mix(NB - 1)

            @block.scalar
            def _(e):
                for k in range(NB):
                    e.wait_ge(s_t, k + 1)
                    if k >= 2:
                        e.wait_ge(s_y, k - 1)
                    e.activation(zt[:, k % 2, :], pt[k % 2][:, :], ACT.Copy).then_inc(s_a, 1)


def pointwise(nc, stage, ins):
    with stage_tools(nc, stage) as t:
        s_v = t.sem("vector")
        with nc.Block() as block:
            @block.vector
            def _(e):
                ins(e).then_inc(s_v, 1)
                e.wait_ge(s_v, 1)


def flow_layer(nc, g, a, dr):
    bf = mybir.dt.bfloat16
    with stage_tools(nc, "l3") as t:
        s_ld, s_v, s_ids, s_st = t.sem("loaded"), t.sem("vector"), t.sem("ids"), t.sem("stored")
        g.src_i, g.dst_c, g.src_f = t.sb("src_i", [P, EC], I32), t.sb("dst_c", [P, EC]), t.sb("src_f", [P, EC])
        g.ids, g.ids16, g.pd3 = t.sb("ids", [P, NP]), t.sb("ids16", [P, NP], F16), t.sb("pd3", [P, NB, 3, FH], bf)
        sums, res = t.sb("sums", [P, NB, HID]), t.sb("res", [P, NB, HID])
        with ExitStack() as c1:
            t1 = Tools(nc, c1, "l3a")
            PD, src_part, pad = t1.sb("PD", [P, NB, FH]), t1.sb("src_part", [P, NB, FH]), t1.sb("pad", [P, EC])
            dst_i = t1.sb("dst_i", [P, EC], I32)
            linear(nc, g, "flow_src", g.h[:, :, :], D, a["Wf1_src"], None, src_part)
            linear(nc, g, "flow_dst", g.h[:, :, :], D, a["Wf1_dst"], a["bf1_twice"], PD)
            with nc.Block() as block:
                @block.sync
                def _(e):
                    e.dma_start(g.src_i[:, :], a["src"]).then_inc(s_ld, 16)
                    e.dma_start(dst_i[:, :], a["dst"]).then_inc(s_ld, 16)
                    e.dma_start(dr["table3"].rearrange("(b p) f -> p b f", p=P), src_part[:, :, :]).then_inc(s_st, 16)
                    e.wait_ge(s_st, 16)

                @block.gpsimd
                def _(e):
                    e.iota(g.ids[:, :], [[1, NP]], base=-HALF, channel_multiplier=0,
                           allow_small_or_imprecise_dtypes=True).then_inc(s_ids, 1)

                @block.vector
                def _(e):
                    c = Chain(e, s_v)
                    e.wait_ge(s_ld, 32)
                    c(e.tensor_copy(g.dst_c[:, :], dst_i[:, :]))
                    c(e.tensor_scalar(g.dst_c[:, :], g.dst_c[:, :], -float(HALF), None, ALU.add))
                    c(e.tensor_copy(g.src_f[:, :], g.src_i[:, :]))
                    c(e.tensor_scalar(g.src_f[:, :], g.src_f[:, :], -float(HALF), None, ALU.add))
                    e.wait_ge(s_ids, 1)
                    c(e.tensor_copy(g.ids16[:, :], g.ids[:, :]))
                    c(e.tensor_scalar(pad[:, :], g.dst_c[:, :], float(HALF), 2.0 * NP, ALU.is_ge, ALU.mult))
                    c(e.tensor_tensor(g.src_f[:, :], g.src_f[:, :], pad[:, :], ALU.add))
                    c(e.tensor_copy(g.pd3[:, :, 0, :], PD[:, :, :]))
                    c(e.tensor_tensor(PD[:, :, :], PD[:, :, :], g.pd3[:, :, 0, :], ALU.subtract))
                    c(e.tensor_copy(g.pd3[:, :, 1, :], PD[:, :, :]))
                    c(e.tensor_tensor(PD[:, :, :], PD[:, :, :], g.pd3[:, :, 1, :], ALU.subtract))
                    c(e.tensor_copy(g.pd3[:, :, 2, :], PD[:, :, :]))
        edge_flows(nc, g, a, dr, sums)
        with ExitStack() as c2:
            back = Tools(nc, c2, "l3b").sb("back", [P, NP])
            backward_sums(nc, g, a, dr, back)
            node_flows(nc, g, a, sums, back, res)
        linear(nc, g, "node1", res[:, :, :], HID, a["Wn1"], a["bn1"], sums)
        linear(nc, g, "node2", sums[:, :, :], HID, a["Wn2"], a["bn2"], res[:, :, 0:D], relu=True)
        pointwise(nc, "last_add", lambda e: e.tensor_tensor(g.x[:, :, :], g.x[:, :, :], res[:, :, 0:D], ALU.add))


def cg_tables():
    import math
    combos = [(0, 0, 0), (0, 1, 1), (1, 0, 1), (1, 1, 0), (1, 1, 1), (2, 1, 1)]

    def coeff(j1, m1, j2, m2, j3, m3):
        if m3 != m1 + m2:
            return 0.0
        f = math.factorial
        pref = (2 * j3 + 1) * f(j3 + j1 - j2) * f(j3 - j1 + j2) * f(j1 + j2 - j3) / f(j1 + j2 + j3 + 1)
        pref *= f(j3 + m3) * f(j3 - m3) * f(j1 - m1) * f(j1 + m1) * f(j2 - m2) * f(j2 + m2)
        s = 0.0
        for v in range(max(0, j2 - j3 - m1, j1 + m2 - j3), min(j1 + j2 - j3, j1 - m1, j2 + m2) + 1):
            s += (-1) ** v / (f(v) * f(j1 + j2 - j3 - v) * f(j1 - m1 - v) * f(j2 + m2 - v) * f(j3 - j2 + m1 + v) * f(j3 - j1 - m2 + v))
        return math.sqrt(pref) * s

    def qmat(l):
        q = np.zeros((2 * l + 1, 2 * l + 1), dtype=np.complex128)
        for m in range(-l, 0):
            q[l + m, l + abs(m)] = 1 / np.sqrt(2)
            q[l + m, l - abs(m)] = -1j / np.sqrt(2)
        q[l, l] = 1.0
        for m in range(1, l + 1):
            q[l + m, l + abs(m)] = (-1) ** m / np.sqrt(2)
            q[l + m, l - abs(m)] = 1j * (-1) ** m / np.sqrt(2)
        return (-1j) ** l * q

    M = 8
    cg = np.zeros((H9 * D, D), np.float32)
    which = np.zeros((H9 * D, D, 3), np.int64)
    first = {0: 0, 1: 1, 2: 4}
    for idx, (le, ln, lo) in enumerate(combos):
        C = np.zeros((2 * le + 1, 2 * ln + 1, 2 * lo + 1), dtype=np.complex128)
        for m1 in range(-le, le + 1):
            for m2 in range(-ln, ln + 1):
                if -lo <= m1 + m2 <= lo:
                    C[m1 + le, m2 + ln, m1 + m2 + lo] = coeff(le, m1, ln, m2, lo, m1 + m2)
        C = np.einsum('ij,kl,mn,ikn->jlm', qmat(le), qmat(ln), np.conj(qmat(lo)).T, C).real
        C = (C / np.linalg.norm(C)).astype(np.float32)
        for i in range(2 * le + 1):
            for m in range(M):
                for j in range(2 * ln + 1):
                    for o in range(M):
                        for k in range(2 * lo + 1):
                            r = (first[le] + i) * D + (m if ln == 0 else M + 3 * m + j)
                            q = o if lo == 0 else M + 3 * o + k
                            cg[r, q] = C[i, j, k]
                            which[r, q] = (idx, m, o)
    return cg, which


def program(nc, a, out):
    dr = {n: nc.dram_tensor(n, s, d).ap() for n, s, d in [
        ("table0", (NP, AW), F32), ("table1", (NP, D), F32), ("edge_logit", (T, TS), F32), ("raw", (PN, PS), F32),
        ("counts", (NP, NP), F16),
        ("hidden", (PN, P, JP * FH), F16), ("table3", (NP, FH), F32), ("dst16", (PN, PS), F16),
        ("pair_blocks", (PN, 1), I32)]}
    with ExitStack() as ctx:
        t = Tools(nc, ctx, "keep")

        class Kept:
            pass
        g = Kept()
        g.rows_landed = [[t.sem(f"rows_landed{k}{h}") for h in range(2)] for k in range(3)]
        g.bounds = t.sb("bounds", [1, 2 * NB], I32)
        g.pair_blocks = t.sb("pair_blocks", [1, PN], I32)
        g.node_c = t.sb("node_c", [P, NB])
        g.pcol, g.node_id, g.iota = t.sb("pcol", [P, 1]), t.sb("node_id", [P, NB]), t.sb("iota", [P, P])
        g.block_first = t.sb("block_first", [P, NB + 1])
        g.ident, g.ident16 = t.sb("ident", [P, P]), t.sb("ident16", [P, P], F16)
        g.x, g.h, g.deg = t.sb("x", [P, NB, D]), t.sb("h", [P, NB, D]), t.sb("deg", [P, NB])
        g.deg_out, g.dis, g.ones = t.sb("deg_out", [P, NB]), t.sb("dis", [P, NB]), t.sb("ones", [P, P])
        edges = ExitStack()
        te = Tools(nc, edges, "edges")
        g.src_i, g.dst_c, g.src_f = te.sb("src_i", [P, EC], I32), te.sb("dst_c", [P, EC]), te.sb("src_f", [P, EC])
        g.ids = te.sb("ids", [P, NP])
        with ExitStack() as early:
            g.ids16 = Tools(nc, early, "early").sb("ids16", [P, NP], F16)
            setup(nc, g, a, dr)
            table0(nc, g, a, dr)
            edge_logits(nc, g, a, dr)
            with ExitStack() as l0:
                G = Tools(nc, l0, "l0").sb("G", [P, EC, D + 1])
                count_and_gather(nc, g, a, dr, G)
                raw, best = (Tools(nc, l0, "l0").sb(n, [P, w]) for n, w in (("raw", EC), ("best", NB)))
                raw_logits(nc, g, a, dr, G, raw)
                maxima(nc, g, dr, best)
                sums = Tools(nc, l0, "l0b").sb("sums", [P, NB, D + 1])
                weighted_sums(nc, g, dr, raw, G, best, sums)
                next_layer(nc, g, a, "layer1", dr["table1"], sums=sums)
        with ExitStack() as l1:
            t1 = Tools(nc, l1, "l1")
            sums = t1.sb("sums", [P, NB, H9 * D])
            mixed = t1.sb("mixed", [P, NB, D])
            G = t1.sb("G", [P, EC, D])
            product_sums(nc, g, G, sums, a["harmonics"], dr["table1"])
            mix_products(nc, g, a, sums, mixed)
            next_layer(nc, g, a, "layer2", None, mixed=mixed)
        edges.close()
        residual_gcn(nc, g, a, dr)
        flow_layer(nc, g, a, dr)
        with ExitStack() as fin:
            s_out = Tools(nc, fin, "fin").sem("stored")
            with nc.Block() as block:
                @block.sync
                def _(e):
                    full = N // P
                    e.dma_start(out[0:full * P, :].rearrange("(b p) f -> p b f", p=P), g.x[:, 0:full, :]).then_inc(s_out, 16)
                    e.dma_start(out[full * P:N, :], g.x[0:N - full * P, full, :]).then_inc(s_out, 16)
                    e.wait_ge(s_out, 32)


def layouts(inp):
    def rows(v, n, fill=0):
        return np.concatenate([v, np.full((n - v.shape[0],) + v.shape[1:], fill, v.dtype)])

    def columns(v):
        return np.ascontiguousarray(v.reshape(EC, P, -1).transpose(1, 0, 2))
    i = {k: np.asarray(v) for k, v in inp.items()}
    ep = T * TS
    src, dst = rows(i["src"], ep), rows(i["dst"], ep, NP)
    off = np.array([0.0, 0.0, 0.0, -1.0], np.float32)
    per = np.array([1 / 50.0, 1.0, 1.0, 1 / 10.0], np.float32)
    spread = np.zeros((QT, 4, QT, 4, K8), np.float32)
    for q in range(QT):
        for c in range(4):
            spread[q, c, q, c, :] = per[c] / DENOM
    bias1 = np.tile(((off[:, None] - GRID[None, :]) / DENOM).reshape(-1), QT).astype(np.float32)
    w_edge = np.zeros((QT, 4 * K8, QT, 2 * P), np.float32)
    for q in range(QT):
        w_edge[q, :, q, :] = np.repeat(i["L0_gnn_W_edge"].T, K8, axis=1)
    w_edge = w_edge.reshape(P, QT, 2 * P)
    cg, which = cg_tables()
    w1 = i["L1_gnn_W"][which[..., 0], which[..., 1], which[..., 2]]
    return {
        "x": rows(i["x"], NP), "src": columns(src)[:, :, 0], "dst": columns(dst)[:, :, 0], "dst_rows": dst.reshape(T, TS),
        "node_vec": np.ascontiguousarray(rows(i["node_vec"], NP).reshape(NB, P).T),
        "edge_attr_4": np.ascontiguousarray(rows(i["edge_attr_4"], ep).reshape(QN, QT, TS, 4).transpose(1, 3, 0, 2)
                                            .reshape(4 * QT, QN * TS)),
        "harmonics": columns(rows(np.concatenate([i["edge_weight1"], i["edge_attr_3"], i["edge_attr_5"]], axis=1), ep)),
        "W_att": i["L0_gnn_W_att"], "W_lar": i["L0_gnn_W_lar"], "b_att": i["L0_gnn_b_att"], "b_lar": i["L0_gnn_b_lar"],
        "grid": GRID[None, :], "grid_col": np.tile(GRID, P // K8)[:, None].copy(),
        "spread": spread.reshape(4 * QT, P), "bias1": bias1[:, None], "W_edge": w_edge,
        "W_att_edge": np.ascontiguousarray(i["L0_gnn_W_att"][0, :D * K8].reshape(2, P).T),
        "b_edge": np.ascontiguousarray(np.repeat(i["L0_gnn_b_edge"], K8).reshape(2, P).T),
        "cg": cg, "W1_rep": w1,
        "gamma_hid": i["L2_gnn_bn_gamma_hid"], "beta_hid": i["L2_gnn_bn_beta_hid"],
        "gamma_out": i["L2_gnn_bn_gamma_out"], "beta_out": i["L2_gnn_bn_beta_out"],
        "edge_attr_16": rows(i["edge_attr_16"], ep).reshape(PN, JP, P, ED).transpose(0, 3, 1, 2),
        "Wf1_dst": np.concatenate([i["L3_gnn_Wf1"][0:D], i["L3_gnn_Wf1"][D:2 * D]], axis=1),
        "Wf1_src": np.concatenate([i["L3_gnn_Wf1"][D:2 * D], i["L3_gnn_Wf1"][0:D]], axis=1),
        "Wf1_edge": np.concatenate([i["L3_gnn_Wf1"][2 * D:], i["L3_gnn_Wf1"][2 * D:]], axis=1),
        "bf1_twice": np.concatenate([i["L3_gnn_bf1"], i["L3_gnn_bf1"]]),
        **{k: i["L3_gnn_" + k] for k in ("Wf2", "bf2", "Wn1", "bn1", "Wn2", "bn2")},
        **{k: i["L2_gnn_" + k] for k in ("W_enc1", "b_enc1", "W_hid", "b_hid", "W_dec2", "b_dec2", "W_dec3", "b_dec3",
                                         "Wres_enc1", "bres_enc1", "Wres_dec2", "bres_dec2")},
    }


def kernel(**inputs):
    import concourse.bacc as bacc
    from concourse.bass_utils import run_bass_kernel_spmd as run

    nc = bacc.Bacc("TRN2", target_bir_lowering=False, num_devices=1)
    arrays, a = {}, {}
    for name, v in layouts(inputs).items():
        v = np.ascontiguousarray(v)
        arrays[f"in_{name}_dram"] = v
        a[name] = nc.dram_tensor(f"in_{name}_dram", v.shape, mybir.dt.from_np(v.dtype), kind="ExternalInput").ap()
    out = nc.dram_tensor("out_0_dram", (N, D), F32, kind="ExternalOutput").ap()
    program(nc, a, out)
    r = run(nc, [arrays], core_ids=[0])
    return r.results[0]["out_0_dram"]
```
